# Optimizing a Trainium2 kernel written in Bass

```python
import numpy as np
import jax
import jax.numpy as jnp

def _softmax(x, axis=-1):
    return jax.nn.softmax(x, axis=axis)

def _gelu(x):
    return jax.nn.gelu(x, approximate=True)

def _silu(x):
    return jax.nn.silu(x)

def _sigmoid(x):
    return jax.nn.sigmoid(x)

def _layernorm(x, axis=-1, eps=1e-05):
    m = jnp.mean(x, axis=axis, keepdims=True)
    v = jnp.var(x, axis=axis, keepdims=True)
    return (x - m) / jnp.sqrt(v + eps)

def _scatter_add(tgt, idx, src, axis=0):
    return tgt.at[idx].add(src)

def _segment_sum(src, seg, n):
    return jax.ops.segment_sum(src, seg, n)
kernel_name = 'mk_prb_d1_jaxref_r8_5b882e'

def setup_inputs(seed: int=0):
    np.random.seed(seed)
    _w = jnp.asarray

    def _L0_attn_setup():
        import jax, jax.numpy as jnp
        import numpy as np
        EMBED_DIM = 128
        NUM_HEADS = 16
        HEAD_DIM = EMBED_DIM // NUM_HEADS
        WL_CHANNELS = 16
        BATCH = 1
        SEQ = 128
        KERR = 2.7e-18 * 1000000.0
        SCALE = 1.0 / np.sqrt(HEAD_DIM)
        W_INIT = 0.02
        key = jax.random.key(seed)
        ks = jax.random.split(key, 7)
        x = jax.random.normal(ks[0], (BATCH, SEQ, EMBED_DIM), dtype=jnp.float32)
        Wq = jax.random.normal(ks[1], (EMBED_DIM, EMBED_DIM), dtype=jnp.float32) * W_INIT
        Wk = jax.random.normal(ks[2], (EMBED_DIM, EMBED_DIM), dtype=jnp.float32) * W_INIT
        Wv = jax.random.normal(ks[3], (EMBED_DIM, EMBED_DIM), dtype=jnp.float32) * W_INIT
        Wo = jax.random.normal(ks[4], (EMBED_DIM, EMBED_DIM), dtype=jnp.float32) * W_INIT
        bq = jnp.zeros((EMBED_DIM,), jnp.float32)
        bk = jnp.zeros((EMBED_DIM,), jnp.float32)
        bv = jnp.zeros((EMBED_DIM,), jnp.float32)
        bo = jnp.zeros((EMBED_DIM,), jnp.float32)
        phase_modulators = jax.random.normal(ks[5], (WL_CHANNELS, NUM_HEADS), dtype=jnp.float32)
        interference_weights = jnp.ones((WL_CHANNELS,), jnp.float32)
        return {'x': x, 'Wq': Wq, 'bq': bq, 'Wk': Wk, 'bk': bk, 'Wv': Wv, 'bv': bv, 'Wo': Wo, 'bo': bo, 'phase_modulators': phase_modulators, 'interference_weights': interference_weights}
    _L0_attn_in = _L0_attn_setup()

    def _L0_ffn_setup():
        import jax, jax.numpy as jnp
        import numpy as np
        B, S, D = (4, 256, 128)
        E = 8
        DFF = 512
        CAP_FACTOR = 1.25
        key = jax.random.key(seed)
        ks = jax.random.split(key, 4)
        std_gate = float(np.sqrt(0.1 / D))
        inputs = jax.random.normal(ks[0], (B, S, D), dtype=jnp.float32)
        gate_w = jax.random.normal(ks[1], (E, D), dtype=jnp.float32) * std_gate
        w1 = jax.random.normal(ks[2], (E, D, DFF), dtype=jnp.float32) * (1.0 / np.sqrt(D))
        b1 = jnp.zeros((E, DFF), dtype=jnp.float32)
        w2 = jax.random.normal(ks[3], (E, DFF, D), dtype=jnp.float32) * (1.0 / np.sqrt(DFF))
        b2 = jnp.zeros((E, D), dtype=jnp.float32)
        return {'inputs': inputs, 'gate_w': gate_w, 'w1': w1, 'b1': b1, 'w2': w2, 'b2': b2}
    _L0_ffn_in = _L0_ffn_setup()
    _d = {'L0_attn_x': _L0_attn_in['x'], 'L0_attn_Wq': _L0_attn_in['Wq'], 'L0_attn_bq': _L0_attn_in['bq'], 'L0_attn_Wk': _L0_attn_in['Wk'], 'L0_attn_bk': _L0_attn_in['bk'], 'L0_attn_Wv': _L0_attn_in['Wv'], 'L0_attn_bv': _L0_attn_in['bv'], 'L0_attn_Wo': _L0_attn_in['Wo'], 'L0_attn_bo': _L0_attn_in['bo'], 'L0_attn_phase_modulators': _L0_attn_in['phase_modulators'], 'L0_attn_interference_weights': _L0_attn_in['interference_weights'], 'L0_ffn_gate_w': _L0_ffn_in['gate_w'], 'L0_ffn_w1': _L0_ffn_in['w1'], 'L0_ffn_b1': _L0_ffn_in['b1'], 'L0_ffn_w2': _L0_ffn_in['w2'], 'L0_ffn_b2': _L0_ffn_in['b2']}
    _x0 = _d['L0_attn_x']
    _d['L0_attn_x'] = jax.random.normal(jax.random.fold_in(jax.random.key(seed), 1), (16, 256, 128), dtype=_x0.dtype)
    del _x0
    return _d

def reference(L0_attn_x, L0_attn_Wq, L0_attn_bq, L0_attn_Wk, L0_attn_bk, L0_attn_Wv, L0_attn_bv, L0_attn_Wo, L0_attn_bo, L0_attn_phase_modulators, L0_attn_interference_weights, L0_ffn_gate_w, L0_ffn_w1, L0_ffn_b1, L0_ffn_w2, L0_ffn_b2):

    def _L0_attn_ref(x, Wq, bq, Wk, bk, Wv, bv, Wo, bo, phase_modulators, interference_weights):
        import jax, jax.numpy as jnp
        import numpy as np
        EMBED_DIM = 128
        NUM_HEADS = 16
        HEAD_DIM = EMBED_DIM // NUM_HEADS
        WL_CHANNELS = 16
        BATCH = 1
        SEQ = 128
        KERR = 2.7e-18 * 1000000.0
        SCALE = 1.0 / np.sqrt(HEAD_DIM)
        W_INIT = 0.02
        B, S, E = x.shape
        H, D = (NUM_HEADS, HEAD_DIM)

        def proj(W, b):
            y = jnp.einsum('bse,ef->bsf', x, W) + b
            return y.reshape(B, S, H, D).transpose(0, 2, 1, 3)
        Q = proj(Wq, bq)
        K = proj(Wk, bk)
        V = proj(Wv, bv)
        cos_pm = jnp.cos(phase_modulators)

        def wl_step(acc, wl):
            cpm, iw = wl
            m = cpm[None, :, None, None]
            Qw = Q * m
            Kw = K * m
            scores = jnp.einsum('bhqd,bhkd->bhqk', Qw, Kw) * SCALE
            scores = scores * jnp.cos(KERR * scores * scores)
            attn = jax.nn.softmax(scores, axis=-1)
            out = jnp.einsum('bhqk,bhkd->bhqd', attn, V)
            return (acc + out * iw, None)
        acc0 = jnp.zeros((B, H, S, D), x.dtype)
        acc, _ = jax.lax.scan(wl_step, acc0, (cos_pm, interference_weights))
        combined = acc / WL_CHANNELS
        combined = combined.transpose(0, 2, 1, 3).reshape(B, S, E)
        return jnp.einsum('bse,ef->bsf', combined, Wo) + bo

    def _L0_ffn_ref(inputs, gate_w, w1, b1, w2, b2):
        import jax, jax.numpy as jnp
        import numpy as np
        B, S, D = (4, 256, 128)
        E = 8
        DFF = 512
        CAP_FACTOR = 1.25
        d_model = inputs.shape[-1]
        tokens = inputs.reshape(-1, d_model)
        T = tokens.shape[0]
        num_experts = gate_w.shape[0]
        capacity = int(np.ceil(CAP_FACTOR * T / num_experts))
        logits = jnp.einsum('td,ed->te', tokens.astype(jnp.float32), gate_w)
        probs = jax.nn.softmax(logits, axis=-1)
        expert_idx = jnp.argmax(probs, axis=-1)
        mask = jax.nn.one_hot(expert_idx, num_experts, dtype=jnp.float32)
        ranks = jnp.cumsum(mask, axis=0) - 1.0
        keep = (ranks < capacity) * mask
        pos = ranks.astype(jnp.int32)
        sec_mask = jax.nn.one_hot(pos, capacity, dtype=jnp.float32) * keep[:, :, None]
        combine_weights = probs[:, :, None] * sec_mask
        dispatch = jnp.einsum('tec,td->ecd', sec_mask, tokens)
        h = jax.nn.relu(jnp.einsum('ecd,edh->ech', dispatch, w1) + b1[:, None, :])
        expert_out = jnp.einsum('ech,ehd->ecd', h, w2) + b2[:, None, :]
        ans = jnp.einsum('tec,ecd->td', combine_weights, expert_out)
        return ans.reshape(inputs.shape)
    x = L0_attn_x
    xn = _layernorm(x, axis=-1)
    x = x + _L0_attn_ref(xn, L0_attn_Wq, L0_attn_bq, L0_attn_Wk, L0_attn_bk, L0_attn_Wv, L0_attn_bv, L0_attn_Wo, L0_attn_bo, L0_attn_phase_modulators, L0_attn_interference_weights) + _L0_ffn_ref(xn, L0_ffn_gate_w, L0_ffn_w1, L0_ffn_b1, L0_ffn_w2, L0_ffn_b2)
    return x

_drawn_inputs = setup_inputs


def setup_inputs(seed=0):
    import zlib

    import numpy as np

    out = dict(_drawn_inputs(seed))
    spreads = {'L0_attn_bq': (0.0, 0.8),
     'L0_attn_bk': (0.0, 0.8),
     'L0_attn_bv': (0.0, 0.379),
     'L0_attn_bo': (0.0, 0.1),
     'L0_attn_interference_weights': (1.0, 0.6),
     'L0_ffn_b1': (0.0, 0.585),
     'L0_ffn_b2': (0.0, 0.416)}
    factors = {'L0_attn_Wq': 8.0,
     'L0_attn_Wk': 8.0,
     'L0_attn_Wv': 8.0,
     'L0_attn_Wo': 2.913,
     'L0_attn_phase_modulators': 8.0}
    for name, (base, spread) in spreads.items():
        noise = np.random.default_rng([zlib.crc32(name.encode()), seed]).standard_normal(out[name].shape)
        drawn = base * np.exp(spread * noise) if base else spread * noise
        out[name] = jnp.asarray(drawn.astype(out[name].dtype))
    for name, factor in factors.items():
        out[name] = (out[name] * factor).astype(out[name].dtype)
    return out
```

```python
import numpy as np
import concourse.bass as bass
from concourse import mybir
from contextlib import ExitStack


def attention_and_experts(nc, x, Wq, bq, Wk, bk, Wv, bv, Wo, bo, phase, weights, gate_w, w1, b1, w2, b2, out):
    f32, bf16, i32 = mybir.dt.float32, mybir.dt.bfloat16, mybir.dt.int32
    ALU, ACT, AX = mybir.AluOpType, mybir.ActivationFunctionType, mybir.AxisListType
    ds = bass.ds

    BATCH, SEQ, D = x.shape
    W, H = phase.shape
    HD = D // H
    E, _, DFF = w1.shape
    P = 128
    TOK = BATCH * SEQ
    TILES = TOK // P
    QT = SEQ // P
    SIDES = 2
    SIDE_B = BATCH // SIDES
    SIDE_TILES = TILES // SIDES
    SIDE_TOK = TOK // SIDES
    UNITS = SIDES * H
    BLK = QT * QT * SEQ // QT
    COLS = SIDE_B * BLK
    BANK = 512
    CAP = -(-5 * TOK // (4 * E))
    CT = CAP // P
    HC = CAP // 2
    FCH = DFF // P
    SCALE = 1.0 / np.sqrt(HD)
    KERR = 2.7e-18 * 1000000.0
    EPS = 1e-5
    PARTS = 3
    PROD = PARTS * PARTS * HD
    MAXROW = 96
    STACK = MAXROW + PARTS
    VC = 32
    OC = HD + 1
    GR = 4
    OTW = (BANK // P) * GR
    TWO_PI = 2.0 * np.pi
    C1 = 6.28125
    C2 = float(np.float32(np.round((TWO_PI - C1) * 2.0**21) / 2.0**21))
    C3 = TWO_PI - C1 - C2
    ROUND = 1.5 * 2.0**23
    S_PLAIN = 0.9 * np.sqrt(2.0**-12 / KERR)

    pieces_dram = nc.dram_tensor("qk_parts", (2, SIDES, D, PARTS, SIDE_TOK), bf16, kind="Internal").ap()
    slots_dram = nc.dram_tensor("dispatched", (E * CAP + TOK, D), f32, kind="Internal").ap()
    expert_dram = nc.dram_tensor("expert_out", (E * CAP, D), f32, kind="Internal").ap()

    ctx = ExitStack()
    with ctx:
        def sb(name, shape, dt=f32):
            return ctx.enter_context(nc.sbuf_tensor(name, shape, dt))

        def sem(name):
            return ctx.enter_context(nc.semaphore(name))

        ident = sb("ident", [P, P])
        identb = sb("identb", [P, P], bf16)
        ones_b = sb("ones_b", [P, P], bf16)
        below_b = sb("below_b", [P, P], bf16)
        wq_s, wk_s, wv_s, wo_s = (sb(n, [P, D]) for n in ("wq_s", "wk_s", "wv_s", "wo_s"))
        bq_s, bk_s = sb("bq_s", [P, 1]), sb("bk_s", [P, 1])
        bv_s, bo_s = sb("bv_s", [P, D]), sb("bo_s", [P, D])
        gw_s = sb("gw_s", [P, E])
        phase_s = sb("phase_s", [P, W * H])
        iw_s = sb("iw_s", [P, W])
        cw = sb("cw", [P, UNITS * W])
        base = sb("base", [P, TILES, D])
        xnT = sb("xnT", [P, TOK])
        Vall = sb("Vall", [P, UNITS * SIDE_TILES * HD])
        heads = xnT
        T = [sb(f"T{i}", [P, COLS]) for i in range(2)]
        Pr = [sb(f"Pr{i}", [P, COLS]) for i in range(2)]
        Qs = [sb(f"Qs{i}", [P, SIDE_TOK], bf16) for i in range(2)]
        Ks = [sb(f"Ks{i}", [P, SIDE_TOK], bf16) for i in range(2)]
        Vst = [sb(f"Vst{i}", [P, SIDE_TILES, VC]) for i in range(2)]
        pv_s = [sb(f"pv_s{i}", [P, BANK]) for i in range(2)]
        OT = sb("OT", [P, 2, W * OTW * OC])
        flag = sb("flag", [1, 1], i32)

        banks = [ctx.enter_context(nc.psum_tensor(f"bank{i}", [P, BANK], f32)) for i in range(7)]
        bank_b = ctx.enter_context(nc.psum_tensor("bank_b", [P, 2 * BANK], bf16))

        setup = ExitStack()
        with setup:
            def ssb(name, shape, dt=f32):
                return setup.enter_context(nc.sbuf_tensor(name, shape, dt))

            def ssem(name):
                return setup.enter_context(nc.semaphore(name))

            xn = ssb("xn", [P, TILES, D])
            zeros = T[1][:, COLS - 1024:COLS]
            sq = Pr[0][:, :].rearrange("p (t d) -> p t d", d=D)
            part = [ssb(f"part{i}", [P, PARTS, BANK], bf16) for i in range(2)]
            rest = [ssb(f"rest{i}", [P, BANK]) for i in range(2)]
            stat = ssb("stat", [P, 8, TILES])
            ph = ssb("ph", [P, 4, W * H])
            absmax = ssb("absmax", [P, TOK // BANK, 2])
            qkmax = ssb("qkmax", [P, 2])
            qkone = ssb("qkone", [1, 4])
            lg = ssb("lg", [P, 6, TILES, E])
            maskb = ssb("maskb", [P, TILES, E], bf16)
            r = ssb("r", [P, 10, TILES])
            idx_scatter, idx_gather = ssb("idx_scatter", [P, TILES], i32), ssb("idx_gather", [P, TILES], i32)
            order8, ebase = ssb("order8", [P, E]), ssb("ebase", [P, E])
            token_row = ssb("token_row", [P, TILES])

            x_in = [ssem(f"x_in{c}") for c in range(4)]
            w_in, small_in = ssem("w_in"), ssem("small_in")
            const_ready, dve_const = ssem("const_ready"), ssem("dve_const")
            pool_const = ssem("pool_const")
            centred, squared, var_ready, root_ready, xn_ready = (ssem(n) for n in (
                "centred", "squared", "var_ready", "root_ready", "xn_ready"))
            xT_made, xT_copied = ssem("xT_made"), ssem("xT_copied")
            proj, part1, rest1, part2, part3, absd = (ssem(n) for n in (
                "proj", "part1", "rest1", "part2", "part3", "absd"))
            parts_out = [ssem(f"parts_out{i}") for i in range(2)]
            v_made, v_copied, logits_made = ssem("v_made"), ssem("v_copied"), ssem("logits_made")
            angle, sine = ssem("angle"), ssem("sine")
            chain = ssem("chain")
            gate_in, gate_exp, mask_ready, counts_made = (ssem(n) for n in (
                "gate_in", "gate_exp", "mask_ready", "counts_made"))
            index_ready = ssem("index_ready")
            maxima, maxima_made = ssem("maxima"), ssem("maxima_made")
            zeroed, scattered = ssem("zeroed"), ssem("scattered")
            fc_xT, fc_xTs, fc_h, fc_hs, fc_o, fc_os = (ssem(n) for n in (
                "fc_xT", "fc_xTs", "fc_h", "fc_hs", "fc_o", "fc_os"))
            fc_in = [ssem(f"fc_in{i}") for i in range(2)]
            fc_out = [ssem(f"fc_out{i}") for i in range(2)]
            gathered, base_ready = ssem("gathered"), ssem("base_ready")
            CH = TILES // 4
            NQ = TOK // BANK
            TB = BANK // P

            e_x = [T[0][:, i * CAP:(i + 1) * CAP].rearrange("p (t d) -> p t d", d=D) for i in range(2)]
            e_xT = [T[0][:, (2 + i) * CAP:(3 + i) * CAP] for i in range(2)]
            e_h = T[1][:, 0:FCH * CAP].rearrange("p (f c) -> p f c", f=FCH)
            e_o = [Pr[0][:, i * CAP:(i + 1) * CAP].rearrange("p (t d) -> p t d", d=D) for i in range(2)]
            e_w1 = [Pr[1][:, i * DFF:(i + 1) * DFF] for i in range(2)]
            e_w2 = [Pr[1][:, (2 + i) * DFF:(3 + i) * DFF].rearrange("p (f d) -> p f d", d=D) for i in range(2)]
            b1_s = ssb("b1_s", [P, E, FCH])
            b2_s = ssb("b2_s", [P, E, D])
            got = T[0][:, :].rearrange("p (t d) -> p t d", d=D)

            with nc.Block() as block:

                @block.sync
                def _(sp):
                    xv = x.rearrange("b (t p) d -> p (b t) d", p=P)
                    for c in range(4):
                        sp.dma_start(base[:, c * CH:(c + 1) * CH, :], xv[:, c * CH:(c + 1) * CH, :]).then_inc(x_in[c], 16)
                    for dst, src in ((wq_s, Wq), (wk_s, Wk), (wv_s, Wv), (wo_s, Wo)):
                        sp.dma_start(dst[:, :], src).then_inc(w_in, 16)
                    for m in range(2 * NQ):
                        n, kind = m // 2, m % 2
                        side, col = n // (NQ // SIDES), (n % (NQ // SIDES)) * BANK
                        sp.wait_ge(part3, m + 1)
                        sp.dma_start(pieces_dram[kind, side, :, :, col:col + BANK],
                                     part[m % 2][:, :, :]).then_inc(parts_out[m % 2], 16)
                    for i in range(2):
                        sp.wait_ge(parts_out[i], 16 * NQ)

                    sp.wait_ge(scattered, 16 * TILES)
                    for e in range(E):
                        if e >= 2:
                            sp.wait_ge(fc_os, CT * (e - 1))
                        sp.dma_start(e_x[e % 2], slots_dram[e * CAP:(e + 1) * CAP, :]
                                     .rearrange("(t p) d -> p t d", p=P)).then_inc(fc_in[e % 2], 16)
                        sp.dma_start(e_w1[e % 2], w1[e, :, :]).then_inc(fc_in[e % 2], 16)
                        sp.dma_start(e_w2[e % 2], w2[e, :, :].rearrange("(f p) d -> p f d", p=P)).then_inc(fc_in[e % 2], 16)
                        if e:
                            sp.wait_ge(fc_os, CT * e)
                            sp.dma_start(expert_dram[(e - 1) * CAP:e * CAP, :].rearrange("(t p) d -> p t d", p=P),
                                         e_o[(e - 1) % 2]).then_inc(fc_out[(e - 1) % 2], 16)
                    sp.wait_ge(fc_os, CT * E)
                    sp.dma_start(expert_dram[(E - 1) * CAP:E * CAP, :].rearrange("(t p) d -> p t d", p=P),
                                 e_o[(E - 1) % 2]).then_inc(fc_out[(E - 1) % 2], 16)
                    for i in range(2):
                        sp.wait_ge(fc_out[i], 16 * E // 2)

                @block.gpsimd
                def _(pool):
                    pool.memset(zeros[:, :], 0.0).then_inc(const_ready, 1)
                    pool.memset(ident[:, :], 0.0).then_inc(pool_const, 1)
                    pool.memset(identb[:, :], 0.0).then_inc(pool_const, 1)
                    pool.memset(ones_b[:, :], 1.0).then_inc(pool_const, 1)
                    pool.wait_ge(pool_const, 3)
                    for m in (ident, identb):
                        pool.affine_select(out=m[:, :], in_=m[:, :], compare_op=ALU.not_equal, fill=1.0,
                                           base=0, pattern=[[-1, P]], channel_multiplier=1).then_inc(const_ready, 1)
                    pool.affine_select(out=below_b[:, :], in_=ones_b[:, :], compare_op=ALU.is_gt, fill=0.0,
                                       base=0, pattern=[[1, P]], channel_multiplier=-1).then_inc(const_ready, 1)
                    pool.iota(order8[:, :], pattern=[[-1, E]], base=E, channel_multiplier=0,
                              allow_small_or_imprecise_dtypes=True).then_inc(const_ready, 1)
                    pool.iota(ebase[:, :], pattern=[[CAP, E]], base=0, channel_multiplier=0,
                              allow_small_or_imprecise_dtypes=True).then_inc(const_ready, 1)
                    pool.iota(token_row[:, :], pattern=[[P, TILES]], base=E * CAP, channel_multiplier=1,
                              allow_small_or_imprecise_dtypes=True).then_inc(const_ready, 1)
                    for i in range(2):
                        pool.memset(Qs[i][:, :], 0.0).then_inc(pool_const, 1)
                        pool.memset(Ks[i][:, :], 0.0).then_inc(pool_const, 1)
                        pool.memset(Vst[i][:, :, :], 0.0).then_inc(pool_const, 1)
                    pool.wait_ge(pool_const, 9)
                    for i in range(2):
                        pool.memset(Vst[i][:, :, HD:OC], 1.0).then_inc(pool_const, 1)
                    for i in range(2):
                        pool.wait_ge(pool_const, 11 + i)
                        pool.memset(Ks[i][MAXROW:STACK, :], 1.0).then_inc(pool_const, 1)
                    pool.wait_ge(pool_const, 13)
                    pool.wait_ge(xn_ready, 4)
                    pool.wait_ge(index_ready, 2)
                    pool.wait_ge(zeroed, 16 * (E * CAP * D // (P * 1024)))
                    for t in range(TILES):
                        pool.indirect_dma_start(out=slots_dram, out_offset=bass.IndirectOffsetOnAxis(
                            ap=idx_scatter[:, t:t + 1], axis=0), in_=xn[:, t, :], in_offset=None).then_inc(scattered, 16)
                    for i in range(2):
                        pool.wait_ge(fc_out[i], 16 * E // 2)
                    for t in range(TILES):
                        pool.indirect_dma_start(out=got[:, t, :], out_offset=None, in_=expert_dram,
                                                in_offset=bass.IndirectOffsetOnAxis(ap=idx_gather[:, t:t + 1], axis=0)
                                                ).then_inc(gathered, 16)
                    pool.wait_ge(gathered, 16 * TILES)

                @block.scalar
                def _(act):
                    act.dma_start(bq_s[:, :], bq.rearrange("(d a) -> d a", a=1)).then_inc(small_in, 16)
                    act.dma_start(bk_s[:, :], bk.rearrange("(d a) -> d a", a=1)).then_inc(small_in, 16)
                    act.dma_start(bv_s[:, :], bv.partition_broadcast(P)).then_inc(small_in, 16)
                    act.dma_start(bo_s[:, :], bo.partition_broadcast(P)).then_inc(small_in, 16)
                    act.dma_start(iw_s[:, :], weights.partition_broadcast(P)).then_inc(small_in, 16)
                    act.dma_start(phase_s[:, :], phase.rearrange("w h -> (w h)").partition_broadcast(P)).then_inc(small_in, 16)
                    act.dma_start(gw_s[:, :], gate_w.rearrange("e d -> d e"), allow_slow_non_contiguous=True).then_inc(small_in, 16)
                    act.dma_start(b1_s[:, :, :], b1.rearrange("e (f p) -> p e f", p=P), allow_slow_non_contiguous=True).then_inc(small_in, 16)
                    act.dma_start(b2_s[:, :, :], b2.rearrange("e d -> (e d)").partition_broadcast(P)
                                  .rearrange("p (e d) -> p e d", e=E)).then_inc(small_in, 16)
                    act.wait_ge(const_ready, 1)
                    for z in range(E * CAP * D // (P * 1024)):
                        rows = P * 1024 // D
                        act.dma_start(slots_dram[z * rows:(z + 1) * rows, :].rearrange("(p a) d -> p (a d)", p=P),
                                      zeros[:, :]).then_inc(zeroed, 16)
                    for c in range(4):
                        act.wait_ge(centred, c + 1)
                        nc.scalar.activation(sq[:, c * CH:(c + 1) * CH, :], xn[:, c * CH:(c + 1) * CH, :],
                                             ACT.Square).then_inc(squared, 1)
                    act.wait_ge(var_ready, 1)
                    nc.scalar.activation(stat[:, 3, :], stat[:, 2, :], ACT.Sqrt).then_inc(root_ready, 1)
                    act.wait_ge(angle, 1)
                    nc.scalar.activation(ph[:, 2, :], ph[:, 1, :], ACT.Sin).then_inc(sine, 1)
                    for n in range(NQ):
                        act.wait_ge(xT_made, n + 1)
                        nc.scalar.activation(xnT[:, n * BANK:(n + 1) * BANK], banks[n % 2][:, :],
                                             ACT.Copy).then_inc(xT_copied, 1)
                    act.wait_ge(small_in, 16 * 9)
                    for m in range(2 * NQ):
                        act.wait_ge(proj, m + 1)
                        if m >= 2:
                            act.wait_ge(parts_out[m % 2], 16 * (m // 2))
                            act.wait_ge(absd, m - 1)
                        nc.scalar.activation(part[m % 2][:, 0, :], banks[2 + m % 2][:, :], ACT.Identity,
                                             bias=(bq_s, bk_s)[m % 2][:, :]).then_inc(part1, 1)
                        act.wait_ge(rest1, m + 1)
                        nc.scalar.activation(part[m % 2][:, 1, :], rest[m % 2][:, :], ACT.Copy).then_inc(part2, 1)
                    act.wait_ge(gate_in, 1)
                    nc.scalar.activation(lg[:, 1, :, :], lg[:, 0, :, :], ACT.Exp).then_inc(gate_exp, 1)

                @block.vector
                def _(dve):
                    count = [0]

                    def link(ins):
                        count[0] += 1
                        ins.then_inc(chain, 1)
                        dve.wait_ge(chain, count[0])

                    def over_d(a):
                        return a.unsqueeze(2).to_broadcast([P, a.shape[1], D])

                    for c in range(4):
                        s = slice(c * CH, (c + 1) * CH)
                        dve.wait_ge(x_in[c], 16)
                        link(nc.vector.reduce_sum(stat[:, 0, s], base[:, s, :], AX.X))
                        link(nc.vector.tensor_scalar(stat[:, 1, s], stat[:, 0, s], 1.0 / D, None, ALU.mult))
                        nc.vector.tensor_tensor(xn[:, s, :], base[:, s, :], over_d(stat[:, 1, s]),
                                                ALU.subtract).then_inc(centred, 1)
                    for c in range(4):
                        s = slice(c * CH, (c + 1) * CH)
                        dve.wait_ge(squared, c + 1)
                        link(nc.vector.reduce_sum(stat[:, 4, s], sq[:, s, :], AX.X))
                    nc.vector.tensor_scalar(stat[:, 2, :], stat[:, 4, :], 1.0 / D, EPS, ALU.mult, ALU.add).then_inc(var_ready, 1)
                    dve.wait_ge(root_ready, 1)
                    link(nc.vector.reciprocal(stat[:, 5, :], stat[:, 3, :]))
                    link(nc.vector.tensor_tensor(stat[:, 6, :], stat[:, 5, :], stat[:, 5, :], ALU.mult))
                    link(nc.vector.scalar_tensor_tensor(stat[:, 7, :], stat[:, 6, :], -0.5, stat[:, 2, :], ALU.mult, ALU.mult))
                    link(nc.vector.tensor_scalar(stat[:, 4, :], stat[:, 7, :], 1.5, None, ALU.add))
                    link(nc.vector.tensor_tensor(stat[:, 6, :], stat[:, 5, :], stat[:, 4, :], ALU.mult))
                    for c in range(4):
                        s = slice(c * CH, (c + 1) * CH)
                        nc.vector.tensor_tensor(xn[:, s, :], xn[:, s, :], over_d(stat[:, 6, s]), ALU.mult).then_inc(xn_ready, 1)

                    dve.wait_ge(small_in, 16 * 9)
                    link(nc.vector.tensor_scalar(ph[:, 0, :], phase_s[:, :], 1.0 / TWO_PI, 0.25, ALU.mult, ALU.add))
                    link(nc.vector.tensor_scalar(ph[:, 1, :], ph[:, 0, :], ROUND, None, ALU.add))
                    link(nc.vector.tensor_scalar(ph[:, 0, :], ph[:, 1, :], -ROUND, None, ALU.add))
                    link(nc.vector.scalar_tensor_tensor(ph[:, 1, :], ph[:, 0, :], -C1, phase_s[:, :], ALU.mult, ALU.add))
                    link(nc.vector.scalar_tensor_tensor(ph[:, 2, :], ph[:, 0, :], -C2, ph[:, 1, :], ALU.mult, ALU.add))
                    link(nc.vector.scalar_tensor_tensor(ph[:, 3, :], ph[:, 0, :], -C3, ph[:, 2, :], ALU.mult, ALU.add))
                    link(nc.vector.tensor_scalar(ph[:, 0, :], ph[:, 3, :], np.pi / 2, np.pi, ALU.add, ALU.min))
                    nc.vector.tensor_scalar(ph[:, 1, :], ph[:, 0, :], -np.pi, None, ALU.max).then_inc(angle, 1)
                    dve.wait_ge(sine, 1)
                    for side in range(SIDES):
                        c_side = cw[:, side * H * W:(side + 1) * H * W].rearrange("p (h w) -> p w h", w=W)
                        sin_v = ph[:, 2, :].rearrange("p (w h) -> p w h", w=W)
                        link(nc.vector.scalar_tensor_tensor(c_side, sin_v, SCALE, sin_v, ALU.mult, ALU.mult))
                    link(nc.vector.tensor_scalar(iw_s[:, :], iw_s[:, :], 1.0 / W, None, ALU.mult))

                    def v_evac(n):
                        dve.wait_ge(v_made, n + 1)
                        t0 = n * TB
                        side, ts = t0 // SIDE_TILES, t0 % SIDE_TILES
                        dst = Vall[:, side * H * SIDE_TILES * HD:(side + 1) * H * SIDE_TILES * HD]
                        dst = dst.rearrange("p (h t d) -> p t h d", h=H, d=HD)
                        for i in range(TB):
                            ins = nc.vector.tensor_tensor(dst[:, ts + i, :, :],
                                                          banks[4][:, i * D:(i + 1) * D].rearrange("p (h d) -> p h d", d=HD),
                                                          bv_s[:, :].rearrange("p (h d) -> p h d", d=HD), ALU.add)
                        ins.then_inc(v_copied, 1)

                    for m in range(2 * NQ):
                        dve.wait_ge(part1, m + 1)
                        nc.vector.scalar_tensor_tensor(rest[m % 2][:, :], banks[2 + m % 2][:, :], (bq_s, bk_s)[m % 2][:, :],
                                                       part[m % 2][:, 0, :], ALU.add, ALU.subtract).then_inc(rest1, 1)
                        nc.vector.reduce_max(absmax[:, m // 2, m % 2:m % 2 + 1], part[m % 2][:, 0, :], AX.X,
                                             apply_absolute_value=True).then_inc(absd, 1)
                        if m % 2:
                            v_evac(m // 2)
                        dve.wait_ge(part2, m + 1)
                        nc.vector.tensor_tensor(part[m % 2][:, 2, :], rest[m % 2][:, :], part[m % 2][:, 1, :],
                                                ALU.subtract).then_inc(part3, 1)

                    dve.wait_ge(absd, 2 * NQ)
                    nc.vector.reduce_max(qkmax[:, :], absmax[:, :, :].rearrange("p n k -> p k n"), AX.X).then_inc(maxima, 1)
                    dve.wait_ge(maxima_made, 1)
                    link(nc.vector.reduce_max(qkone[:, 0:2], banks[6][0:1, 0:2 * P].rearrange("a (k p) -> a k p", p=P), AX.X))
                    link(nc.vector.tensor_tensor(qkone[:, 2:3], qkone[:, 0:1], qkone[:, 1:2], ALU.mult))
                    link(nc.vector.tensor_scalar(qkone[:, 3:4], qkone[:, 2:3], SCALE * HD * 1.01, S_PLAIN, ALU.mult, ALU.is_lt))
                    link(nc.vector.tensor_copy(flag[:, :], qkone[:, 3:4]))

                    def over_e(a):
                        return a.unsqueeze(2).to_broadcast([P, TILES, E])

                    def over_t(a):
                        return a.unsqueeze(1).to_broadcast([P, TILES, E])

                    dve.wait_ge(logits_made, 1)
                    dve.wait_ge(const_ready, 7)
                    logits = banks[5][:, 0:TILES * E].rearrange("p (t e) -> p t e", e=E)
                    link(nc.vector.reduce_max(r[:, 0, :], logits, AX.X))
                    nc.vector.tensor_tensor(lg[:, 0, :, :], logits, over_e(r[:, 0, :]), ALU.subtract).then_inc(gate_in, 1)
                    dve.wait_ge(gate_in, 1)
                    link(nc.vector.scalar_tensor_tensor(lg[:, 2, :, :], lg[:, 0, :, :], 0.0, over_t(order8[:, :]), ALU.is_ge, ALU.mult))
                    link(nc.vector.reduce_max(r[:, 1, :], lg[:, 2, :, :], AX.X))
                    link(nc.vector.tensor_tensor(lg[:, 3, :, :], lg[:, 2, :, :], over_e(r[:, 1, :]), ALU.is_equal))
                    nc.vector.tensor_copy(maskb[:, :, :], lg[:, 3, :, :]).then_inc(mask_ready, 1)
                    dve.wait_ge(gate_exp, 1)
                    link(nc.vector.reduce_sum(r[:, 2, :], lg[:, 1, :, :], AX.X))
                    link(nc.vector.reciprocal(r[:, 3, :], r[:, 2, :]))
                    dve.wait_ge(counts_made, 1)
                    within = banks[0][:, 0:TILES * E].rearrange("p (t e) -> p t e", e=E)
                    totals = banks[1][:, 0:TILES * E].rearrange("p (t e) -> p t e", e=E)
                    link(nc.vector.tensor_copy(lg[:, 0, 1:TILES, :], totals[:, 0:TILES - 1, :]))
                    link(nc.vector.memset(lg[:, 0, 0:1, :], 0.0))
                    a, b, shift = 0, 1, 1
                    while shift < TILES:
                        link(nc.vector.tensor_copy(lg[:, b, 0:shift, :], lg[:, a, 0:shift, :]))
                        link(nc.vector.tensor_tensor(lg[:, b, shift:, :], lg[:, a, shift:, :], lg[:, a, 0:TILES - shift, :], ALU.add))
                        a, b, shift = b, a, 2 * shift
                    link(nc.vector.tensor_tensor(lg[:, 2, :, :], within, lg[:, a, :, :], ALU.add))
                    link(nc.vector.tensor_tensor(lg[:, 4, :, :], lg[:, 2, :, :], lg[:, 3, :, :], ALU.mult))
                    link(nc.vector.reduce_sum(r[:, 4, :], lg[:, 4, :, :], AX.X))
                    link(nc.vector.tensor_tensor(lg[:, 5, :, :], lg[:, 3, :, :], over_t(ebase[:, :]), ALU.mult))
                    link(nc.vector.reduce_sum(r[:, 5, :], lg[:, 5, :, :], AX.X))
                    link(nc.vector.tensor_scalar(r[:, 6, :], r[:, 4, :], float(CAP), None, ALU.is_lt))
                    link(nc.vector.tensor_tensor(r[:, 7, :], r[:, 4, :], r[:, 5, :], ALU.add))
                    link(nc.vector.tensor_tensor(r[:, 8, :], r[:, 7, :], token_row[:, :], ALU.subtract))
                    link(nc.vector.tensor_tensor(r[:, 9, :], r[:, 8, :], r[:, 6, :], ALU.mult))
                    link(nc.vector.tensor_tensor(r[:, 8, :], r[:, 9, :], token_row[:, :], ALU.add))
                    nc.vector.tensor_copy(idx_scatter[:, :], r[:, 8, :]).then_inc(index_ready, 1)
                    link(nc.vector.tensor_tensor(r[:, 9, :], r[:, 7, :], r[:, 6, :], ALU.mult))
                    nc.vector.tensor_copy(idx_gather[:, :], r[:, 9, :]).then_inc(index_ready, 1)
                    link(nc.vector.tensor_tensor(r[:, 0, :], r[:, 3, :], r[:, 6, :], ALU.mult))

                    for e in range(E):
                        for half in range(2):
                            k = 2 * e + half
                            dve.wait_ge(fc_xT, k + 1)
                            t0, t1 = (0, TB) if half == 0 else (TB, CT)
                            nc.vector.tensor_copy(e_xT[e % 2][:, t0 * P:t1 * P], banks[half][:, 0:(t1 - t0) * P]).then_inc(fc_xTs, 1)
                        if e:
                            dve.wait_ge(fc_o, CT * e)
                        for k in range(2 * FCH):
                            f, half = k // 2, k % 2
                            n = 2 * FCH * e + k
                            dve.wait_ge(fc_h, n + 1)
                            nc.vector.tensor_scalar(e_h[:, f, half * HC:(half + 1) * HC], banks[2 + n % 2][:, 0:HC],
                                                    b1_s[:, e, f:f + 1], 0.0, ALU.add, ALU.max).then_inc(fc_hs, 1)
                        if e >= 2:
                            dve.wait_ge(fc_out[e % 2], 16 * (e // 2))
                        for t in range(CT):
                            n = CT * e + t
                            dve.wait_ge(fc_o, n + 1)
                            nc.vector.tensor_tensor(e_o[e % 2][:, t, :], banks[4 + n % 2][:, 0:D], b2_s[:, e, :], ALU.add).then_inc(fc_os, 1)

                    link(nc.vector.tensor_tensor(base[:, :, :], base[:, :, :], bo_s[:, :].unsqueeze(1).to_broadcast([P, TILES, D]), ALU.add))
                    dve.wait_ge(gathered, 16 * TILES)
                    link(nc.vector.tensor_tensor(got[:, :, :], got[:, :, :], over_d(r[:, 0, :]), ALU.mult))
                    nc.vector.tensor_tensor(base[:, :, :], base[:, :, :], got[:, :, :], ALU.add).then_inc(base_ready, 1)
                    dve.wait_ge(base_ready, 1)

                @block.tensor
                def _(pe):
                    pe.wait_ge(const_ready, 4)
                    for n in range(NQ):
                        pe.wait_ge(xn_ready, (n * TB) // CH + 1)
                        if n >= 2:
                            pe.wait_ge(xT_copied, n - 1)
                        for i in range(TB):
                            ins = nc.tensor.transpose(banks[n % 2][:, i * P:(i + 1) * P], xn[:, n * TB + i, :], ident[:, :])
                        ins.then_inc(xT_made, 1)
                    pe.wait_ge(w_in, 16 * 4)
                    pe.wait_ge(small_in, 16 * 9)
                    for n in range(NQ):
                        pe.wait_ge(xT_copied, n + 1)
                        cols = xnT[:, n * BANK:(n + 1) * BANK]
                        for kind, w in enumerate((wq_s, wk_s)):
                            m = 2 * n + kind
                            if m >= 2:
                                pe.wait_ge(rest1, m - 1)
                            nc.tensor.matmul(banks[2 + m % 2][:, :], w[:, :], cols, start=True, stop=True).then_inc(proj, 1)
                        if n >= 1:
                            pe.wait_ge(v_copied, n)
                        for i in range(TB):
                            t = n * TB + i
                            ins = nc.tensor.matmul(banks[4][:, i * D:(i + 1) * D], xnT[:, t * P:(t + 1) * P], wv_s[:, :], start=True, stop=True)
                        ins.then_inc(v_made, 1)
                        for i in range(TB):
                            t = n * TB + i
                            ins = nc.tensor.matmul(banks[5][:, t * E:(t + 1) * E], xnT[:, t * P:(t + 1) * P], gw_s[:, :], start=True, stop=True)
                    ins.then_inc(logits_made, 1)
                    pe.wait_ge(maxima, 1)
                    nc.tensor.matmul(banks[6][0:1, 0:P], qkmax[:, 0:1], ident[:, :], start=True, stop=True)
                    nc.tensor.matmul(banks[6][0:1, P:2 * P], qkmax[:, 1:2], ident[:, :], start=True, stop=True).then_inc(maxima_made, 1)
                    pe.wait_ge(mask_ready, 1)
                    masks = maskb[:, :, :].rearrange("p t e -> p (t e)")
                    nc.tensor.matmul(banks[0][:, 0:TILES * E], below_b[:, :], masks, start=True, stop=True)
                    nc.tensor.matmul(banks[1][:, 0:TILES * E], ones_b[:, :], masks, start=True, stop=True).then_inc(counts_made, 1)
                    pe.wait_ge(index_ready, 2)
                    for e in range(E):
                        pe.wait_ge(fc_in[e % 2], 48 * (e // 2 + 1))
                        for half in range(2):
                            if e:
                                pe.wait_ge(fc_xTs, 2 * e - 1 + half)
                            for t in range(0 if half == 0 else TB, TB if half == 0 else CT):
                                ins = nc.tensor.transpose(banks[half][:, (t % TB) * P:(t % TB + 1) * P], e_x[e % 2][:, t, :], ident[:, :])
                            ins.then_inc(fc_xT, 1)
                        pe.wait_ge(fc_xTs, 2 * e + 2)
                        for k in range(2 * FCH):
                            f, half = k // 2, k % 2
                            n = 2 * FCH * e + k
                            if n >= 2:
                                pe.wait_ge(fc_hs, n - 1)
                            nc.tensor.matmul(banks[2 + n % 2][:, 0:HC], e_w1[e % 2][:, f * P:(f + 1) * P],
                                             e_xT[e % 2][:, half * HC:(half + 1) * HC], start=True, stop=True).then_inc(fc_h, 1)
                        pe.wait_ge(fc_hs, 2 * FCH * (e + 1))
                        for t in range(CT):
                            n = CT * e + t
                            if n >= 2:
                                pe.wait_ge(fc_os, n - 1)
                            for f in range(FCH):
                                ins = nc.tensor.matmul(banks[4 + n % 2][:, 0:D], e_h[:, f, t * P:(t + 1) * P], e_w2[e % 2][:, f, :],
                                                       start=f == 0, stop=f == FCH - 1)
                            ins.then_inc(fc_o, 1)

        att = ExitStack()
        with att:
            def asb(name, shape, dt=f32):
                return att.enter_context(nc.sbuf_tensor(name, shape, dt))

            def asem(name):
                return att.enter_context(nc.semaphore(name))

            negmax = [asb(f"negmax{i}", [P, SIDE_TILES]) for i in range(2)]
            nm_rest = asb("nm_rest", [P, SIDE_TILES])
            nm_parts = asb("nm_parts", [P, P], bf16)
            nm_rows = asb("nm_rows", [PARTS * SIDE_TILES, P], bf16)
            rsum = [asb(f"rsum{i}", [P, W, OTW]) for i in range(2)]
            gain = asb("gain", [P, W, OTW])
            terms = asb("terms", [P, W, OTW * HD])

            stack_in = [asem(f"stack_in{i}") for i in range(2)]
            rows_in = [asem(f"rows_in{i}") for i in range(2)]
            s_made, s_read, st_made, t_copied = (asem(n) for n in ("s_made", "s_read", "st_made", "t_copied"))
            split, nm_turned, nm_copied = asem("split"), asem("nm_turned"), asem("nm_copied")
            v_staged, exp_done, pv_done, pv_copied, turned, turned_copied = (asem(n) for n in (
                "v_staged", "exp_done", "pv_done", "pv_copied", "turned", "turned_copied"))
            cleared = asem("cleared")
            rsum_ready, summed, pool_step = asem("rsum_ready"), asem("summed"), asem("pool_step")

            pv_bank, tr_bank, s_bank, st_bank = banks[0:2], banks[2], banks[3:5], banks[5:7]
            SP_, TPAIRS = SIDE_B, SIDE_B

            def load_stack(sp, u, par):
                rows = pieces_dram[:, :, :, :, :].rearrange("k s f i c -> k (s f) i c")
                for i in range(PARTS):
                    blk = slice(i * PARTS * HD, (i + 1) * PARTS * HD)
                    sp.dma_start(Ks[par][blk, :], rows[1, ds(u * HD, HD), :, :].rearrange("d j c -> (d j) c")).then_inc(stack_in[par], 16)
                    for j in range(PARTS):
                        sp.dma_start(Qs[par][blk.start + j:blk.stop:PARTS, :], rows[0, ds(u * HD, HD), i, :]).then_inc(stack_in[par], 16)

            LOADS = (PARTS + PARTS * PARTS) * 16

            def load_rows(sp, u, par):
                sp.wait_ge(nm_copied, u + 2)
                for i in range(PARTS):
                    sp.dma_start(Qs[par][MAXROW + i:MAXROW + i + 1, :].rearrange("a (t c) -> a t c", c=P),
                                 nm_rows[i * SIDE_TILES:(i + 1) * SIDE_TILES, :]).then_inc(rows_in[par], 16)

            ROWS = PARTS * 16

            def dve_wait_rows_out(dve, pair, par):
                dve.wait_ge(rows_in[1 - par], ROWS * (pair + par))

            def pe_score_pair(pe, u, par, p, r):
                pe.wait_ge(s_read, u * SIDE_B + p + 1)
                for qt in range(QT):
                    ins = nc.tensor.matmul(s_bank[r][:, qt * SEQ:(qt + 1) * SEQ], Qs[par][0:PROD, ds(p * SEQ + qt * P, P)],
                                           Ks[par][0:PROD, ds(p * SEQ, SEQ)], start=True, stop=True)
                ins.then_inc(s_made, 1)

            def dve_score_pair(dve, u, par, p, r):
                dve.wait_ge(s_made, u * SIDE_B + p + 1)
                nc.vector.reduce_max(negmax[par][:, ds(p * QT, QT)], s_bank[r][:, :].rearrange("p (t k) -> p t k", k=SEQ),
                                     AX.X, negate=True).then_inc(s_read, 1)

            def dve_split(dve, u, par):
                n = SIDE_TILES
                dve.wait_ge(s_read, (u + 1) * SIDE_B + 2)
                dve.wait_ge(nm_turned, u + 1)
                nc.vector.tensor_copy(nm_parts[:, 0:n], negmax[par][:, :]).then_inc(split, 1)
                dve.wait_ge(split, 4 * u + 1)
                nc.vector.tensor_tensor(nm_rest[:, :], negmax[par][:, :], nm_parts[:, 0:n], ALU.subtract).then_inc(split, 1)
                dve.wait_ge(split, 4 * u + 2)
                nc.vector.tensor_copy(nm_parts[:, n:2 * n], nm_rest[:, :]).then_inc(split, 1)
                dve.wait_ge(split, 4 * u + 3)
                nc.vector.tensor_tensor(nm_parts[:, 2 * n:3 * n], nm_rest[:, :], nm_parts[:, n:2 * n], ALU.subtract).then_inc(split, 1)

            def pe_turn_max(pe, u):
                pe.wait_ge(split, 4 * u + 4)
                pe.wait_ge(nm_copied, u + 1)
                nc.tensor.transpose(bank_b[:, 0:P], nm_parts[:, :], identb[:, :]).then_inc(nm_turned, 1)

            def dve_turn_max(dve, u):
                dve.wait_ge(nm_turned, u + 2)
                nc.vector.tensor_copy(nm_rows[:, :], bank_b[0:PARTS * SIDE_TILES, 0:P]).then_inc(nm_copied, 1)

            def pe_transposed_pair(pe, u, par, p, r):
                pe.wait_ge(t_copied, u * SIDE_B + p + 1)
                for kt in range(QT):
                    ins = nc.tensor.matmul(st_bank[r][:, kt * SEQ:(kt + 1) * SEQ], Ks[par][0:STACK, ds(p * SEQ + kt * P, P)],
                                           Qs[par][0:STACK, ds(p * SEQ, SEQ)], start=True, stop=True)
                ins.then_inc(st_made, 1)

            def dve_transposed_pair(dve, u, par, p, r, after=None):
                dve.wait_ge(st_made, u * SIDE_B + p + 1)
                if after is not None:
                    dve.wait_ge(exp_done, after)
                nc.vector.tensor_copy(T[par][:, ds(p * BANK, BANK)], st_bank[r][:, :]).then_inc(t_copied, 1)

            def pe_products(pe, u, par, g, r):
                pe.wait_ge(v_staged, u + 1)
                pe.wait_ge(exp_done, g + 1)
                pe.wait_ge(pv_copied, g + 1)
                for half in range(2):
                    for kt in range(QT):
                        for j in range(GR):
                            blk = (2 * j + half) * QT + kt
                            ins = nc.tensor.matmul(pv_bank[r][VC * j:VC * (j + 1), half * SEQ:(half + 1) * SEQ], Vst[par][:, blk, :],
                                                   Pr[r][:, blk * SEQ:(blk + 1) * SEQ], start=kt == 0, stop=kt == QT - 1)
                ins.then_inc(pv_done, 1)

            def pe_turn(pe, g, r):
                pe.wait_ge(pv_copied, g + 1 + 2)
                pe.wait_ge(turned_copied, g + 1)
                for q in range(BANK // P):
                    ins = nc.tensor.transpose(tr_bank[:, q * P:(q + 1) * P], pv_s[r][:, q * P:(q + 1) * P], ident[:, :])
                ins.then_inc(turned, 1)

            def act_step(act, g, par, r):
                act.wait_ge(pv_done, g + 1)
                nc.scalar.activation(Pr[r][:, :], T[par][:, :], ACT.Exp, scale=cw[:, ds(g, 1)]).then_inc(exp_done, 1)

            def dve_products(dve, g, r):
                dve.wait_ge(pv_done, g + 1 + 2)
                dve.wait_ge(turned, g + 1)
                nc.vector.tensor_copy(pv_s[r][:, :], pv_bank[r][:, :]).then_inc(pv_copied, 1)

            def dve_turned(dve, u, g, par, w):
                dve.wait_ge(summed, u + 1)
                dve.wait_ge(turned, g + 1 + 2)
                dst = OT[:, par, ds(w * OTW * OC, OTW * OC)].rearrange("p (a c) -> p a c", c=OC)
                nc.vector.tensor_copy(dst, tr_bank[:, :].rearrange("p (a c) -> p a c", c=VC)[:, :, 0:OC]).then_inc(turned_copied, 1)

            def dve_rsum(dve, u, par):
                dve.wait_ge(turned_copied, W * (u + 1) + 1)
                row_sums = OT[:, par, :].rearrange("p (a c) -> p a c", c=OC)[:, :, HD:OC]
                nc.vector.reciprocal(rsum[par][:, :, :].rearrange("p w (a b) -> p (w a) b", b=1), row_sums).then_inc(rsum_ready, 1)

            def pool_unit(pool, u, par):
                pool.wait_ge(rsum_ready, u + 1)
                nc.gpsimd.tensor_tensor(gain[:, :, :], rsum[par][:, :, :], iw_s[:, :].unsqueeze(2).to_broadcast([P, W, OTW]),
                                        ALU.mult).then_inc(pool_step, 1)
                pool.wait_ge(pool_step, 5 * u + 1)
                o = OT[:, par, :].rearrange("p (a c) -> p a c", c=OC)[:, :, 0:HD]
                nc.gpsimd.tensor_tensor(terms[:, :, :].rearrange("p w (a d) -> p (w a) d", d=HD), o,
                                        gain[:, :, :].rearrange("p w a -> p (w a)").unsqueeze(2).to_broadcast([P, W * OTW, HD]),
                                        ALU.mult).then_inc(pool_step, 1)
                half, n = W // 2, 2
                while half > 1:
                    pool.wait_ge(pool_step, 5 * u + n)
                    nc.gpsimd.tensor_tensor(terms[:, 0:half, :], terms[:, 0:half, :], terms[:, half:2 * half, :], ALU.add).then_inc(pool_step, 1)
                    half, n = half // 2, n + 1
                pool.wait_ge(pool_step, 5 * u + n)
                first = u * HD + (u // H) * (SIDE_TILES - 1) * D
                dst = heads[:, ds(first, (SIDE_TILES - 1) * D + HD)]
                dst = bass.AP(dst.tensor, dst.offset, [dst.ap[0], [D, BANK // P], [GR * D, GR], [1, HD]])
                a, b = (terms[:, i, :].rearrange("p (q j d) -> p q j d", j=GR, d=HD) for i in range(2))
                nc.gpsimd.tensor_tensor(dst, a, b, ALU.add).then_inc(summed, 1)

            def stage_v(pool, u, par):
                nc.gpsimd.tensor_copy(Vst[par][:, :, 0:HD], Vall[:, ds(u * SIDE_TILES * HD, SIDE_TILES * HD)]
                                      .rearrange("p (t d) -> p t d", d=HD)).then_inc(v_staged, 1)

            A_PAIRS = SIDE_B // 4
            LAST = UNITS // 2 - 1

            def units(eng, unit):
                with eng.Fori(0, LAST) as i:
                    for par in range(2):
                        unit(i, par, True, True)
                unit(LAST, 0, False, True)
                unit(LAST, 1, False, False)

            def plain_sync(sp):
                for u in range(2):
                    load_stack(sp, u, u)
                for u in range(2):
                    load_rows(sp, u, u)

                def unit(pair, par, two_ahead, one_ahead):
                    u = 2 * pair + par
                    if two_ahead:
                        sp.wait_ge(st_made, SIDE_B * (u + 1))
                        load_stack(sp, u + 2, par)
                        load_rows(sp, u + 2, par)
                units(sp, unit)
                for i in range(2):
                    sp.wait_ge(rows_in[i], ROWS * UNITS // 2)
                    sp.wait_ge(stack_in[i], LOADS * UNITS // 2)

            def plain_tensor(pe):
                pe.sem_inc(pv_done, 2)
                pe.sem_inc(turned, 2)
                pe.sem_inc(nm_turned, 1)
                for u in range(2):
                    pe.wait_ge(stack_in[u], LOADS)
                    for p in range(SIDE_B):
                        pe_score_pair(pe, u, u, p, p % 2)
                    pe_turn_max(pe, u)
                    if u == 0:
                        pe.wait_ge(rows_in[0], ROWS)
                        for p in range(SIDE_B):
                            pe_transposed_pair(pe, 0, 0, p, p % 2)

                def unit(pair, par, two_ahead, one_ahead):
                    u = 2 * pair + par
                    with pe.Fori(0, 2) as k:
                        for r in range(2):
                            pe_products(pe, u, par, u * W + 2 * k + r, r)
                            if two_ahead:
                                if r == 0:
                                    pe.wait_ge(stack_in[par], LOADS * (pair + 2))
                                for c in range(A_PAIRS):
                                    pe_score_pair(pe, u + 2, par, (2 * k + r) * A_PAIRS + c, c % 2)
                            pe_turn(pe, u * W + 2 * k + r, r)
                    with pe.Fori(0, 4) as k:
                        for r in range(2):
                            pe_products(pe, u, par, u * W + 4 + 2 * k + r, r)
                            if one_ahead:
                                if r == 0:
                                    pe.wait_ge(rows_in[1 - par], ROWS * (pair + 1 + par))
                                pe_transposed_pair(pe, u + 1, 1 - par, 2 * k + r, r)
                            pe_turn(pe, u * W + 4 + 2 * k + r, r)
                    if two_ahead:
                        pe_turn_max(pe, u + 2)
                    with pe.Fori(0, 2) as k:
                        for r in range(2):
                            pe_products(pe, u, par, u * W + 12 + 2 * k + r, r)
                            pe_turn(pe, u * W + 12 + 2 * k + r, r)
                units(pe, unit)

            def plain_scalar(act):
                def unit(pair, par, two_ahead, one_ahead):
                    u = 2 * pair + par
                    act.wait_ge(t_copied, SIDE_B * (u + 1) + 2)
                    with act.Fori(0, W // 2) as k:
                        for r in range(2):
                            act_step(act, u * W + 2 * k + r, par, r)
                units(act, unit)

            def plain_vector(dve):
                dve.sem_inc(s_read, 2)
                dve.sem_inc(t_copied, 2)
                dve.sem_inc(pv_copied, 2)
                dve.sem_inc(turned_copied, 1)
                dve.sem_inc(nm_copied, 1)
                nc.vector.memset(nm_parts[:, :], 0.0).then_inc(cleared, 1)
                dve.wait_ge(cleared, 1)
                for u in range(2):
                    for p in range(SIDE_B):
                        dve_score_pair(dve, u, u, p, p % 2)
                    dve_split(dve, u, u)
                    if u == 1:
                        dve_wait_rows_out(dve, 0, 1)
                    dve_turn_max(dve, u)
                    if u == 0:
                        for p in range(SIDE_B):
                            dve_transposed_pair(dve, 0, 0, p, p % 2)

                def unit(pair, par, two_ahead, one_ahead):
                    u = 2 * pair + par
                    with dve.Fori(0, 2) as k:
                        for r in range(2):
                            dve_products(dve, u * W + 2 * k + r, r)
                            if two_ahead:
                                for c in range(A_PAIRS):
                                    dve_score_pair(dve, u + 2, par, (2 * k + r) * A_PAIRS + c, c % 2)
                            dve_turned(dve, u, u * W + 2 * k + r, par, 2 * k + r)
                    if two_ahead:
                        dve_split(dve, u + 2, par)
                    with dve.Fori(0, 4) as k:
                        for r in range(2):
                            dve_products(dve, u * W + 4 + 2 * k + r, r)
                            if one_ahead:
                                dve_transposed_pair(dve, u + 1, 1 - par, 2 * k + r, r, after=W * u + 1)
                            dve_turned(dve, u, u * W + 4 + 2 * k + r, par, 4 + 2 * k + r)
                    if two_ahead:
                        dve_wait_rows_out(dve, pair + 1, par)
                        dve_turn_max(dve, u + 2)
                    with dve.Fori(0, 2) as k:
                        for r in range(2):
                            dve_products(dve, u * W + 12 + 2 * k + r, r)
                            dve_turned(dve, u, u * W + 12 + 2 * k + r, par, 12 + 2 * k + r)
                    dve_rsum(dve, u, par)
                units(dve, unit)

            def plain_gpsimd(pool):
                pool.sem_inc(summed, 2)
                for u in range(2):
                    stage_v(pool, u, u)

                def unit(pair, par, two_ahead, one_ahead):
                    u = 2 * pair + par
                    pool_unit(pool, u, par)
                    if two_ahead:
                        stage_v(pool, u + 2, par)
                units(pool, unit)

            Qg, Kg = Qs[0][0:PROD, 0:SEQ], Ks[0][0:PROD, 0:SEQ]
            g_raw, g_s, g_n, g_a, g_b, g_cos, g_y, g_p = (T[0][:, i * SEQ:(i + 1) * SEQ] for i in range(8))
            g_acc = T[0][:, 8 * SEQ:9 * SEQ]
            g_accT = T[0][:, 9 * SEQ:10 * SEQ]
            g_col = asb("g_col", [P, 4])
            g_in, g_start, g_scores, g_angle, g_sine, g_exp, g_sum, g_chain, g_turned, g_copied, g_out, g_done = (asem(n) for n in (
                "g_in", "g_start", "g_scores", "g_angle", "g_sine", "g_exp", "g_sum", "g_chain", "g_turned", "g_copied",
                "g_out", "g_done"))
            CHAIN = 13

            def general_tiles(eng, tile):
                with eng.Fori(0, UNITS) as u:
                    with eng.Fori(0, SIDE_B) as b:
                        tile(u, b, (u * SIDE_B + b) * QT)

            def general_sync(sp):
                def tile(u, b, n):
                    sp.wait_ge(g_scores, n + QT)
                    rows = pieces_dram[:, :, :, :, :].rearrange("k s f i c -> k (s f) i c")
                    for i in range(PARTS):
                        for j in range(PARTS):
                            at = slice(i * PARTS * HD + j, (i + 1) * PARTS * HD, PARTS)
                            sp.dma_start(Qs[0][at, 0:SEQ], rows[0, ds(u * HD, HD), i, ds(b * SEQ, SEQ)]).then_inc(g_in, 16)
                            sp.dma_start(Ks[0][at, 0:SEQ], rows[1, ds(u * HD, HD), j, ds(b * SEQ, SEQ)]).then_inc(g_in, 16)
                general_tiles(sp, tile)
                sp.wait_ge(g_in, 2 * PARTS * PARTS * 16 * UNITS * SIDE_B)

            def general_tensor(pe):
                pe.sem_inc(g_scores, QT)

                def tile(u, b, n0):
                    for qt in range(QT):
                        n = n0 + qt
                        if qt == 0:
                            pe.wait_ge(g_in, (u * SIDE_B + b + 1) * (2 * PARTS * PARTS * 16))
                        pe.wait_ge(g_done, n + 1)
                        nc.tensor.matmul(banks[0][:, 0:SEQ], Qg[:, qt * P:(qt + 1) * P], Kg, start=True, stop=True).then_inc(g_scores, 1)
                        pe.wait_ge(g_sum, W * (n + 1))
                        for kt in range(QT):
                            ins = nc.tensor.transpose(banks[1][:, kt * P:(kt + 1) * P], g_acc[:, kt * P:(kt + 1) * P], ident[:, :])
                        ins.then_inc(g_turned, 1)
                        pe.wait_ge(g_copied, n + 1)
                        for kt in range(QT):
                            ins = nc.tensor.matmul(banks[2][:, 0:HD], g_accT[:, kt * P:(kt + 1) * P],
                                                   Vall[:, ds(u * SIDE_TILES * HD + (b * QT + kt) * HD, HD)], start=kt == 0, stop=kt == QT - 1)
                        ins.then_inc(g_out, 1)
                general_tiles(pe, tile)

            def general_scalar(act):
                def tile(u, b, n0):
                    for qt in range(QT):
                        with act.Fori(0, W) as w:
                            m = (n0 + qt) * W + w
                            act.wait_ge(g_angle, m + 1)
                            nc.scalar.activation(g_cos, g_b, ACT.Sin).then_inc(g_sine, 1)
                            act.wait_ge(g_chain, CHAIN * m + 11)
                            nc.scalar.activation(g_p, g_y, ACT.Exp, bias=g_col[:, 0:1], accum_out=g_col[:, 1:2]).then_inc(g_exp, 1)
                general_tiles(act, tile)

            def general_vector(dve):
                dve.sem_inc(g_done, 1)

                def tile(u, b, n0):
                    for qt in range(QT):
                        n = n0 + qt
                        dve.wait_ge(g_scores, n + 1 + QT)
                        nc.vector.tensor_copy(g_raw, banks[0][:, 0:SEQ]).then_inc(g_start, 1)
                        nc.vector.memset(g_acc, 0.0).then_inc(g_start, 1)
                        with dve.Fori(0, W) as w:
                            m = n * W + w

                            def link(k, ins):
                                ins.then_inc(g_chain, 1)
                                dve.wait_ge(g_chain, CHAIN * m + k)

                            dve.wait_ge(g_start, 2 * (n + 1))
                            link(1, nc.vector.tensor_scalar(g_s, g_raw, cw[:, ds(u * W + w, 1)], None, ALU.mult))
                            link(2, nc.vector.scalar_tensor_tensor(g_a, g_s, KERR, g_s, ALU.mult, ALU.mult))
                            link(3, nc.vector.tensor_scalar(g_n, g_a, 1.0 / TWO_PI, 0.25, ALU.mult, ALU.add))
                            link(4, nc.vector.tensor_scalar(g_b, g_n, ROUND, None, ALU.add))
                            link(5, nc.vector.tensor_scalar(g_n, g_b, -ROUND, None, ALU.add))
                            link(6, nc.vector.scalar_tensor_tensor(g_b, g_n, -C1, g_a, ALU.mult, ALU.add))
                            link(7, nc.vector.scalar_tensor_tensor(g_a, g_n, -C2, g_b, ALU.mult, ALU.add))
                            link(8, nc.vector.scalar_tensor_tensor(g_b, g_n, -C3, g_a, ALU.mult, ALU.add))
                            link(9, nc.vector.tensor_scalar(g_a, g_b, np.pi / 2, np.pi, ALU.add, ALU.min))
                            nc.vector.tensor_scalar(g_b, g_a, -np.pi, None, ALU.max).then_inc(g_angle, 1)
                            dve.wait_ge(g_sine, m + 1)
                            link(10, nc.vector.tensor_tensor(g_y, g_s, g_cos, ALU.mult))
                            link(11, nc.vector.reduce_max(g_col[:, 0:1], g_y, AX.X, negate=True))
                            dve.wait_ge(g_exp, m + 1)
                            link(12, nc.vector.reciprocal(g_col[:, 2:3], g_col[:, 1:2]))
                            link(13, nc.vector.tensor_tensor(g_col[:, 3:4], g_col[:, 2:3], iw_s[:, ds(w, 1)], ALU.mult))
                            nc.vector.scalar_tensor_tensor(g_acc, g_p, g_col[:, 3:4], g_acc, ALU.mult, ALU.add).then_inc(g_sum, 1)
                            dve.wait_ge(g_sum, m + 1)
                        dve.wait_ge(g_turned, n + 1)
                        nc.vector.tensor_copy(g_accT, banks[1][:, 0:SEQ]).then_inc(g_copied, 1)
                        dve.wait_ge(g_out, n + 1)
                        first = u * HD + (u // H) * (SIDE_TILES - 1) * D + (b * QT + qt) * D
                        nc.vector.tensor_copy(heads[:, ds(first, HD)], banks[2][:, 0:HD]).then_inc(g_done, 1)
                general_tiles(dve, tile)
                dve.wait_ge(g_done, UNITS * SIDE_B * QT + 1)

            with nc.Block() as block:

                @block.sync
                def _(sp):
                    plain = sp.value_load(flag[0:1, 0:1], min_val=0, max_val=1)
                    with sp.If(plain == 1):
                        plain_sync(sp)
                    with sp.Else():
                        general_sync(sp)

                @block.tensor
                def _(pe):
                    plain = pe.value_load(flag[0:1, 0:1], min_val=0, max_val=1)
                    with pe.If(plain == 1):
                        plain_tensor(pe)
                    with pe.Else():
                        general_tensor(pe)

                @block.scalar
                def _(act):
                    plain = act.value_load(flag[0:1, 0:1], min_val=0, max_val=1)
                    with act.If(plain == 1):
                        plain_scalar(act)
                    with act.Else():
                        general_scalar(act)

                @block.vector
                def _(dve):
                    plain = dve.value_load(flag[0:1, 0:1], min_val=0, max_val=1)
                    with dve.If(plain == 1):
                        plain_vector(dve)
                    with dve.Else():
                        general_vector(dve)

                @block.gpsimd
                def _(pool):
                    plain = pool.value_load(flag[0:1, 0:1], min_val=0, max_val=1)
                    with pool.If(plain == 1):
                        plain_gpsimd(pool)

        fin = ExitStack()
        with fin:
            def fsem(name):
                return fin.enter_context(nc.semaphore(name))

            hT = [fin.enter_context(nc.sbuf_tensor(f"hT{i}", [P, BANK], f32)) for i in range(2)]
            h_turned, h_copied, o_made, o_added, stored = (fsem(n) for n in (
                "h_turned", "h_copied", "o_made", "o_added", "stored"))
            TB = BANK // P
            hv = heads[:, :].rearrange("p (t f) -> p t f", f=D)
            with nc.Block() as block:

                @block.tensor
                def _(pe):
                    def project(n):
                        pe.wait_ge(h_copied, n + 1)
                        if n >= 2:
                            pe.wait_ge(o_added, n - 1)
                        for i in range(TB):
                            ins = nc.tensor.matmul(banks[2 + n % 2][:, i * D:(i + 1) * D], hT[n % 2][:, i * P:(i + 1) * P],
                                                   wo_s[:, :], start=True, stop=True)
                        ins.then_inc(o_made, 1)

                    for n in range(TILES // TB):
                        if n >= 2:
                            pe.wait_ge(h_copied, n - 1)
                        for i in range(TB):
                            t = n * TB + i
                            ins = nc.tensor.transpose(banks[n % 2][:, i * P:(i + 1) * P],
                                                      hv[:, t, :], ident[:, :])
                        ins.then_inc(h_turned, 1)
                        if n:
                            project(n - 1)
                    project(TILES // TB - 1)

                @block.scalar
                def _(act):
                    for n in range(TILES // TB):
                        act.wait_ge(h_turned, n + 1)
                        if n >= 2:
                            act.wait_ge(o_made, n - 1)
                        nc.scalar.activation(hT[n % 2][:, :], banks[n % 2][:, :], ACT.Copy).then_inc(h_copied, 1)

                @block.vector
                def _(dve):
                    for n in range(TILES // TB):
                        dve.wait_ge(o_made, n + 1)
                        b = base[:, n * TB:(n + 1) * TB, :]
                        nc.vector.tensor_tensor(b, b, banks[2 + n % 2][:, :].rearrange("p (t d) -> p t d", d=D), ALU.add).then_inc(o_added, 1)

                @block.sync
                def _(sp):
                    ov = out.rearrange("b (t p) d -> p (b t) d", p=P)
                    for n in range(TILES // TB):
                        sp.wait_ge(o_added, n + 1)
                        sp.dma_start(ov[:, n * TB:(n + 1) * TB, :], base[:, n * TB:(n + 1) * TB, :]).then_inc(stored, 16)
                    sp.wait_ge(stored, 16 * (TILES // TB))


_INS = ['L0_attn_x', 'L0_attn_Wq', 'L0_attn_bq', 'L0_attn_Wk', 'L0_attn_bk', 'L0_attn_Wv', 'L0_attn_bv', 'L0_attn_Wo',
        'L0_attn_bo', 'L0_attn_phase_modulators', 'L0_attn_interference_weights', 'L0_ffn_gate_w', 'L0_ffn_w1',
        'L0_ffn_b1', 'L0_ffn_w2', 'L0_ffn_b2']


def kernel(**inputs):
    import numpy as _np
    import concourse.bacc as _bacc
    from concourse import mybir as _mybir
    from concourse.bass_utils import run_bass_kernel_spmd as _run

    nc = _bacc.Bacc("TRN2", target_bir_lowering=False, num_devices=1)
    arrays, args = {}, []
    for name in _INS:
        a = _np.ascontiguousarray(inputs[name])
        arrays[f"in_{name}_dram"] = a
        args.append(nc.dram_tensor(f"in_{name}_dram", a.shape, _mybir.dt.from_np(a.dtype), kind="ExternalInput").ap())
    shape = inputs['L0_attn_x'].shape
    out = nc.dram_tensor("out_0_dram", shape, _mybir.dt.float32, kind="ExternalOutput").ap()
    attention_and_experts(nc, *args, out)
    r = _run(nc, [arrays], core_ids=[0])
    return r.results[0]["out_0_dram"]
```

```python
import numpy as np
import concourse.bass as bass
from concourse import mybir
from contextlib import ExitStack


def attention_and_experts(nc, x, Wq, bq, Wk, bk, Wv, bv, Wo, bo, phase, weights, gate_w, w1, b1, w2, b2, out):
    f32, bf16, i32 = mybir.dt.float32, mybir.dt.bfloat16, mybir.dt.int32
    ALU, ACT, AX = mybir.AluOpType, mybir.ActivationFunctionType, mybir.AxisListType
    ds = bass.ds

    BATCH, SEQ, D = x.shape
    W, H = phase.shape
    HD = D // H
    E, _, DFF = w1.shape
    P = 128
    TOK = BATCH * SEQ
    TILES = TOK // P
    QT = SEQ // P
    SIDES = 2
    SIDE_B = BATCH // SIDES
    SIDE_TILES = TILES // SIDES
    SIDE_TOK = TOK // SIDES
    UNITS = SIDES * H
    BLK = QT * SEQ
    COLS = SIDE_B * BLK
    BANK = 512
    CAP = -(-5 * TOK // (4 * E))
    CT = CAP // P
    HC = CAP // 2
    FCH = DFF // P
    SCALE = 1.0 / np.sqrt(HD)
    KERR = 2.7e-18 * 1000000.0
    EPS = 1e-5
    PARTS = 3
    PROD = PARTS * PARTS * HD
    MAXROW = 96
    STACK = MAXROW + PARTS
    VC = 32
    OC = HD + 1
    GR = 4
    OTW = (BANK // P) * GR
    TWO_PI = 2.0 * np.pi
    C1 = 6.28125
    C2 = float(np.float32(np.round((TWO_PI - C1) * 2.0**21) / 2.0**21))
    C3 = TWO_PI - C1 - C2
    ROUND = 1.5 * 2.0**23
    S_PLAIN = 0.9 * np.sqrt(2.0**-12 / KERR)

    parts_dram = nc.dram_tensor("qk_parts", (2, SIDES, D, PARTS, SIDE_TOK), bf16, kind="Internal").ap()
    slots_dram = nc.dram_tensor("dispatched", (E * CAP + TOK, D), f32, kind="Internal").ap()
    expert_dram = nc.dram_tensor("expert_out", (E * CAP, D), f32, kind="Internal").ap()

    TB = BANK // P
    NQ = TOK // BANK
    NQ_SIDE = NQ // SIDES
    CHUNKS = 4
    CH = TILES // CHUNKS
    WH = W // 2
    RING = 2
    ZCOLS = 1024

    ctx = ExitStack()
    with ctx:
        def sb(name, shape, dt=f32):
            return ctx.enter_context(nc.sbuf_tensor(name, shape, dt))

        def sem(name):
            return ctx.enter_context(nc.semaphore(name))

        ident = sb("ident", [P, P])
        identb = sb("identb", [P, P], bf16)
        ones_b = sb("ones_b", [P, P], bf16)
        below_b = sb("below_b", [P, P], bf16)
        one_col = sb("one_col", [P, 1])
        order8, ebase = sb("order8", [P, E]), sb("ebase", [P, E])
        token_row = sb("token_row", [P, TILES])
        wq_s, wk_s, wv_s, wo_s = (sb(n, [P, D]) for n in ("wq_s", "wk_s", "wv_s", "wo_s"))
        bq_s, bk_s = sb("bq_s", [P, 1]), sb("bk_s", [P, 1])
        bv_s, bo_s = sb("bv_s", [P, D]), sb("bo_s", [P, D])
        gw_s = sb("gw_s", [P, E])
        b1_s = sb("b1_s", [P, E, FCH])
        iw_s = sb("iw_s", [P, W])
        cw = sb("cw", [P, UNITS * W])
        base = sb("base", [P, TILES, D])
        xnT = sb("xnT", [P, TOK])
        heads = xnT
        region = sb("region", [P, TOK])
        xn = region[:, :].rearrange("p (t d) -> p t d", d=D)
        Vall = sb("Vall", [P, UNITS * SIDE_TILES * HD])
        T = [sb(f"T{i}", [P, COLS]) for i in range(2)]
        Pr = [sb(f"Pr{i}", [P, COLS]) for i in range(RING)]
        work = sb("work", [P, 2 * CAP + 4 * DFF])
        PARTW = PARTS * BANK // 2
        part = [work[:, i * PARTW:(i + 1) * PARTW].bitcast(bf16).rearrange("p (i c) -> p i c", i=PARTS) for i in range(2)]
        part0 = [Pr[m // NQ_SIDE][:, (m % NQ_SIDE) * PARTW:(m % NQ_SIDE + 1) * PARTW].bitcast(bf16).rearrange("p (i c) -> p i c", i=PARTS)
                 for m in range(2 * NQ_SIDE)]
        rest = [work[:, 2 * PARTW + i * BANK:2 * PARTW + (i + 1) * BANK] for i in range(2)]
        e_x = [region[:, i * CAP:(i + 1) * CAP].rearrange("p (t d) -> p t d", d=D) for i in range(2)]
        e_h = region[:, 2 * CAP:2 * CAP + FCH * CAP].rearrange("p (f c) -> p f c", f=FCH)
        e_xT = work[:, 0:CAP]
        e_o = work[:, CAP:2 * CAP].rearrange("p (t d) -> p t d", d=D)
        e_w1 = [work[:, 2 * CAP + i * DFF:2 * CAP + (i + 1) * DFF] for i in range(2)]
        e_w2 = [work[:, 2 * CAP + (2 + i) * DFF:2 * CAP + (3 + i) * DFF].rearrange("p (f d) -> p f d", d=D) for i in range(2)]
        e_b2 = [sb(f"e_b2{i}", [P, D]) for i in range(2)]
        lg = sb("lg", [P, 6, TILES * E])
        maskb = sb("maskb", [P, TILES * E], bf16)
        r = sb("r", [P, 10, TILES])
        idx_scatter, idx_gather = sb("idx_scatter", [P, TILES], i32), sb("idx_gather", [P, TILES], i32)
        Qs = [sb(f"Qs{i}", [P, SIDE_TOK], bf16) for i in range(2)]
        Ks = [sb(f"Ks{i}", [P, SIDE_TOK], bf16) for i in range(2)]
        Vst = [sb(f"Vst{i}", [P, SIDE_TILES, VC]) for i in range(2)]
        pv_s = [sb(f"pv_s{i}", [P, BANK]) for i in range(2)]
        OT = [sb(f"OT{i}", [P, WH * OTW * OC]) for i in range(2)]
        rsum = [sb(f"rsum{i}", [P, WH * OTW]) for i in range(2)]
        gain = sb("gain", [P, WH * OTW])
        terms = sb("terms", [P, WH + 1, OTW * HD])
        negmax = [sb(f"negmax{i}", [P, SIDE_TILES]) for i in range(2)]
        nm_rest = sb("nm_rest", [P, SIDE_TILES])
        nm_parts = sb("nm_parts", [P, P], bf16)
        nm_rows = sb("nm_rows", [PARTS * SIDE_TILES, P], bf16)
        flag = sb("flag", [1, 1], i32)

        banks = [ctx.enter_context(nc.psum_tensor(f"bank{i}", [P, BANK], f32)) for i in range(7)]
        bank_b = ctx.enter_context(nc.psum_tensor("bank_b", [P, 2 * BANK], bf16))
        pv_bank, tr_bank, sc_bank, x_bank = banks[0:2], banks[2], banks[3:5], banks[5:7]

        stack_in = [sem(f"stack_in{i}") for i in range(2)]
        LOADS = (1 + PARTS) * 16
        parts_out = [sem(f"parts_out{i}") for i in range(2)]
        small_in, const_ready = sem("small_in"), sem("const_ready")
        SMALL = 10 * 16

        def over(a, n):
            return a.unsqueeze(2).to_broadcast([P, a.shape[1], n])

        def load_stack(sp, u, par, c0=0, n=SIDE_TOK, done=None):
            rows = parts_dram[:, :, :, :, :].rearrange("k s f i c -> k (s f) i c")
            q, k = (rows[kind, ds(u * HD, HD), :, ds(c0, n)] for kind in range(2))
            (d_step, _), (i_step, _), (c_step, _) = k.ap
            to = slice(0, n) if done else slice(c0, c0 + n)
            sp.dma_start(Ks[par][0:PROD, to], bass.AP(k.tensor, k.offset, [[0, PARTS], [i_step, HD * PARTS], [c_step, n]])
                         ).then_inc(done or stack_in[par], 16)
            for i in range(PARTS):
                qi = q[:, i, :]
                sp.dma_start(Qs[par][i * PARTS * HD:(i + 1) * PARTS * HD, to],
                             bass.AP(qi.tensor, qi.offset, [[d_step, HD], [0, PARTS], [c_step, n]])).then_inc(done or stack_in[par], 16)

        def store_parts(sp, m):
            n, kind = m // 2, m % 2
            col = (n % NQ_SIDE) * BANK
            src = part0[m] if n < NQ_SIDE else part[m % 2]
            sp.dma_start(parts_dram[kind, n // NQ_SIDE, :, :, col:col + BANK], src).then_inc(parts_out[m // 4 if n < NQ_SIDE else m % 2], 16)

        def v_to_tiles(n, bank):
            side, ts = n // NQ_SIDE, (n % NQ_SIDE) * TB
            size = H * SIDE_TILES * HD
            dst = Vall[:, side * size:(side + 1) * size].rearrange("p (h t d) -> p t h d", h=H, d=HD)
            for i in range(TB):
                ins = nc.vector.tensor_tensor(dst[:, ts + i, :, :], bank[:, i * D:(i + 1) * D].rearrange("p (h d) -> p h d", d=HD),
                                              bv_s[:, :].rearrange("p (h d) -> p h d", d=HD), ALU.add)
            return ins

        setup = ExitStack()
        with setup:
            def ssem(name):
                return setup.enter_context(nc.semaphore(name))

            zeros = T[1][:, COLS - ZCOLS:COLS]
            phase_s = T[0][:, 0:W * H]
            ph = T[0][:, W * H:5 * W * H].rearrange("p (a b) -> p a b", a=4)
            stats = T[0][:, 1280:1280 + 6 * TILES].rearrange("p (t s) -> p t s", s=6)
            mv = T[0][:, 1536:1536 + 2 * TILES].rearrange("p (t s) -> p t s", s=2)
            ln = T[0][:, 1664:1664 + 6 * TILES].rearrange("p (a t) -> p a t", a=6)
            wsq = T[0][:, 2048:2048 + 2 * D]
            brow = T[0][0:1, 2560:2560 + 2 * D]
            bound = T[0][0:1, 3072:3072 + 4 * D]
            one = T[0][0:1, 3584:3588]
            gb_rows = T[1][0:E * FCH, 0:2 * P].rearrange("p (a b) -> p a b", a=2)
            one_root = T[1][:, 2 * P:2 * P + 1]

            x_in = [ssem(f"x_in{c}") for c in range(CHUNKS)]
            wqk_in, w_in, zeroed, pool_const = ssem("wqk_in"), ssem("w_in"), ssem("zeroed"), ssem("pool_const")
            chain, var_ready, root_ready, xn_ready = (ssem(n) for n in ("chain", "var_ready", "root_ready", "xn_ready"))
            xT_made, xT_copied = ssem("xT_made"), ssem("xT_copied")
            proj, part1, rest1, part2, part3 = (ssem(n) for n in ("proj", "part1", "rest1", "part2", "part3"))
            v_made, v_copied = ssem("v_made"), ssem("v_copied")
            angle, sine = ssem("angle"), ssem("sine")
            gb_turned, gb_copied = ssem("gb_turned"), ssem("gb_copied")
            w_squared, norms_made, norms_ready = ssem("w_squared"), ssem("norms_made"), ssem("norms_ready")

            with nc.Block() as block:

                @block.sync
                def _(sp):
                    xv = x.rearrange("b (t p) d -> p (b t) d", p=P)
                    for c in range(CHUNKS):
                        sp.dma_start(base[:, c * CH:(c + 1) * CH, :], xv[:, c * CH:(c + 1) * CH, :]).then_inc(x_in[c], 16)
                        if c == 0:
                            for dst, src in ((wq_s, Wq), (wk_s, Wk)):
                                sp.dma_start(dst[:, :], src).then_inc(wqk_in, 16)
                    for dst, src in ((wv_s, Wv), (wo_s, Wo)):
                        sp.dma_start(dst[:, :], src).then_inc(w_in, 16)
                    sp.wait_ge(const_ready, 1)
                    rows = P * ZCOLS // D
                    for z in range(E * CAP // rows):
                        sp.dma_start(slots_dram[z * rows:(z + 1) * rows, :].rearrange("(p a) d -> p (a d)", p=P), zeros).then_inc(zeroed, 16)

                    def load_half(half):
                        sp.wait_ge(parts_out[half], 16 * NQ_SIDE)
                        for u in range(2):
                            load_stack(sp, u, u, half * SIDE_TOK // 2, SIDE_TOK // 2)

                    for m in range(2 * NQ_SIDE):
                        sp.wait_ge(part3, m + 1)
                        store_parts(sp, m)
                        if m == 5:
                            sp.wait_ge(pool_const, 13)
                            load_half(0)
                    load_half(1)
                    sp.wait_ge(zeroed, 16 * (E * CAP // rows))

                @block.gpsimd
                def _(pool):
                    pool.memset(zeros, 0.0).then_inc(const_ready, 1)
                    pool.memset(one_col[:, :], 1.0).then_inc(const_ready, 1)
                    pool.memset(ident[:, :], 0.0).then_inc(pool_const, 1)
                    pool.memset(identb[:, :], 0.0).then_inc(pool_const, 1)
                    pool.memset(ones_b[:, :], 1.0).then_inc(pool_const, 1)
                    pool.wait_ge(pool_const, 3)
                    for m in (ident, identb):
                        pool.affine_select(out=m[:, :], in_=m[:, :], compare_op=ALU.not_equal, fill=1.0,
                                           base=0, pattern=[[-1, P]], channel_multiplier=1).then_inc(const_ready, 1)
                    for i in range(2):
                        pool.memset(Qs[i][:, :], 0.0).then_inc(pool_const, 1)
                        pool.memset(Ks[i][:, :], 0.0).then_inc(pool_const, 1)
                        pool.memset(Vst[i][:, :, :], 0.0).then_inc(pool_const, 1)
                    pool.wait_ge(pool_const, 9)
                    for i in range(2):
                        pool.memset(Vst[i][:, :, HD:OC], 1.0).then_inc(pool_const, 1)
                    for i in range(2):
                        pool.wait_ge(pool_const, 11 + i)
                        pool.memset(Ks[i][MAXROW:STACK, :], 1.0).then_inc(pool_const, 1)
                    pool.wait_ge(pool_const, 13)
                    pool.memset(nm_parts[:, :], 0.0)
                    pool.affine_select(out=below_b[:, :], in_=ones_b[:, :], compare_op=ALU.is_gt, fill=0.0,
                                       base=0, pattern=[[1, P]], channel_multiplier=-1)
                    pool.iota(order8[:, :], pattern=[[-1, E]], base=E, channel_multiplier=0, allow_small_or_imprecise_dtypes=True)
                    pool.iota(ebase[:, :], pattern=[[CAP, E]], base=0, channel_multiplier=0, allow_small_or_imprecise_dtypes=True)
                    pool.iota(token_row[:, :], pattern=[[P, TILES]], base=E * CAP, channel_multiplier=1,
                              allow_small_or_imprecise_dtypes=True)

                @block.scalar
                def _(act):
                    act.dma_start(bq_s[:, :], bq.rearrange("(d a) -> d a", a=1)).then_inc(small_in, 16)
                    act.dma_start(bk_s[:, :], bk.rearrange("(d a) -> d a", a=1)).then_inc(small_in, 16)
                    act.dma_start(brow[:, 0:D], bq.rearrange("(a d) -> a d", a=1)).then_inc(small_in, 16)
                    act.dma_start(brow[:, D:2 * D], bk.rearrange("(a d) -> a d", a=1)).then_inc(small_in, 16)
                    act.dma_start(phase_s, phase.rearrange("w h -> (w h)").partition_broadcast(P)).then_inc(small_in, 16)
                    act.dma_start(iw_s[:, :], weights.partition_broadcast(P)).then_inc(small_in, 16)
                    act.dma_start(bv_s[:, :], bv.partition_broadcast(P)).then_inc(small_in, 16)
                    act.dma_start(bo_s[:, :], bo.partition_broadcast(P)).then_inc(small_in, 16)
                    act.dma_start(gb_rows[0:E * FCH, 0, :], b1.rearrange("e (f p) -> (e f) p", p=P)).then_inc(small_in, 16)
                    act.dma_start(gb_rows[0:E, 1, :], gate_w).then_inc(small_in, 16)

                    def root(c):
                        act.wait_ge(var_ready, c + 1)
                        s = slice(c * CH, (c + 1) * CH)
                        nc.scalar.activation(ln[:, 1, s], ln[:, 0, s], ACT.Sqrt).then_inc(root_ready, 1)

                    act.wait_ge(const_ready, 2)
                    nc.scalar.activation(one_root, one_col[:, :], ACT.Sqrt)
                    root(0)
                    root(1)

                    def copy_xT(n):
                        act.wait_ge(xT_made, n + 1)
                        nc.scalar.activation(xnT[:, n * BANK:(n + 1) * BANK], banks[n % 2][:, :], ACT.Copy).then_inc(xT_copied, 1)

                    def first_part(m):
                        act.wait_ge(proj, m + 1)
                        nc.scalar.activation(part0[m][:, 0, :], banks[2 + m % 4][:, :], ACT.Identity,
                                             bias=(bq_s, bk_s)[m % 2][:, :]).then_inc(part1, 1)

                    def second_part(m):
                        act.wait_ge(rest1, m + 1)
                        nc.scalar.activation(part0[m][:, 1, :], rest[m % 2], ACT.Copy).then_inc(part2, 1)

                    copy_xT(0)
                    act.wait_ge(small_in, SMALL)
                    for m in range(2 * NQ_SIDE):
                        if m % 2 == 0 and m // 2 + 1 < NQ_SIDE:
                            copy_xT(m // 2 + 1)
                        first_part(m)
                        if m:
                            second_part(m - 1)
                    second_part(2 * NQ_SIDE - 1)
                    root(2)
                    root(3)
                    act.wait_ge(norms_made, 1)
                    nc.scalar.activation(bound[:, 0:2 * D], banks[6][0:1, 0:2 * D], ACT.Sqrt, scale=float(D)).then_inc(norms_ready, 1)
                    act.wait_ge(angle, 1)
                    nc.scalar.activation(ph[:, 2, :], ph[:, 1, :], ACT.Sin).then_inc(sine, 1)
                    for n in range(NQ_SIDE, NQ):
                        copy_xT(n)

                @block.vector
                def _(dve):
                    count = [0]

                    def link(ins):
                        count[0] += 1
                        ins.then_inc(chain, 1)
                        dve.wait_ge(chain, count[0])

                    def moments(c):
                        dve.wait_ge(x_in[c], 16)
                        for t in range(c * CH, (c + 1) * CH):
                            ins = nc.vector.bn_stats(stats[:, t, :], base[:, t, :])
                        link(ins)
                        for t in range(c * CH, (c + 1) * CH):
                            ins = nc.vector.bn_aggr(mv[:, t, :], stats[:, t, :])
                        link(ins)
                        s = slice(c * CH, (c + 1) * CH)
                        nc.vector.tensor_scalar(ln[:, 0, s], mv[:, s, 1], EPS, None, ALU.add).then_inc(var_ready, 1)

                    def normalise(c):
                        s = slice(c * CH, (c + 1) * CH)
                        dve.wait_ge(root_ready, c + 1)
                        link(nc.vector.reciprocal(ln[:, 2, s], ln[:, 1, s]))
                        link(nc.vector.tensor_tensor(ln[:, 3, s], ln[:, 2, s], ln[:, 2, s], ALU.mult))
                        link(nc.vector.scalar_tensor_tensor(ln[:, 4, s], ln[:, 3, s], -0.5, ln[:, 0, s], ALU.mult, ALU.mult))
                        link(nc.vector.scalar_tensor_tensor(ln[:, 5, s], ln[:, 4, s], 1.5, ln[:, 2, s], ALU.add, ALU.mult))
                        for t in range(c * CH, (c + 1) * CH):
                            nc.vector.tensor_scalar(xn[:, t, :], base[:, t, :], mv[:, t, 0:1], ln[:, 5, t:t + 1],
                                                    ALU.subtract, ALU.mult).then_inc(xn_ready, 1)

                    for c in range(2):
                        moments(c)
                        normalise(c)
                    dve.wait_ge(wqk_in, 32)
                    nc.vector.tensor_tensor(wsq[:, 0:D], wq_s[:, :], wq_s[:, :], ALU.mult).then_inc(w_squared, 1)
                    nc.vector.tensor_tensor(wsq[:, D:2 * D], wk_s[:, :], wk_s[:, :], ALU.mult).then_inc(w_squared, 1)
                    dve.wait_ge(small_in, SMALL)
                    link(nc.vector.tensor_scalar(ph[:, 0, :], phase_s, 1.0 / TWO_PI, 0.25, ALU.mult, ALU.add))
                    link(nc.vector.tensor_scalar(ph[:, 1, :], ph[:, 0, :], ROUND, None, ALU.add))
                    link(nc.vector.tensor_scalar(ph[:, 0, :], ph[:, 1, :], -ROUND, None, ALU.add))
                    link(nc.vector.scalar_tensor_tensor(ph[:, 1, :], ph[:, 0, :], -C1, phase_s, ALU.mult, ALU.add))
                    link(nc.vector.scalar_tensor_tensor(ph[:, 2, :], ph[:, 0, :], -C2, ph[:, 1, :], ALU.mult, ALU.add))
                    link(nc.vector.scalar_tensor_tensor(ph[:, 3, :], ph[:, 0, :], -C3, ph[:, 2, :], ALU.mult, ALU.add))
                    link(nc.vector.tensor_scalar(ph[:, 0, :], ph[:, 3, :], np.pi / 2, np.pi, ALU.add, ALU.min))
                    nc.vector.tensor_scalar(ph[:, 1, :], ph[:, 0, :], -np.pi, None, ALU.max).then_inc(angle, 1)

                    def rest_of(m):
                        dve.wait_ge(part1, m + 1)
                        if m >= 2:
                            dve.wait_ge(part3, m - 1)
                        nc.vector.scalar_tensor_tensor(rest[m % 2], banks[2 + m % 4][:, :], (bq_s, bk_s)[m % 2][:, :],
                                                       part0[m][:, 0, :], ALU.add, ALU.subtract).then_inc(rest1, 1)

                    def third_part(m):
                        dve.wait_ge(part2, m + 1)
                        nc.vector.tensor_tensor(part0[m][:, 2, :], rest[m % 2], part0[m][:, 1, :], ALU.subtract).then_inc(part3, 1)

                    for m in range(2 * NQ_SIDE):
                        rest_of(m)
                        if m:
                            third_part(m - 1)
                        if m in (2, 4):
                            moments(m // 2 + 1)
                    third_part(2 * NQ_SIDE - 1)
                    normalise(2)
                    normalise(3)
                    for n in range(NQ_SIDE):
                        dve.wait_ge(v_made, n + 1)
                        v_to_tiles(n, banks[3 + n % 2]).then_inc(v_copied, 1)
                    dve.wait_ge(gb_turned, 1)
                    nc.vector.tensor_copy(b1_s[:, :, :].rearrange("p e f -> p (e f)"), banks[5][:, 0:E * FCH]).then_inc(gb_copied, 1)
                    nc.vector.tensor_copy(gw_s[:, :], banks[5][:, E * FCH:E * FCH + E]).then_inc(gb_copied, 1)

                    dve.wait_ge(sine, 1)
                    for side in range(SIDES):
                        c_side = cw[:, side * H * W:(side + 1) * H * W].rearrange("p (h w) -> p w h", w=W)
                        sin_v = ph[:, 2, :].rearrange("p (w h) -> p w h", w=W)
                        nc.vector.scalar_tensor_tensor(c_side, sin_v, SCALE, sin_v, ALU.mult, ALU.mult)
                    link(nc.vector.tensor_scalar(iw_s[:, :], iw_s[:, :], 1.0 / W, None, ALU.mult))
                    dve.wait_ge(norms_ready, 1)
                    link(nc.vector.scalar_tensor_tensor(bound[:, 2 * D:4 * D], brow, -1.0, brow, ALU.mult, ALU.max))
                    link(nc.vector.tensor_tensor(brow, bound[:, 0:2 * D], bound[:, 2 * D:4 * D], ALU.add))
                    link(nc.vector.reduce_max(one[:, 0:2], brow.rearrange("a (k p) -> a k p", p=D), AX.X))
                    link(nc.vector.tensor_tensor(one[:, 2:3], one[:, 0:1], one[:, 1:2], ALU.mult))
                    link(nc.vector.tensor_scalar(one[:, 3:4], one[:, 2:3], SCALE * HD, S_PLAIN, ALU.mult, ALU.is_lt))
                    link(nc.vector.tensor_copy(flag[:, :], one[:, 3:4]))

                @block.tensor
                def _(pe):
                    def turn_x(n):
                        pe.wait_ge(xn_ready, (n + 1) * TB)
                        if n >= 2:
                            pe.wait_ge(xT_copied, n - 1)
                        for i in range(TB):
                            ins = nc.tensor.transpose(banks[n % 2][:, i * P:(i + 1) * P], xn[:, n * TB + i, :], ident[:, :])
                        ins.then_inc(xT_made, 1)

                    pe.wait_ge(const_ready, 4)
                    turn_x(0)
                    pe.wait_ge(wqk_in, 32)
                    for n in range(NQ_SIDE):
                        pe.wait_ge(xT_copied, n + 1)
                        for kind, w in enumerate((wq_s, wk_s)):
                            m = 2 * n + kind
                            if m >= 4:
                                pe.wait_ge(rest1, m - 3)
                            nc.tensor.matmul(banks[2 + m % 4][:, :], w[:, :], xnT[:, n * BANK:(n + 1) * BANK],
                                             start=True, stop=True).then_inc(proj, 1)
                            if kind == 0 and n + 1 < NQ_SIDE:
                                turn_x(n + 1)
                    pe.wait_ge(w_squared, 2)
                    nc.tensor.matmul(banks[6][0:1, 0:2 * D], one_col[:, :], wsq, start=True, stop=True).then_inc(norms_made, 1)
                    pe.wait_ge(w_in, 32)
                    for n in range(NQ_SIDE):
                        if n >= 2:
                            pe.wait_ge(v_copied, n - 1)
                        else:
                            pe.wait_ge(rest1, 2 * NQ_SIDE - 2 + n)
                        for i in range(TB):
                            t = n * TB + i
                            ins = nc.tensor.matmul(banks[3 + n % 2][:, i * D:(i + 1) * D], xnT[:, t * P:(t + 1) * P], wv_s[:, :], start=True, stop=True)
                        ins.then_inc(v_made, 1)
                    pe.wait_ge(small_in, SMALL)
                    pe.wait_ge(rest1, 2 * NQ_SIDE)
                    nc.tensor.transpose(banks[5][:, 0:E * FCH], gb_rows[:, 0, :], ident[0:E * FCH, 0:E * FCH])
                    nc.tensor.transpose(banks[5][:, E * FCH:E * FCH + E], gb_rows[0:E, 1, :], ident[0:E, 0:E]).then_inc(gb_turned, 1)
                    for n in range(NQ_SIDE, NQ):
                        turn_x(n)

        att = ExitStack()
        with att:
            def asem(name):
                return att.enter_context(nc.semaphore(name))

            rows_in = [asem(f"rows_in{i}") for i in range(2)]
            ROWS = PARTS * 16
            sc_made, sc_read = asem("sc_made"), asem("sc_read")
            split, nm_turned, nm_copied = asem("split"), asem("nm_turned"), asem("nm_copied")
            v_staged, exp_done, pv_done, pv_copied, turned, turned_copied = (asem(n) for n in (
                "v_staged", "exp_done", "pv_done", "pv_copied", "turned", "turned_copied"))
            rsum_ready, half_read, summed, pool_step = asem("rsum_ready"), asem("half_read"), asem("summed"), asem("pool_step")
            last_half = asem("last_half")

            x_made, x_read = asem("x_made"), asem("x_read")
            part_step, side_parts, logits_made = asem("part_step"), asem("side_parts"), asem("logits_made")
            logits_bank = bank_b[:, BANK:2 * BANK].bitcast(f32)
            route, gate_in, gate_exp, mask_ready, index_ready = (asem(n) for n in (
                "route", "gate_in", "gate_exp", "mask_ready", "index_ready"))
            scattered, gathered, pool_comb, base_ready = asem("scattered"), [asem(f"gathered{c}") for c in range(CHUNKS)], asem("pool_comb"), asem("base_ready")
            fc_in = [asem(f"fc_in{i}") for i in range(2)]
            fc_out, h_ready, stored0 = asem("fc_out"), asem("h_ready"), asem("stored0")

            QK1 = 2 * NQ_SIDE
            V1 = NQ_SIDE
            EI = 2 + 2 * FCH + CT
            X0 = QK1 + V1 + 2
            XO = X0 + E * EI

            def pe_side1(pe, w):
                if w % 2 == 0:
                    i = w // 2
                    n, kind = NQ_SIDE + i // 2, i % 2
                    if i >= 2:
                        pe.wait_ge(x_read, i - 1)
                    nc.tensor.matmul(x_bank[i % 2][:, :], (wq_s, wk_s)[kind][:, :], xnT[:, n * BANK:(n + 1) * BANK],
                                     start=True, stop=True).then_inc(x_made, 1)
                else:
                    for t in range(w // 2 * TB, (w // 2 + 1) * TB):
                        ins = nc.tensor.matmul(logits_bank[:, t * E:(t + 1) * E], xnT[:, t * P:(t + 1) * P], gw_s[:, :], start=True, stop=True)
                    ins.then_inc(logits_made, 1)

            def dve_side1(dve, w):
                i = w // 2
                m = QK1 + i
                p_, r_ = part[i % 2], rest[i % 2]
                if w % 2 == 0:
                    dve.wait_ge(x_made, i + 1)
                    dve.wait_ge(parts_out[i % 2], 16 * (NQ_SIDE + i // 2))
                    nc.vector.tensor_scalar(p_[:, 0, :], x_bank[i % 2][:, :], (bq_s, bk_s)[i % 2][:, :], None, ALU.add).then_inc(part_step, 1)
                    dve.wait_ge(part_step, 2 * i + 1)
                    nc.vector.scalar_tensor_tensor(r_, x_bank[i % 2][:, :], (bq_s, bk_s)[i % 2][:, :], p_[:, 0, :],
                                                   ALU.add, ALU.subtract).then_inc(x_read, 1)
                else:
                    dve.wait_ge(x_read, i + 1)
                    nc.vector.tensor_copy(p_[:, 1, :], r_).then_inc(part_step, 1)
                    dve.wait_ge(part_step, 2 * i + 2)
                    nc.vector.tensor_tensor(p_[:, 2, :], r_, p_[:, 1, :], ALU.subtract).then_inc(side_parts, 1)

            SIDE1_EARLY = 6

            def sp_side1(sp, i0, i1):
                for i in range(i0, i1):
                    sp.wait_ge(side_parts, i + 1)
                    store_parts(sp, QK1 + i)
                if i1 == QK1:
                    for i in range(2):
                        sp.wait_ge(parts_out[i], 16 * NQ)

            def pe_routing(pe, w):
                if w < V1:
                    i = QK1 + w
                    pe.wait_ge(x_read, i - 1)
                    for q in range(TB):
                        t = (NQ_SIDE + w) * TB + q
                        ins = nc.tensor.matmul(x_bank[i % 2][:, q * D:(q + 1) * D], xnT[:, t * P:(t + 1) * P], wv_s[:, :], start=True, stop=True)
                    ins.then_inc(x_made, 1)
                if w == 6:
                    pe.wait_ge(mask_ready, 1)
                    pe.wait_ge(x_read, QK1 + V1)
                    for i, before in enumerate((below_b, ones_b)):
                        nc.tensor.matmul(x_bank[i][:, 0:TILES * E], before[:, :], maskb[:, :], start=True, stop=True).then_inc(x_made, 1)

            def dve_routing(dve, w):
                te = [P, TILES, E]
                g = [lg[:, a, :].rearrange("p (t e) -> p t e", e=E) for a in range(6)]
                n = [ROUTED[w]]

                def link(ins):
                    n[0] += 1
                    ins.then_inc(route, 1)
                    dve.wait_ge(route, n[0])

                if w < V1:
                    dve.wait_ge(x_made, QK1 + w + 1)
                    v_to_tiles(NQ_SIDE + w, x_bank[(QK1 + w) % 2]).then_inc(x_read, 1)
                if w == 4:
                    dve.wait_ge(logits_made, NQ)
                    link(nc.vector.tensor_copy(lg[:, 5, :], logits_bank))
                    link(nc.vector.reduce_max(r[:, 0, :], g[5], AX.X))
                    nc.vector.tensor_tensor(g[0], g[5], over(r[:, 0, :], E), ALU.subtract).then_inc(gate_in, 1)
                    dve.wait_ge(gate_in, 1)
                    link(nc.vector.scalar_tensor_tensor(g[2], g[0], 0.0, order8[:, :].unsqueeze(1).to_broadcast(te), ALU.is_ge, ALU.mult))
                if w == 5:
                    link(nc.vector.reduce_max(r[:, 1, :], g[2], AX.X))
                    link(nc.vector.tensor_tensor(g[3], g[2], over(r[:, 1, :], E), ALU.is_equal))
                    nc.vector.tensor_copy(maskb[:, :], lg[:, 3, :]).then_inc(mask_ready, 1)
                if w == 6:
                    dve.wait_ge(x_made, QK1 + V1 + 2)
                    dve.wait_ge(gate_exp, 1)
                    link(nc.vector.tensor_copy(lg[:, 2, :], x_bank[0][:, 0:TILES * E]))
                    link(nc.vector.memset(lg[:, 0, 0:E], 0.0))
                    nc.vector.tensor_copy(lg[:, 0, E:TILES * E], x_bank[1][:, 0:(TILES - 1) * E]).then_inc(x_read, 2)
                    dve.wait_ge(x_read, QK1 + V1 + 2)
                if 7 <= w < 12:
                    shift = 1 << (w - 7)
                    a, b = (0, 4) if w % 2 else (4, 0)
                    link(nc.vector.tensor_copy(lg[:, b, 0:shift * E], lg[:, a, 0:shift * E]))
                    link(nc.vector.tensor_tensor(lg[:, b, shift * E:], lg[:, a, shift * E:], lg[:, a, 0:(TILES - shift) * E], ALU.add))
                if w == 12:
                    link(nc.vector.tensor_tensor(g[5], g[2], g[4], ALU.add))
                    link(nc.vector.tensor_tensor(g[2], g[5], g[3], ALU.mult))
                    link(nc.vector.reduce_sum(r[:, 4, :], g[2], AX.X))
                if w == 13:
                    link(nc.vector.tensor_tensor(g[5], g[3], ebase[:, :].unsqueeze(1).to_broadcast(te), ALU.mult))
                    link(nc.vector.reduce_sum(r[:, 5, :], g[5], AX.X))
                    link(nc.vector.reduce_sum(r[:, 2, :], g[1], AX.X))
                    link(nc.vector.reciprocal(r[:, 3, :], r[:, 2, :]))
                if w == 14:
                    link(nc.vector.tensor_scalar(r[:, 6, :], r[:, 4, :], float(CAP), None, ALU.is_lt))
                    link(nc.vector.tensor_tensor(r[:, 7, :], r[:, 4, :], r[:, 5, :], ALU.add))
                    link(nc.vector.tensor_tensor(r[:, 8, :], r[:, 7, :], token_row[:, :], ALU.subtract))
                    link(nc.vector.tensor_tensor(r[:, 9, :], r[:, 8, :], r[:, 6, :], ALU.mult))
                    link(nc.vector.tensor_tensor(r[:, 8, :], r[:, 9, :], token_row[:, :], ALU.add))
                if w == 15:
                    nc.vector.tensor_copy(idx_scatter[:, :], r[:, 8, :]).then_inc(index_ready, 1)
                    link(nc.vector.tensor_tensor(r[:, 9, :], r[:, 7, :], r[:, 6, :], ALU.mult))
                    nc.vector.tensor_copy(idx_gather[:, :], r[:, 9, :]).then_inc(index_ready, 1)
                    nc.vector.tensor_tensor(r[:, 0, :], r[:, 3, :], r[:, 6, :], ALU.mult).then_inc(index_ready, 1)

            links = {4: 3, 5: 2, 6: 2, 7: 2, 8: 2, 9: 2, 10: 2, 11: 2, 12: 3, 13: 4, 14: 5, 15: 1}
            ROUTED = [sum(links.get(v, 0) for v in range(w)) for w in range(W)]

            def act_gate(act):
                act.wait_ge(gate_in, 1)
                nc.scalar.activation(lg[:, 1, :], lg[:, 0, :], ACT.Exp).then_inc(gate_exp, 1)

            def pool_scatter(pool, c):
                if c == 0:
                    pool.wait_ge(index_ready, 3)
                for t in range(c * CH, (c + 1) * CH):
                    pool.indirect_dma_start(out=slots_dram, out_offset=bass.IndirectOffsetOnAxis(
                        ap=idx_scatter[:, t:t + 1], axis=0), in_=xn[:, t, :], in_offset=None).then_inc(scattered, 16)

            def sp_expert_in(sp, e, par):
                sp.dma_start(e_x[par], slots_dram[ds(e * CAP, CAP), :].rearrange("(t p) d -> p t d", p=P)).then_inc(fc_in[par], 16)
                w1_rows = w1.rearrange("e d f -> (e d) f")
                w2_rows = w2.rearrange("e f d -> (e f) d")
                sp.dma_start(e_w1[par], w1_rows[ds(e * D, D), :]).then_inc(fc_in[par], 16)
                sp.dma_start(e_w2[par], w2_rows[ds(e * DFF, DFF), :].rearrange("(f p) d -> p f d", p=P)).then_inc(fc_in[par], 16)
                sp.dma_start(e_b2[par][:, :], b2.rearrange("e d -> (e d)")[ds(e * D, D)].partition_broadcast(P)).then_inc(fc_in[par], 16)

            def sp_expert_out(sp, e):
                sp.wait_ge(x_read, (e + 1) * EI + X0)
                sp.dma_start(expert_dram[ds(e * CAP, CAP), :].rearrange("(t p) d -> p t d", p=P), e_o).then_inc(fc_out, 16)

            def pe_expert(pe, e, pair_e, par, w):
                if w >= EI:
                    return
                bank = x_bank[w % 2]
                if w == 0:
                    pe.wait_ge(fc_in[par], (pair_e + 1) * 64)
                pe.wait_ge(x_read, e * EI + (X0 + w - 1 if w else X0))
                if w < 2:
                    for t in range(w * TB, min(CT, (w + 1) * TB)):
                        ins = nc.tensor.transpose(bank[:, (t % TB) * P:(t % TB + 1) * P], e_x[par][:, t, :], ident[:, :])
                elif w < 2 + 2 * FCH:
                    f, half = (w - 2) // 2, (w - 2) % 2
                    if w == 2:
                        pe.wait_ge(x_read, e * EI + (X0 + 2))
                    ins = nc.tensor.matmul(bank[:, 0:HC], e_w1[par][:, f * P:(f + 1) * P], e_xT[:, half * HC:(half + 1) * HC],
                                           start=True, stop=True)
                else:
                    t = w - 2 - 2 * FCH
                    if t == 0:
                        pe.wait_ge(x_read, e * EI + (X0 + 2 + 2 * FCH))
                    for f in range(FCH):
                        ins = nc.tensor.matmul(bank[:, 0:D], e_h[:, f, t * P:(t + 1) * P], e_w2[par][:, f, :], start=f == 0, stop=f == FCH - 1)
                ins.then_inc(x_made, 1)

            def dve_expert(dve, e, par, w):
                if w >= EI:
                    return
                bank = x_bank[w % 2]
                dve.wait_ge(x_made, e * EI + (X0 + w + 1))
                if w < 2:
                    t0, t1 = w * TB, min(CT, (w + 1) * TB)
                    ins = nc.vector.tensor_copy(e_xT[:, t0 * P:t1 * P], bank[:, 0:(t1 - t0) * P])
                elif w < 2 + 2 * FCH:
                    f, half = (w - 2) // 2, (w - 2) % 2
                    ins = nc.vector.tensor_scalar(e_h[:, f, half * HC:(half + 1) * HC], bank[:, 0:HC],
                                                  b1_s[:, :, :].rearrange("p e f -> p (e f)")[:, ds(e * FCH + f, 1)], 0.0, ALU.add, ALU.max)
                else:
                    t = w - 2 - 2 * FCH
                    if t == 0:
                        dve.wait_ge(fc_out, e * 16 + 16)
                    ins = nc.vector.tensor_tensor(e_o[:, t, :], bank[:, 0:D], e_b2[par][:, :], ALU.add)
                ins.then_inc(x_read, 1)

            def pool_combine(pool, c):
                if c == 0:
                    pool.wait_ge(fc_out, 16 * (E + 1))
                s = slice(c * CH, (c + 1) * CH)
                got = region[:, :].rearrange("p (t d) -> p t d", d=D)
                for t in range(c * CH, (c + 1) * CH):
                    pool.indirect_dma_start(out=got[:, t, :], out_offset=None, in_=expert_dram,
                                            in_offset=bass.IndirectOffsetOnAxis(ap=idx_gather[:, t:t + 1], axis=0)).then_inc(gathered[c], 16)
                nc.gpsimd.tensor_tensor(base[:, s, :], base[:, s, :], bo_s[:, :].unsqueeze(1).to_broadcast([P, CH, D]),
                                        ALU.add).then_inc(pool_comb, 1)
                pool.wait_ge(gathered[c], 16 * CH)
                nc.gpsimd.tensor_tensor(got[:, s, :], got[:, s, :], over(r[:, 0, s], D), ALU.mult).then_inc(pool_comb, 1)
                pool.wait_ge(pool_comb, 2 * (c + 1))
                nc.gpsimd.tensor_tensor(base[:, s, :], base[:, s, :], got[:, s, :], ALU.add).then_inc(base_ready, 1)

            hv = heads[:, :].rearrange("p (t f) -> p t f", f=D)
            hT0 = region[:, 0:BANK]
            OUT_STEPS = W // 2

            def pe_output(pe, n, w):
                i = XO + 2 * n
                if w == 0:
                    pe.wait_ge(x_read, i)
                    for q in range(TB):
                        ins = nc.tensor.transpose(x_bank[0][:, q * P:(q + 1) * P], hv[:, n * TB + q, :], ident[:, :])
                    ins.then_inc(x_made, 1)
                if w == 2:
                    pe.wait_ge(x_read, i + 1)
                    for q in range(TB):
                        ins = nc.tensor.matmul(x_bank[1][:, q * D:(q + 1) * D], hT0[:, q * P:(q + 1) * P], wo_s[:, :], start=True, stop=True)
                    ins.then_inc(x_made, 1)

            def dve_output(dve, n, w):
                i = XO + 2 * n
                if w == 0:
                    dve.wait_ge(x_made, i + 1)
                    dve.wait_ge(base_ready, CHUNKS)
                    nc.vector.tensor_copy(hT0, x_bank[0][:, :]).then_inc(x_read, 1)
                if w == 2:
                    dve.wait_ge(x_made, i + 2)
                    b = base[:, n * TB:(n + 1) * TB, :]
                    nc.vector.tensor_tensor(b, b, x_bank[1][:, :].rearrange("p (t d) -> p t d", d=D), ALU.add).then_inc(x_read, 1)

            ov = out.rearrange("b (t p) d -> p (b t) d", p=P)

            def sp_output(sp):
                for n in range(NQ_SIDE):
                    sp.wait_ge(x_read, XO + 2 * n + 2)
                    sp.dma_start(ov[:, n * TB:(n + 1) * TB, :], base[:, n * TB:(n + 1) * TB, :]).then_inc(stored0, 16)
                sp.wait_ge(stored0, 16 * NQ_SIDE)

            def load_rows(sp, u, par):
                sp.wait_ge(nm_copied, u + 2)
                for i in range(PARTS):
                    sp.dma_start(Qs[par][MAXROW + i:MAXROW + i + 1, :].rearrange("a (t c) -> a t c", c=P),
                                 nm_rows[i * SIDE_TILES:(i + 1) * SIDE_TILES, :]).then_inc(rows_in[par], 16)

            BEFORE = 3 * SIDE_B
            EARLY = SIDE_B // 2
            T0_NO = SIDE_B + EARLY

            def pair_no(u, kind, two_ahead=True):
                return BEFORE + 2 * SIDE_B * u + (SIDE_B if kind and two_ahead else 0)

            def pe_scores(pe, no, par, p, rr):
                pe.wait_ge(sc_read, no + p + 1)
                for qt in range(QT):
                    ins = nc.tensor.matmul(sc_bank[rr][:, qt * SEQ:(qt + 1) * SEQ], Qs[par][0:PROD, ds(p * SEQ + qt * P, P)],
                                           Ks[par][0:PROD, ds(p * SEQ, SEQ)], start=True, stop=True)
                ins.then_inc(sc_made, 1)

            def dve_scores(dve, no, par, p, rr):
                dve.wait_ge(sc_made, no + p + 1)
                nc.vector.reduce_max(negmax[par][:, ds(p * QT, QT)], sc_bank[rr][:, :].rearrange("p (t k) -> p t k", k=SEQ),
                                     AX.X, negate=True).then_inc(sc_read, 1)

            def pe_transposed(pe, no, par, p, rr):
                pe.wait_ge(sc_read, no + p + 1)
                for kt in range(QT):
                    ins = nc.tensor.matmul(sc_bank[rr][:, kt * SEQ:(kt + 1) * SEQ], Ks[par][0:STACK, ds(p * SEQ + kt * P, P)],
                                           Qs[par][0:STACK, ds(p * SEQ, SEQ)], start=True, stop=True)
                ins.then_inc(sc_made, 1)

            def dve_transposed(dve, no, par, p, rr):
                dve.wait_ge(sc_made, no + p + 1)
                nc.vector.tensor_copy(T[par][:, ds(p * BANK, BANK)], sc_bank[rr][:, :]).then_inc(sc_read, 1)

            def dve_split(dve, no, u, par):
                n = SIDE_TILES
                dve.wait_ge(sc_read, no + SIDE_B + 2)
                dve.wait_ge(nm_turned, u + 1)
                nc.vector.tensor_copy(nm_parts[:, 0:n], negmax[par][:, :]).then_inc(split, 1)
                dve.wait_ge(split, 4 * u + 1)
                nc.vector.tensor_tensor(nm_rest[:, :], negmax[par][:, :], nm_parts[:, 0:n], ALU.subtract).then_inc(split, 1)
                dve.wait_ge(split, 4 * u + 2)
                nc.vector.tensor_copy(nm_parts[:, n:2 * n], nm_rest[:, :]).then_inc(split, 1)
                dve.wait_ge(split, 4 * u + 3)
                nc.vector.tensor_tensor(nm_parts[:, 2 * n:3 * n], nm_rest[:, :], nm_parts[:, n:2 * n], ALU.subtract).then_inc(split, 1)

            def pe_turn_max(pe, u):
                pe.wait_ge(split, 4 * u + 4)
                pe.wait_ge(nm_copied, u + 1)
                nc.tensor.transpose(bank_b[:, 0:P], nm_parts[:, :], identb[:, :]).then_inc(nm_turned, 1)

            def dve_turn_max(dve, pair, par):
                u = 2 * pair + par
                if not (isinstance(pair, int) and u == 0):
                    dve.wait_ge(rows_in[1 - par], ROWS * (pair + par))
                dve.wait_ge(nm_turned, u + 2)
                nc.vector.tensor_copy(nm_rows[:, :], bank_b[0:PARTS * SIDE_TILES, 0:P]).then_inc(nm_copied, 1)

            def pe_products(pe, u, par, g, rr):
                pe.wait_ge(v_staged, u + 1)
                pe.wait_ge(exp_done, g + 1)
                pe.wait_ge(pv_copied, g + 1)
                for half in range(2):
                    for kt in range(QT):
                        for j in range(GR):
                            blk = (2 * j + half) * QT + kt
                            ins = nc.tensor.matmul(pv_bank[rr][VC * j:VC * (j + 1), half * SEQ:(half + 1) * SEQ], Vst[par][:, blk, :],
                                                   Pr[rr][:, blk * SEQ:(blk + 1) * SEQ], start=kt == 0, stop=kt == QT - 1)
                ins.then_inc(pv_done, 1)

            def dve_products(dve, g, rr):
                dve.wait_ge(pv_done, g + 1 + 2)
                dve.wait_ge(turned, g + 1)
                nc.vector.tensor_copy(pv_s[rr][:, :], pv_bank[rr][:, :]).then_inc(pv_copied, 1)

            def pe_turn(pe, g, rr):
                pe.wait_ge(pv_copied, g + 1 + 2)
                pe.wait_ge(turned_copied, g + 1)
                for q in range(BANK // P):
                    ins = nc.tensor.transpose(tr_bank[:, q * P:(q + 1) * P], pv_s[rr][:, q * P:(q + 1) * P], ident[:, :])
                ins.then_inc(turned, 1)

            def dve_turned(dve, u, g, half, w):
                dve.wait_ge(half_read, 2 * u + half + 1)
                dve.wait_ge(turned, g + 1 + 2)
                dst = OT[half][:, ds(w * OTW * OC, OTW * OC)].rearrange("p (a c) -> p a c", c=OC)
                nc.vector.tensor_copy(dst, tr_bank[:, :].rearrange("p (a c) -> p a c", c=VC)[:, :, 0:OC]).then_inc(turned_copied, 1)

            def dve_row_sums(dve, u, half):
                dve.wait_ge(turned_copied, W * u + WH * (half + 1) + 1)
                row_sums = OT[half][:, :].rearrange("p (a c) -> p a c", c=OC)[:, :, HD:OC]
                nc.vector.reciprocal(rsum[half][:, :].rearrange("p (a b) -> p a b", b=1), row_sums).then_inc(rsum_ready, 1)

            def act_step(act, g, par, rr):
                act.wait_ge(pv_done, g + 1)
                nc.scalar.activation(Pr[rr][:, :], T[par][:, :], ACT.Exp, scale=cw[:, ds(g, 1)]).then_inc(exp_done, 1)

            def sum_half(eng, ops, step, first, u, half):
                a = WH * OTW
                eng.wait_ge(rsum_ready, 2 * u + half + 1)
                ops.tensor_tensor(gain[:, :].rearrange("p (w a) -> p w a", a=OTW), rsum[half][:, :].rearrange("p (w a) -> p w a", a=OTW),
                                  over(iw_s[:, half * WH:(half + 1) * WH], OTW), ALU.mult).then_inc(step, 1)
                eng.wait_ge(step, first + 1)
                o = OT[half][:, :].rearrange("p (a c) -> p a c", c=OC)[:, :, 0:HD]
                ops.tensor_tensor(terms[:, 0:WH, :].rearrange("p w (a d) -> p (w a) d", d=HD), o, over(gain[:, :], HD),
                                  ALU.mult).then_inc(half_read, 1)
                eng.wait_ge(half_read, 2 * u + half + 3)
                n, k = WH // 2, 1
                while n > 1:
                    ops.tensor_tensor(terms[:, 0:n, :], terms[:, 0:n, :], terms[:, n:2 * n, :], ALU.add).then_inc(step, 1)
                    n, k = n // 2, k + 1
                    eng.wait_ge(step, first + k)
                if half == 0:
                    ops.tensor_tensor(terms[:, WH, :], terms[:, 0, :], terms[:, 1, :], ALU.add).then_inc(step, 1)
                    return k + 1
                ops.tensor_tensor(terms[:, 0, :], terms[:, 0, :], terms[:, 1, :], ALU.add).then_inc(step, 1)
                eng.wait_ge(step, first + k + 1)
                at = u * HD + (u // H) * (SIDE_TILES - 1) * D
                dst = heads[:, ds(at, (SIDE_TILES - 1) * D + HD)]
                dst = bass.AP(dst.tensor, dst.offset, [dst.ap[0], [D, BANK // P], [GR * D, GR], [1, HD]])
                x_, y_ = (terms[:, i, :].rearrange("p (q j d) -> p q j d", j=GR, d=HD) for i in (0, WH))
                ops.tensor_tensor(dst, x_, y_, ALU.add).then_inc(summed, 1)
                return k + 1

            HALF_STEPS = WH.bit_length()

            def stage_v(pool, u, par):
                nc.gpsimd.tensor_copy(Vst[par][:, :, 0:HD], Vall[:, ds(u * SIDE_TILES * HD, SIDE_TILES * HD)]
                                      .rearrange("p (t d) -> p t d", d=HD)).then_inc(v_staged, 1)

            A, B, C = range(3)
            PHASES = ((A, 0, W // 4), (B, W // 4, 3 * W // 4), (C, 3 * W // 4, W))
            A_PAIRS = SIDE_B // (W // 4)
            LAST = UNITS // 2 - 1
            EPAIR = 2

            def run_steps(eng, step, after, beside):
                for phase, w0, w1_ in PHASES:
                    if beside is not None:
                        for w in range(w0, w1_):
                            step(phase, w, w % 2)
                            if w == WH - 1:
                                after(None)
                    elif phase == B:
                        for v0, v1 in ((w0, WH), (WH, w1_)):
                            with eng.Fori(0, (v1 - v0) // 2) as k:
                                for rr in range(2):
                                    step(phase, v0 + 2 * k + rr, rr)
                            if v1 == WH:
                                after(None)
                    else:
                        with eng.Fori(0, (w1_ - w0) // 2) as k:
                            for rr in range(2):
                                step(phase, w0 + 2 * k + rr, rr)
                    after(phase)

            FIRST, PLAIN, EXPERT, FINAL = range(4)

            def units(eng, unit):
                for par in range(2):
                    unit(0, par, FIRST)
                for par in range(2):
                    unit(1, par, PLAIN)
                with eng.Fori(EPAIR, EPAIR + E // 2) as pair:
                    for par in range(2):
                        unit(pair, par, EXPERT)
                with eng.Fori(EPAIR + E // 2, LAST) as pair:
                    for par in range(2):
                        unit(pair, par, PLAIN)
                for par in range(2):
                    unit(LAST, par, FINAL)

            def plain_tensor(pe):
                pe.sem_inc(pv_done, 2)
                pe.sem_inc(turned, 2)
                pe.sem_inc(nm_turned, 1)
                for u in range(2):
                    pe.wait_ge(stack_in[u], 2 * LOADS)
                    for p in range(SIDE_B):
                        if u == 1 and p == EARLY:
                            pe.wait_ge(rows_in[0], ROWS)
                            for q in range(SIDE_B):
                                pe_transposed(pe, T0_NO, 0, q, q % 2)
                        pe_scores(pe, 2 * SIDE_B if u and p >= EARLY else SIDE_B * u, u, p, p % 2)
                    pe_turn_max(pe, u)

                def unit(pair, par, kind):
                    u = 2 * pair + par
                    two, one = kind != FINAL, kind != FINAL or par == 0

                    def step(phase, w, rr):
                        g = u * W + w
                        pe_products(pe, u, par, g, rr)
                        if phase == A and two:
                            pe.wait_ge(stack_in[par], LOADS * (pair + 3))
                            for c in range(A_PAIRS):
                                pe_scores(pe, pair_no(u, 0), par, w * A_PAIRS + c, c % 2)
                        if phase == B and one:
                            pe.wait_ge(rows_in[1 - par], ROWS * (pair + 1 + par))
                            pe_transposed(pe, pair_no(u, 1, two), 1 - par, w - W // 4, rr)
                        if kind == FIRST:
                            (pe_side1, pe_routing)[par](pe, w)
                        elif kind == EXPERT:
                            pe_expert(pe, u - 2 * EPAIR, pair - EPAIR, par, w)
                        elif kind == FINAL:
                            pe_output(pe, 2 * par + w // OUT_STEPS, w % OUT_STEPS)
                        pe_turn(pe, g, rr)

                    def after(phase):
                        if phase == B and two:
                            pe_turn_max(pe, u + 2)

                    run_steps(pe, step, after, None if kind == PLAIN else kind)
                units(pe, unit)

            def plain_vector(dve):
                dve.sem_inc(sc_read, 2)
                dve.sem_inc(pv_copied, 2)
                dve.sem_inc(turned_copied, 1)
                dve.sem_inc(nm_copied, 1)
                for u in range(2):
                    for p in range(SIDE_B):
                        if u == 1 and p == EARLY:
                            for q in range(SIDE_B):
                                dve_transposed(dve, T0_NO, 0, q, q % 2)
                        dve_scores(dve, 2 * SIDE_B if u and p >= EARLY else SIDE_B * u, u, p, p % 2)
                    dve_split(dve, 2 * SIDE_B * u, u, u)
                    dve_turn_max(dve, 0, u)

                def unit(pair, par, kind):
                    u = 2 * pair + par
                    two, one = kind != FINAL, kind != FINAL or par == 0

                    def step(phase, w, rr):
                        g = u * W + w
                        dve_products(dve, g, rr)
                        if phase == A and two:
                            for c in range(A_PAIRS):
                                dve_scores(dve, pair_no(u, 0), par, w * A_PAIRS + c, c % 2)
                        if phase == B and one:
                            dve.wait_ge(exp_done, W * u + 1)
                            dve_transposed(dve, pair_no(u, 1, two), 1 - par, w - W // 4, rr)
                        if kind == FIRST:
                            (dve_side1, dve_routing)[par](dve, w)
                        elif kind == EXPERT:
                            dve_expert(dve, u - 2 * EPAIR, par, w)
                        elif kind == FINAL:
                            dve_output(dve, 2 * par + w // OUT_STEPS, w % OUT_STEPS)
                        half = halves[0]
                        dve_turned(dve, u, g, half, w - half * WH)

                    halves = [0]

                    def after(phase):
                        if phase == A and two:
                            dve_split(dve, pair_no(u, 0), u + 2, par)
                        if phase is None:
                            dve_row_sums(dve, u, 0)
                            halves[0] = 1
                        if phase == B and two:
                            dve_turn_max(dve, pair + 1, par)
                        if phase == C:
                            dve_row_sums(dve, u, 1)

                    run_steps(dve, step, after, None if kind == PLAIN else kind)
                units(dve, unit)
                dve.wait_ge(pool_step, HALF_STEPS * (2 * UNITS - 1))
                sum_half(dve, nc.vector, last_half, 0, UNITS - 1, 1)
                dve.wait_ge(summed, UNITS)

            def plain_scalar(act):
                def unit(pair, par, kind):
                    u = 2 * pair + par
                    if kind == FIRST and par == 0:
                        act.wait_ge(sc_read, T0_NO + SIDE_B + 2)
                    elif kind == FINAL and par == 1:
                        act.wait_ge(sc_read, pair_no(u, 0) - SIDE_B + 2)
                    for half in range(2):
                        with act.Fori(0, WH // 2) as k:
                            for rr in range(2):
                                if not (kind == FIRST and par == 0) and not (kind == FINAL and par == 1):
                                    act.wait_ge(sc_read, pair_no(u, 0) + 2)
                                act_step(act, u * W + half * WH + 2 * k + rr, par, rr)
                        if kind == FIRST and par == 1 and half == 0:
                            act_gate(act)
                units(act, unit)

            def plain_gpsimd(pool):
                pool.sem_inc(half_read, 2)
                pool.sem_inc(fc_out, 16)
                for u in range(2):
                    stage_v(pool, u, u)

                def unit(u, par, last=False):
                    for half in range(1 if last else 2):
                        sum_half(pool, nc.gpsimd, pool_step, HALF_STEPS * (2 * u + half), u, half)
                        c = 2 * u + half - 3
                        if isinstance(u, int) and 0 <= c < CHUNKS:
                            pool_scatter(pool, c)
                        if isinstance(u, int) and CU <= u < CU + 2:
                            pool_combine(pool, 2 * (u - CU) + half)

                CU = 2 * EPAIR + E + 1
                for u in range(H):
                    unit(u, u % 2)
                    stage_next(pool, u)
                with pool.Fori(H // 2, LAST) as pair:
                    for par in range(2):
                        unit(2 * pair + par, par)
                        stage_v(pool, 2 * pair + par + 2, par)
                unit(UNITS - 2, 0)
                unit(UNITS - 1, 1, last=True)

            def stage_next(pool, u):
                if u == H - 2:
                    pool.wait_ge(x_read, QK1 + V1)
                stage_v(pool, u + 2, u % 2)

            def plain_sync(sp):
                for u in range(2):
                    load_rows(sp, u, u)

                def unit(u, par, e=None, next_expert=False):
                    sp.wait_ge(sc_made, pair_no(u, 0))
                    load_stack(sp, u + 2, par)
                    if e is not None:
                        sp_expert_out(sp, e)
                    if next_expert:
                        sp_expert_in(sp, e + 2, 1 - par)
                    load_rows(sp, u + 2, par)

                sp.wait_ge(sc_made, T0_NO + SIDE_B)
                load_stack(sp, 2, 0)
                sp_side1(sp, 0, SIDE1_EARLY)
                load_rows(sp, 2, 0)
                sp.wait_ge(sc_made, pair_no(1, 0))
                load_stack(sp, 3, 1)
                sp_side1(sp, SIDE1_EARLY, QK1)
                load_rows(sp, 3, 1)
                unit(2, 0)
                unit(3, 1)
                sp.wait_ge(scattered, 16 * TILES)
                for e in range(2):
                    sp_expert_in(sp, e, e)
                EU = 2 * EPAIR
                unit(EU, 0)
                with sp.Fori(0, E // 2 - 1) as pair:
                    for k in range(2):
                        unit(EU + 1 + 2 * pair + k, 1 - k, 2 * pair + k, next_expert=True)
                for k in range(2):
                    unit(EU + E - 1 + k, 1 - k, E - 2 + k)
                unit(EU + E + 1, 1)
                with sp.Fori(EPAIR + E // 2 + 1, LAST) as pair:
                    for par in range(2):
                        unit(2 * pair + par, par)
                sp_output(sp)
                for i in range(2):
                    sp.wait_ge(rows_in[i], ROWS * UNITS // 2)
                    sp.wait_ge(stack_in[i], LOADS * (UNITS // 2 + 1))

            Qg, Kg = Qs[0][0:PROD, 0:SEQ], Ks[0][0:PROD, 0:SEQ]
            g_raw, g_s, g_n, g_a, g_b, g_cos, g_y, g_p = (T[0][:, i * SEQ:(i + 1) * SEQ] for i in range(8))
            g_acc = T[0][:, 8 * SEQ:9 * SEQ]
            g_accT = T[0][:, 9 * SEQ:10 * SEQ]
            g_col = sb("g_col", [P, 4])
            g_in, g_start, g_scores, g_angle, g_sine, g_exp, g_sum, g_chain, g_turned, g_copied, g_out, g_done = (asem(n) for n in (
                "g_in", "g_start", "g_scores", "g_angle", "g_sine", "g_exp", "g_sum", "g_chain", "g_turned", "g_copied",
                "g_out", "g_done"))
            CHAIN = 13

            def general_tiles(eng, tile):
                with eng.Fori(0, UNITS) as u:
                    with eng.Fori(0, SIDE_B) as b:
                        tile(u, b, (u * SIDE_B + b) * QT)

            def general_sync(sp):
                def tile(u, b, n):
                    sp.wait_ge(g_scores, n + QT)
                    load_stack(sp, u, 0, b * SEQ, SEQ, g_in)
                for i in range(2):
                    sp.wait_ge(stack_in[i], 2 * LOADS)
                general_tiles(sp, tile)
                sp.wait_ge(g_in, LOADS * UNITS * SIDE_B)

            def general_tensor(pe):
                pe.sem_inc(g_scores, QT)

                def tile(u, b, n0):
                    for qt in range(QT):
                        n = n0 + qt
                        if qt == 0:
                            pe.wait_ge(g_in, (u * SIDE_B + b + 1) * LOADS)
                        pe.wait_ge(g_done, n + 1)
                        nc.tensor.matmul(banks[0][:, 0:SEQ], Qg[:, qt * P:(qt + 1) * P], Kg, start=True, stop=True).then_inc(g_scores, 1)
                        pe.wait_ge(g_sum, W * (n + 1))
                        for kt in range(QT):
                            ins = nc.tensor.transpose(banks[1][:, kt * P:(kt + 1) * P], g_acc[:, kt * P:(kt + 1) * P], ident[:, :])
                        ins.then_inc(g_turned, 1)
                        pe.wait_ge(g_copied, n + 1)
                        for kt in range(QT):
                            ins = nc.tensor.matmul(banks[2][:, 0:HD], g_accT[:, kt * P:(kt + 1) * P],
                                                   Vall[:, ds(u * SIDE_TILES * HD + (b * QT + kt) * HD, HD)], start=kt == 0, stop=kt == QT - 1)
                        ins.then_inc(g_out, 1)
                general_tiles(pe, tile)

            def general_scalar(act):
                def tile(u, b, n0):
                    for qt in range(QT):
                        with act.Fori(0, W) as w:
                            m = (n0 + qt) * W + w
                            act.wait_ge(g_angle, m + 1)
                            nc.scalar.activation(g_cos, g_b, ACT.Sin).then_inc(g_sine, 1)
                            act.wait_ge(g_chain, CHAIN * m + 11)
                            nc.scalar.activation(g_p, g_y, ACT.Exp, bias=g_col[:, 0:1], accum_out=g_col[:, 1:2]).then_inc(g_exp, 1)
                general_tiles(act, tile)

            def general_vector(dve):
                dve.sem_inc(g_done, 1)

                def tile(u, b, n0):
                    for qt in range(QT):
                        n = n0 + qt
                        dve.wait_ge(g_scores, n + 1 + QT)
                        nc.vector.tensor_copy(g_raw, banks[0][:, 0:SEQ]).then_inc(g_start, 1)
                        nc.vector.memset(g_acc, 0.0).then_inc(g_start, 1)
                        with dve.Fori(0, W) as w:
                            m = n * W + w

                            def link(k, ins):
                                ins.then_inc(g_chain, 1)
                                dve.wait_ge(g_chain, CHAIN * m + k)

                            dve.wait_ge(g_start, 2 * (n + 1))
                            link(1, nc.vector.tensor_scalar(g_s, g_raw, cw[:, ds(u * W + w, 1)], None, ALU.mult))
                            link(2, nc.vector.scalar_tensor_tensor(g_a, g_s, KERR, g_s, ALU.mult, ALU.mult))
                            link(3, nc.vector.tensor_scalar(g_n, g_a, 1.0 / TWO_PI, 0.25, ALU.mult, ALU.add))
                            link(4, nc.vector.tensor_scalar(g_b, g_n, ROUND, None, ALU.add))
                            link(5, nc.vector.tensor_scalar(g_n, g_b, -ROUND, None, ALU.add))
                            link(6, nc.vector.scalar_tensor_tensor(g_b, g_n, -C1, g_a, ALU.mult, ALU.add))
                            link(7, nc.vector.scalar_tensor_tensor(g_a, g_n, -C2, g_b, ALU.mult, ALU.add))
                            link(8, nc.vector.scalar_tensor_tensor(g_b, g_n, -C3, g_a, ALU.mult, ALU.add))
                            link(9, nc.vector.tensor_scalar(g_a, g_b, np.pi / 2, np.pi, ALU.add, ALU.min))
                            nc.vector.tensor_scalar(g_b, g_a, -np.pi, None, ALU.max).then_inc(g_angle, 1)
                            dve.wait_ge(g_sine, m + 1)
                            link(10, nc.vector.tensor_tensor(g_y, g_s, g_cos, ALU.mult))
                            link(11, nc.vector.reduce_max(g_col[:, 0:1], g_y, AX.X, negate=True))
                            dve.wait_ge(g_exp, m + 1)
                            link(12, nc.vector.reciprocal(g_col[:, 2:3], g_col[:, 1:2]))
                            link(13, nc.vector.tensor_tensor(g_col[:, 3:4], g_col[:, 2:3], iw_s[:, ds(w, 1)], ALU.mult))
                            nc.vector.scalar_tensor_tensor(g_acc, g_p, g_col[:, 3:4], g_acc, ALU.mult, ALU.add).then_inc(g_sum, 1)
                            dve.wait_ge(g_sum, m + 1)
                        dve.wait_ge(g_turned, n + 1)
                        nc.vector.tensor_copy(g_accT, banks[1][:, 0:SEQ]).then_inc(g_copied, 1)
                        dve.wait_ge(g_out, n + 1)
                        first = u * HD + (u // H) * (SIDE_TILES - 1) * D + (b * QT + qt) * D
                        nc.vector.tensor_copy(heads[:, ds(first, HD)], banks[2][:, 0:HD]).then_inc(g_done, 1)
                general_tiles(dve, tile)

            def general_experts(eng, expert):
                with eng.Fori(0, E // 2) as pair:
                    for par in range(2):
                        expert(2 * pair + par, pair, par)

            def plain_or_general(eng, plain, general):
                chosen = eng.value_load(flag[0:1, 0:1], min_val=0, max_val=1)
                with eng.If(chosen == 1):
                    plain(eng)
                with eng.Else():
                    general(eng)

            def all_general_sync(sp):
                sp_side1(sp, 0, QK1)
                sp.wait_ge(scattered, 16 * TILES)

                def expert(e, pair, par):
                    sp.wait_ge(x_read, e * EI + X0)
                    sp_expert_in(sp, e, par)
                    sp_expert_out(sp, e)
                general_experts(sp, expert)
                general_sync(sp)
                sp_output(sp)

            def all_general_tensor(pe):
                for w in range(W):
                    pe_side1(pe, w)
                for w in range(W):
                    pe_routing(pe, w)

                def expert(e, pair, par):
                    for w in range(EI):
                        pe_expert(pe, e, pair, par, w)
                general_experts(pe, expert)
                general_tensor(pe)
                pe.wait_ge(g_done, UNITS * SIDE_B * QT + 1)
                for n in range(NQ_SIDE):
                    for w in range(OUT_STEPS):
                        pe_output(pe, n, w)

            def all_general_scalar(act):
                act_gate(act)
                general_scalar(act)

            def all_general_vector(dve):
                for w in range(W):
                    dve_side1(dve, w)
                for w in range(W):
                    dve_routing(dve, w)

                def expert(e, pair, par):
                    for w in range(EI):
                        dve_expert(dve, e, par, w)
                general_experts(dve, expert)
                general_vector(dve)
                for n in range(NQ_SIDE):
                    for w in range(OUT_STEPS):
                        dve_output(dve, n, w)

            def all_general_gpsimd(pool):
                pool.sem_inc(fc_out, 16)
                for c in range(CHUNKS):
                    pool_scatter(pool, c)
                for c in range(CHUNKS):
                    pool_combine(pool, c)

            with nc.Block() as block:

                @block.sync
                def _(sp):
                    plain_or_general(sp, plain_sync, all_general_sync)

                @block.tensor
                def _(pe):
                    plain_or_general(pe, plain_tensor, all_general_tensor)

                @block.scalar
                def _(act):
                    plain_or_general(act, plain_scalar, all_general_scalar)

                @block.vector
                def _(dve):
                    plain_or_general(dve, plain_vector, all_general_vector)

                @block.gpsimd
                def _(pool):
                    plain_or_general(pool, plain_gpsimd, all_general_gpsimd)

        fin = ExitStack()
        with fin:
            def fsem(name):
                return fin.enter_context(nc.semaphore(name))

            hT = [T[1][:, i * BANK:(i + 1) * BANK] for i in range(2)]
            h_turned, h_copied, o_made, o_added, stored = (fsem(n) for n in (
                "h_turned", "h_copied", "o_made", "o_added", "stored"))
            hv = heads[:, :].rearrange("p (t f) -> p t f", f=D)
            T0 = SIDE_TILES
            N = SIDE_TILES // TB

            with nc.Block() as block:

                @block.tensor
                def _(pe):
                    def project(n):
                        pe.wait_ge(h_copied, n + 1)
                        if n >= 2:
                            pe.wait_ge(o_added, n - 1)
                        for i in range(TB):
                            ins = nc.tensor.matmul(banks[2 + n % 2][:, i * D:(i + 1) * D], hT[n % 2][:, i * P:(i + 1) * P],
                                                   wo_s[:, :], start=True, stop=True)
                        ins.then_inc(o_made, 1)

                    for n in range(N):
                        if n >= 2:
                            pe.wait_ge(h_copied, n - 1)
                        for i in range(TB):
                            t = T0 + n * TB + i
                            ins = nc.tensor.transpose(banks[n % 2][:, i * P:(i + 1) * P],
                                                      hv[:, t, :], ident[:, :])
                        ins.then_inc(h_turned, 1)
                        if n:
                            project(n - 1)
                    project(N - 1)

                @block.scalar
                def _(act):
                    for n in range(N):
                        act.wait_ge(h_turned, n + 1)
                        if n >= 2:
                            act.wait_ge(o_made, n - 1)
                        nc.scalar.activation(hT[n % 2], banks[n % 2][:, :], ACT.Copy).then_inc(h_copied, 1)

                @block.vector
                def _(dve):
                    for n in range(N):
                        dve.wait_ge(o_made, n + 1)
                        b = base[:, T0 + n * TB:T0 + (n + 1) * TB, :]
                        nc.vector.tensor_tensor(b, b, banks[2 + n % 2][:, :].rearrange("p (t d) -> p t d", d=D), ALU.add).then_inc(o_added, 1)

                @block.sync
                def _(sp):
                    ov = out.rearrange("b (t p) d -> p (b t) d", p=P)
                    for n in range(N):
                        sp.wait_ge(o_added, n + 1)
                        sp.dma_start(ov[:, T0 + n * TB:T0 + (n + 1) * TB, :], base[:, T0 + n * TB:T0 + (n + 1) * TB, :]).then_inc(stored, 16)
                    sp.wait_ge(stored, 16 * (N))
_INS = ['L0_attn_x', 'L0_attn_Wq', 'L0_attn_bq', 'L0_attn_Wk', 'L0_attn_bk', 'L0_attn_Wv', 'L0_attn_bv', 'L0_attn_Wo',
        'L0_attn_bo', 'L0_attn_phase_modulators', 'L0_attn_interference_weights', 'L0_ffn_gate_w', 'L0_ffn_w1',
        'L0_ffn_b1', 'L0_ffn_w2', 'L0_ffn_b2']


def kernel(**inputs):
    import numpy as _np
    import concourse.bacc as _bacc
    from concourse import mybir as _mybir
    from concourse.bass_utils import run_bass_kernel_spmd as _run

    nc = _bacc.Bacc("TRN2", target_bir_lowering=False, num_devices=1)
    arrays, args = {}, []
    for name in _INS:
        a = _np.ascontiguousarray(inputs[name])
        arrays[f"in_{name}_dram"] = a
        args.append(nc.dram_tensor(f"in_{name}_dram", a.shape, _mybir.dt.from_np(a.dtype), kind="ExternalInput").ap())
    shape = inputs['L0_attn_x'].shape
    out = nc.dram_tensor("out_0_dram", shape, _mybir.dt.float32, kind="ExternalOutput").ap()
    attention_and_experts(nc, *args, out)
    r = _run(nc, [arrays], core_ids=[0])
    return r.results[0]["out_0_dram"]
```

```python
import numpy as np
import concourse.bass as bass
from concourse import mybir
from contextlib import ExitStack


def attention_and_experts(nc, x, Wq, bq, Wk, bk, Wv, bv, Wo, bo, phase, weights, gate_w, w1, b1, w2, b2, out):
    f32, bf16, i32 = mybir.dt.float32, mybir.dt.bfloat16, mybir.dt.int32
    ALU, ACT, AX = mybir.AluOpType, mybir.ActivationFunctionType, mybir.AxisListType
    ds = bass.ds

    BATCH, SEQ, D = x.shape
    W, H = phase.shape
    HD = D // H
    E, _, DFF = w1.shape
    P = 128
    TOK = BATCH * SEQ
    TILES = TOK // P
    QT = SEQ // P
    SIDES = 2
    SIDE_B = BATCH // SIDES
    SIDE_TILES = TILES // SIDES
    SIDE_TOK = TOK // SIDES
    UNITS = SIDES * H
    BLK = QT * SEQ
    COLS = SIDE_B * BLK
    BANK = 512
    CAP = -(-5 * TOK // (4 * E))
    CT = CAP // P
    HC = CAP // 2
    FCH = DFF // P
    SCALE = 1.0 / np.sqrt(HD)
    KERR = 2.7e-18 * 1000000.0
    EPS = 1e-5
    PARTS = 3
    PROD = PARTS * PARTS * HD
    MAXROW = 96
    STACK = MAXROW + PARTS
    VC = 32
    OC = HD + 1
    GR = 4
    OTW = (BANK // P) * GR
    TWO_PI = 2.0 * np.pi
    C1 = 6.28125
    C2 = float(np.float32(np.round((TWO_PI - C1) * 2.0**21) / 2.0**21))
    C3 = TWO_PI - C1 - C2
    ROUND = 1.5 * 2.0**23
    S_PLAIN = 0.9 * np.sqrt(2.0**-12 / KERR)

    parts_dram = nc.dram_tensor("qk_parts", (2, SIDES, D, PARTS, SIDE_TOK), bf16, kind="Internal").ap()
    slots_dram = nc.dram_tensor("dispatched", (E * CAP + TOK, D), f32, kind="Internal").ap()
    expert_dram = nc.dram_tensor("expert_out", (E * CAP, D), f32, kind="Internal").ap()

    TB = BANK // P
    NQ = TOK // BANK
    NQ_SIDE = NQ // SIDES
    CHUNKS = 4
    CH = TILES // CHUNKS
    WH = W // 2
    RING = 2
    ZCOLS = 1024

    ctx = ExitStack()
    with ctx:
        def sb(name, shape, dt=f32):
            return ctx.enter_context(nc.sbuf_tensor(name, shape, dt))

        def sem(name):
            return ctx.enter_context(nc.semaphore(name))

        ident = sb("ident", [P, P])
        identb = sb("identb", [P, P], bf16)
        ones_b = sb("ones_b", [P, P], bf16)
        below_b = sb("below_b", [P, P], bf16)
        one_col = sb("one_col", [P, 1])
        order8, ebase = sb("order8", [P, E]), sb("ebase", [P, E])
        token_row = sb("token_row", [P, TILES])
        wq_s, wk_s, wv_s, wo_s = (sb(n, [P, D]) for n in ("wq_s", "wk_s", "wv_s", "wo_s"))
        bq_s, bk_s = sb("bq_s", [P, 1]), sb("bk_s", [P, 1])
        bv_s, bo_s = sb("bv_s", [P, D]), sb("bo_s", [P, D])
        gw_s = sb("gw_s", [P, E])
        b1_s = sb("b1_s", [P, E, FCH])
        iw_s = sb("iw_s", [P, W])
        cw = sb("cw", [P, UNITS * W])
        base = sb("base", [P, TILES, D])
        xnT = sb("xnT", [P, TOK])
        heads = xnT
        region = sb("region", [P, TOK])
        xn = region[:, :].rearrange("p (t d) -> p t d", d=D)
        Vall = sb("Vall", [P, UNITS * SIDE_TILES * HD])
        T = [sb(f"T{i}", [P, COLS]) for i in range(2)]
        Pr = [sb(f"Pr{i}", [P, COLS]) for i in range(RING)]
        work = sb("work", [P, 2 * CAP + 4 * DFF])
        PARTW = PARTS * BANK // 2
        part = [work[:, i * PARTW:(i + 1) * PARTW].bitcast(bf16).rearrange("p (i c) -> p i c", i=PARTS) for i in range(2)]
        part0 = [Pr[m // NQ_SIDE][:, (m % NQ_SIDE) * PARTW:(m % NQ_SIDE + 1) * PARTW].bitcast(bf16).rearrange("p (i c) -> p i c", i=PARTS)
                 for m in range(2 * NQ_SIDE)]
        rest = [work[:, 2 * PARTW + i * BANK:2 * PARTW + (i + 1) * BANK] for i in range(2)]
        e_x = [region[:, i * CAP:(i + 1) * CAP].rearrange("p (t d) -> p t d", d=D) for i in range(2)]
        e_h = region[:, 2 * CAP:2 * CAP + FCH * CAP].rearrange("p (f c) -> p f c", f=FCH)
        e_xT = work[:, 0:CAP]
        e_o = work[:, CAP:2 * CAP].rearrange("p (t d) -> p t d", d=D)
        e_w1 = [work[:, 2 * CAP + i * DFF:2 * CAP + (i + 1) * DFF] for i in range(2)]
        e_w2 = [work[:, 2 * CAP + (2 + i) * DFF:2 * CAP + (3 + i) * DFF].rearrange("p (f d) -> p f d", d=D) for i in range(2)]
        e_b2 = [sb(f"e_b2{i}", [P, D]) for i in range(2)]
        lg = sb("lg", [P, 6, TILES * E])
        maskb = sb("maskb", [P, TILES * E], bf16)
        r = sb("r", [P, 10, TILES])
        idx_scatter, idx_gather = sb("idx_scatter", [P, TILES], i32), sb("idx_gather", [P, TILES], i32)
        Qs = [sb(f"Qs{i}", [P, SIDE_TOK], bf16) for i in range(2)]
        Ks = [sb(f"Ks{i}", [P, SIDE_TOK], bf16) for i in range(2)]
        Vst = [sb(f"Vst{i}", [P, SIDE_TILES, VC]) for i in range(2)]
        pv_s = [sb(f"pv_s{i}", [P, BANK]) for i in range(2)]
        OT = [sb(f"OT{i}", [P, WH * OTW * OC]) for i in range(2)]
        rsum = [sb(f"rsum{i}", [P, WH * OTW]) for i in range(2)]
        gain = sb("gain", [P, WH * OTW])
        terms = sb("terms", [P, WH + 1, OTW * HD])
        flat_terms = terms[:, :, :].rearrange("p w a -> p (w a)")
        mv = flat_terms[:, 0:2 * TILES].rearrange("p (t s) -> p t s", s=2)
        ln = flat_terms[:, 2 * TILES:8 * TILES].rearrange("p (a t) -> p a t", a=6)
        negmax = [sb(f"negmax{i}", [P, SIDE_TILES]) for i in range(2)]
        nm_rest = sb("nm_rest", [P, SIDE_TILES])
        nm_parts = sb("nm_parts", [P, P], bf16)
        nm_rows = sb("nm_rows", [PARTS * SIDE_TILES, P], bf16)
        flag = sb("flag", [1, 1], i32)

        banks = [ctx.enter_context(nc.psum_tensor(f"bank{i}", [P, BANK], f32)) for i in range(7)]
        bank_b = ctx.enter_context(nc.psum_tensor("bank_b", [P, 2 * BANK], bf16))
        pv_bank, tr_bank, sc_bank, x_bank = banks[0:2], banks[2], banks[3:5], banks[5:7]

        stack_in = [sem(f"stack_in{i}") for i in range(2)]
        LOADS = (1 + PARTS) * 16
        parts_out = [sem(f"parts_out{i}") for i in range(2)]
        small_in, const_ready = sem("small_in"), sem("const_ready")
        SMALL = 8 * 16

        def over(a, n):
            return a.unsqueeze(2).to_broadcast([P, a.shape[1], n])

        def load_stack(sp, u, par, c0=0, n=SIDE_TOK, done=None):
            rows = parts_dram[:, :, :, :, :].rearrange("k s f i c -> k (s f) i c")
            q, k = (rows[kind, ds(u * HD, HD), :, ds(c0, n)] for kind in range(2))
            (d_step, _), (i_step, _), (c_step, _) = k.ap
            to = slice(0, n) if done else slice(c0, c0 + n)
            sp.dma_start(Ks[par][0:PROD, to], bass.AP(k.tensor, k.offset, [[0, PARTS], [i_step, HD * PARTS], [c_step, n]])
                         ).then_inc(done or stack_in[par], 16)
            for i in range(PARTS):
                qi = q[:, i, :]
                sp.dma_start(Qs[par][i * PARTS * HD:(i + 1) * PARTS * HD, to],
                             bass.AP(qi.tensor, qi.offset, [[d_step, HD], [0, PARTS], [c_step, n]])).then_inc(done or stack_in[par], 16)

        def store_parts(sp, m):
            n, kind = m // 2, m % 2
            col = (n % NQ_SIDE) * BANK
            src = part0[m] if n < NQ_SIDE else part[m % 2]
            sp.dma_start(parts_dram[kind, n // NQ_SIDE, :, :, col:col + BANK], src).then_inc(parts_out[m // 4 if n < NQ_SIDE else m % 2], 16)

        def v_to_tiles(n, bank):
            side, ts = n // NQ_SIDE, (n % NQ_SIDE) * TB
            size = H * SIDE_TILES * HD
            dst = Vall[:, side * size:(side + 1) * size].rearrange("p (h t d) -> p t h d", h=H, d=HD)
            return nc.vector.tensor_tensor(dst[:, ts:ts + TB, :, :], bank[:, :].rearrange("p (t h d) -> p t h d", h=H, d=HD),
                                           bv_s[:, :].rearrange("p (h d) -> p h d", d=HD).unsqueeze(1).to_broadcast([P, TB, H, HD]), ALU.add)

        setup = ExitStack()
        with setup:
            def ssem(name):
                return setup.enter_context(nc.semaphore(name))

            zeros = T[1][:, COLS - ZCOLS:COLS]
            cut = [0]

            def scratch(n):
                cut[0] += n
                return T[0][:, cut[0] - n:cut[0]]

            phase_s = scratch(W * H)
            ph = scratch(4 * W * H).rearrange("p (a b) -> p a b", a=4)
            stats = scratch(6 * TILES).rearrange("p (t s) -> p t s", s=6)
            wsq = scratch(2 * D)
            brow = scratch(2 * D)[0:1, :]
            bound = scratch(4 * D)[0:1, :]
            one = scratch(4)[0:1, :]
            gb_rows = T[1][0:E * FCH, 0:2 * P].rearrange("p (a b) -> p a b", a=2)
            one_root = T[1][:, 2 * P:2 * P + 1]

            x_in = [ssem(f"x_in{c}") for c in range(CHUNKS)]
            bias_in, root_table = ssem("bias_in"), ssem("root_table")
            wqk_in, w_in, zeroed, pool_const = ssem("wqk_in"), ssem("w_in"), ssem("zeroed"), ssem("pool_const")
            chain, pool_chain, var_ready, root_ready, rstd_ready, xn_ready = (ssem(n) for n in (
                "chain", "pool_chain", "var_ready", "root_ready", "rstd_ready", "xn_ready"))
            xT_made, xT_copied = ssem("xT_made"), ssem("xT_copied")
            proj, part1, rest1, part2, part3 = (ssem(n) for n in ("proj", "part1", "rest1", "part2", "part3"))
            v_made = ssem("v_made")
            angle, sine = ssem("angle"), ssem("sine")
            gb_turned = ssem("gb_turned")
            w_squared, norms_made, norms_ready = ssem("w_squared"), ssem("norms_made"), ssem("norms_ready")

            with nc.Block() as block:

                @block.sync
                def _(sp):
                    xv = x.rearrange("b (t p) d -> p (b t) d", p=P)
                    for c in range(CHUNKS):
                        sp.dma_start(base[:, c * CH:(c + 1) * CH, :], xv[:, c * CH:(c + 1) * CH, :]).then_inc(x_in[c], 16)
                        if c == 0:
                            for dst, src in ((wq_s, Wq), (wk_s, Wk)):
                                sp.dma_start(dst[:, :], src).then_inc(wqk_in, 16)
                    sp.dma_start(phase_s, phase.rearrange("w h -> (w h)").partition_broadcast(P)).then_inc(small_in, 16)
                    sp.dma_start(brow[:, 0:D], bq.rearrange("(a d) -> a d", a=1)).then_inc(small_in, 16)
                    sp.dma_start(brow[:, D:2 * D], bk.rearrange("(a d) -> a d", a=1)).then_inc(small_in, 16)
                    sp.dma_start(iw_s[:, :], weights.partition_broadcast(P)).then_inc(small_in, 16)
                    sp.dma_start(bv_s[:, :], bv.partition_broadcast(P)).then_inc(small_in, 16)
                    sp.dma_start(bo_s[:, :], bo.partition_broadcast(P)).then_inc(small_in, 16)
                    sp.dma_start(gb_rows[0:E * FCH, 0, :], b1.rearrange("e (f p) -> (e f) p", p=P)).then_inc(small_in, 16)
                    sp.dma_start(gb_rows[0:E, 1, :], gate_w).then_inc(small_in, 16)
                    for dst, src in ((wv_s, Wv), (wo_s, Wo)):
                        sp.dma_start(dst[:, :], src).then_inc(w_in, 16)
                    sp.wait_ge(const_ready, 1)
                    rows = P * ZCOLS // D
                    for z in range(E * CAP // rows):
                        sp.dma_start(slots_dram[z * rows:(z + 1) * rows, :].rearrange("(p a) d -> p (a d)", p=P), zeros).then_inc(zeroed, 16)

                    for m in range(2 * NQ_SIDE):
                        sp.wait_ge(part3, m + 1)
                        store_parts(sp, m)
                    sp.wait_ge(pool_const, 13)
                    sp.wait_ge(parts_out[0], 16 * NQ_SIDE)
                    load_stack(sp, 0, 0, 0, SIDE_TOK // 2)
                    sp.wait_ge(parts_out[1], 16 * NQ_SIDE)
                    load_stack(sp, 0, 0, SIDE_TOK // 2, SIDE_TOK // 2)
                    load_stack(sp, 1, 1)
                    sp.wait_ge(zeroed, 16 * (E * CAP // rows))

                @block.gpsimd
                def _(pool):
                    pool.memset(one_col[:, :], 1.0).then_inc(root_table, 1)
                    pool.memset(zeros, 0.0).then_inc(const_ready, 1)
                    pool.memset(ident[:, :], 0.0).then_inc(pool_const, 1)
                    pool.memset(identb[:, :], 0.0).then_inc(pool_const, 1)
                    pool.memset(ones_b[:, :], 1.0).then_inc(pool_const, 1)
                    pool.wait_ge(pool_const, 3)
                    for m in (ident, identb):
                        pool.affine_select(out=m[:, :], in_=m[:, :], compare_op=ALU.not_equal, fill=1.0,
                                           base=0, pattern=[[-1, P]], channel_multiplier=1).then_inc(const_ready, 1)
                    for i in range(2):
                        pool.memset(Qs[i][:, :], 0.0).then_inc(pool_const, 1)
                        pool.memset(Ks[i][:, :], 0.0).then_inc(pool_const, 1)
                        pool.memset(Vst[i][:, :, :], 0.0).then_inc(pool_const, 1)
                    pool.wait_ge(pool_const, 9)
                    for i in range(2):
                        pool.memset(Vst[i][:, :, HD:OC], 1.0).then_inc(pool_const, 1)
                    for i in range(2):
                        pool.wait_ge(pool_const, 11 + i)
                        pool.memset(Ks[i][MAXROW:STACK, :], 1.0).then_inc(pool_const, 1)
                    pool.wait_ge(pool_const, 13)
                    pool.memset(nm_parts[:, :], 0.0)
                    pool.affine_select(out=below_b[:, :], in_=ones_b[:, :], compare_op=ALU.is_gt, fill=0.0,
                                       base=0, pattern=[[1, P]], channel_multiplier=-1)
                    pool.iota(order8[:, :], pattern=[[-1, E]], base=E, channel_multiplier=0, allow_small_or_imprecise_dtypes=True)
                    pool.iota(ebase[:, :], pattern=[[CAP, E]], base=0, channel_multiplier=0, allow_small_or_imprecise_dtypes=True)
                    pool.iota(token_row[:, :], pattern=[[P, TILES]], base=E * CAP, channel_multiplier=1,
                              allow_small_or_imprecise_dtypes=True)

                    pool_steps = [0]

                    def link(ins):
                        pool_steps[0] += 1
                        ins.then_inc(pool_chain, 1)
                        pool.wait_ge(pool_chain, pool_steps[0])

                    pool.wait_ge(wqk_in, 32)
                    nc.gpsimd.tensor_tensor(wsq[:, 0:D], wq_s[:, :], wq_s[:, :], ALU.mult).then_inc(w_squared, 1)
                    nc.gpsimd.tensor_tensor(wsq[:, D:2 * D], wk_s[:, :], wk_s[:, :], ALU.mult).then_inc(w_squared, 1)
                    pool.wait_ge(small_in, SMALL)
                    link(nc.gpsimd.tensor_scalar(ph[:, 0, :], phase_s, 1.0 / TWO_PI, 0.25, ALU.mult, ALU.add))
                    link(nc.gpsimd.tensor_scalar(ph[:, 1, :], ph[:, 0, :], ROUND, None, ALU.add))
                    link(nc.gpsimd.tensor_scalar(ph[:, 0, :], ph[:, 1, :], -ROUND, None, ALU.add))
                    for i, c in enumerate((C1, C2, C3)):
                        source, product, rest_ = ((phase_s, 1, 2), (ph[:, 2, :], 1, 3), (ph[:, 3, :], 1, 2))[i]
                        link(nc.gpsimd.tensor_scalar(ph[:, product, :], ph[:, 0, :], -c, None, ALU.mult))
                        link(nc.gpsimd.tensor_tensor(ph[:, rest_, :], ph[:, product, :], source, ALU.add))
                    link(nc.gpsimd.tensor_scalar(ph[:, 0, :], ph[:, 2, :], np.pi / 2, np.pi, ALU.add, ALU.min))
                    nc.gpsimd.tensor_scalar(ph[:, 1, :], ph[:, 0, :], -np.pi, None, ALU.max).then_inc(angle, 1)
                    nc.gpsimd.tensor_scalar(iw_s[:, :], iw_s[:, :], 1.0 / W, None, ALU.mult)
                    pool.wait_ge(sine, 1)
                    link(nc.gpsimd.tensor_scalar(ph[:, 0, :], ph[:, 2, :], SCALE, None, ALU.mult))
                    scaled, cosine = (ph[:, i, :].rearrange("p (w h) -> p w h", w=W) for i in (0, 2))
                    for side in range(SIDES):
                        c_side = cw[:, side * H * W:(side + 1) * H * W].rearrange("p (h w) -> p w h", w=W)
                        nc.gpsimd.tensor_tensor(c_side, scaled, cosine, ALU.mult)

                @block.scalar
                def _(act):
                    act.dma_start(bq_s[:, :], bq.rearrange("(d a) -> d a", a=1)).then_inc(bias_in, 16)
                    act.dma_start(bk_s[:, :], bk.rearrange("(d a) -> d a", a=1)).then_inc(bias_in, 16)

                    def root(c, n=1):
                        act.wait_ge(var_ready, c + n)
                        s = slice(c * CH, (c + n) * CH)
                        nc.scalar.activation(ln[:, 1, s], ln[:, 0, s], ACT.Sqrt).then_inc(root_ready, 1)

                    act.wait_ge(root_table, 1)
                    nc.scalar.activation(one_root, one_col[:, :], ACT.Sqrt)
                    root(0)

                    def copy_xT(n):
                        act.wait_ge(xT_made, n + 1)
                        nc.scalar.activation(xnT[:, n * BANK:(n + 1) * BANK], banks[n % 2][:, :], ACT.Copy).then_inc(xT_copied, 1)

                    def first_part(m):
                        act.wait_ge(proj, m + 1)
                        nc.scalar.activation(part0[m][:, 0, :], banks[2 + m % 4][:, :], ACT.Identity,
                                             bias=(bq_s, bk_s)[m % 2][:, :]).then_inc(part1, 1)

                    def second_part(m):
                        act.wait_ge(rest1, m + 1)
                        nc.scalar.activation(part0[m][:, 1, :], rest[m % 2], ACT.Copy).then_inc(part2, 1)

                    copy_xT(0)
                    root(1)
                    act.wait_ge(bias_in, 32)
                    for m in range(2 * NQ_SIDE):
                        first_part(m)
                        if m % 2 == 0 and m // 2 + 1 < NQ_SIDE:
                            copy_xT(m // 2 + 1)
                        if m:
                            second_part(m - 1)
                    second_part(2 * NQ_SIDE - 1)
                    act.wait_ge(gb_turned, 1)
                    nc.scalar.activation(b1_s[:, :, :].rearrange("p e f -> p (e f)"), banks[0][:, 0:E * FCH], ACT.Copy)
                    nc.scalar.activation(gw_s[:, :], banks[0][:, E * FCH:E * FCH + E], ACT.Copy)
                    root(2, 2)
                    act.wait_ge(norms_made, 1)
                    nc.scalar.activation(bound[:, 0:2 * D], banks[6][0:1, 0:2 * D], ACT.Sqrt, scale=float(D)).then_inc(norms_ready, 1)
                    act.wait_ge(angle, 1)
                    nc.scalar.activation(ph[:, 2, :], ph[:, 1, :], ACT.Sin).then_inc(sine, 1)
                @block.vector
                def _(dve):
                    count = [0]

                    def link(ins):
                        count[0] += 1
                        ins.then_inc(chain, 1)
                        dve.wait_ge(chain, count[0])

                    def sums(c):
                        dve.wait_ge(x_in[c], 16)
                        for t in range(c * CH, (c + 1) * CH):
                            ins = nc.vector.bn_stats(stats[:, t, :], base[:, t, :])
                        link(ins)

                    def moments(c):
                        for t in range(c * CH, (c + 1) * CH):
                            ins = nc.vector.bn_aggr(mv[:, t, :], stats[:, t, :])
                        link(ins)
                        s = slice(c * CH, (c + 1) * CH)
                        nc.vector.tensor_scalar(ln[:, 0, s], mv[:, s, 1], EPS, None, ALU.add).then_inc(var_ready, 1)

                    def inverse_root(c, n=1):
                        s = slice(c * CH, (c + n) * CH)
                        dve.wait_ge(root_ready, c + 1)
                        link(nc.vector.reciprocal(ln[:, 2, s], ln[:, 1, s]))
                        link(nc.vector.tensor_tensor(ln[:, 3, s], ln[:, 2, s], ln[:, 2, s], ALU.mult))
                        link(nc.vector.scalar_tensor_tensor(ln[:, 4, s], ln[:, 3, s], -0.5, ln[:, 0, s], ALU.mult, ALU.mult))
                        nc.vector.scalar_tensor_tensor(ln[:, 5, s], ln[:, 4, s], 1.5, ln[:, 2, s], ALU.add, ALU.mult).then_inc(rstd_ready, 1)

                    def normalise(c):
                        inverse_root(c)
                        dve.wait_ge(rstd_ready, c + 1)
                        for t in range(c * CH, (c + 1) * CH):
                            nc.vector.tensor_scalar(xn[:, t, :], base[:, t, :], mv[:, t, 0:1], ln[:, 5, t:t + 1],
                                                    ALU.subtract, ALU.mult).then_inc(xn_ready, 1)

                    sums(0)
                    moments(0)
                    sums(1)
                    normalise(0)
                    moments(1)
                    normalise(1)

                    def rest_of(m):
                        dve.wait_ge(part1, m + 1)
                        if m >= 2:
                            dve.wait_ge(part3, m - 1)
                        nc.vector.scalar_tensor_tensor(rest[m % 2], banks[2 + m % 4][:, :], (bq_s, bk_s)[m % 2][:, :],
                                                       part0[m][:, 0, :], ALU.add, ALU.subtract).then_inc(rest1, 1)

                    def third_part(m):
                        dve.wait_ge(part2, m + 1)
                        nc.vector.tensor_tensor(part0[m][:, 2, :], rest[m % 2], part0[m][:, 1, :], ALU.subtract).then_inc(part3, 1)

                    for m in range(2 * NQ_SIDE):
                        rest_of(m)
                        if m:
                            third_part(m - 1)
                    third_part(2 * NQ_SIDE - 1)
                    for c in range(2, CHUNKS):
                        sums(c)
                        moments(c)
                    for n in range(NQ_SIDE):
                        dve.wait_ge(v_made, n + 1)
                        v_to_tiles(n, banks[2 + n])
                    inverse_root(2, 2)
                    dve.wait_ge(norms_ready, 1)
                    dve.wait_ge(small_in, SMALL)
                    link(nc.vector.scalar_tensor_tensor(bound[:, 2 * D:4 * D], brow, -1.0, brow, ALU.mult, ALU.max))
                    link(nc.vector.tensor_tensor(brow, bound[:, 0:2 * D], bound[:, 2 * D:4 * D], ALU.add))
                    link(nc.vector.reduce_max(one[:, 0:2], brow.rearrange("a (k p) -> a k p", p=D), AX.X))
                    link(nc.vector.tensor_tensor(one[:, 2:3], one[:, 0:1], one[:, 1:2], ALU.mult))
                    link(nc.vector.tensor_scalar(one[:, 3:4], one[:, 2:3], SCALE * HD, S_PLAIN, ALU.mult, ALU.is_lt))
                    link(nc.vector.tensor_copy(flag[:, :], one[:, 3:4]))

                @block.tensor
                def _(pe):
                    def turn_x(n):
                        pe.wait_ge(xn_ready, (n + 1) * TB)
                        if n >= 2:
                            pe.wait_ge(xT_copied, n - 1)
                        for i in range(TB):
                            ins = nc.tensor.transpose(banks[n % 2][:, i * P:(i + 1) * P], xn[:, n * TB + i, :], ident[:, :])
                        ins.then_inc(xT_made, 1)

                    pe.wait_ge(const_ready, 3)
                    turn_x(0)
                    pe.wait_ge(wqk_in, 32)
                    for n in range(NQ_SIDE):
                        pe.wait_ge(xT_copied, n + 1)
                        for kind, w in enumerate((wq_s, wk_s)):
                            m = 2 * n + kind
                            if m >= 4:
                                pe.wait_ge(rest1, m - 3)
                            nc.tensor.matmul(banks[2 + m % 4][:, :], w[:, :], xnT[:, n * BANK:(n + 1) * BANK],
                                             start=True, stop=True).then_inc(proj, 1)
                            if kind == 0 and n + 1 < NQ_SIDE:
                                turn_x(n + 1)
                    pe.wait_ge(w_squared, 2)
                    nc.tensor.matmul(banks[6][0:1, 0:2 * D], one_col[:, :], wsq, start=True, stop=True).then_inc(norms_made, 1)
                    pe.wait_ge(w_in, 32)
                    pe.wait_ge(rest1, 2 * NQ_SIDE)
                    for n in range(NQ_SIDE):
                        for i in range(TB):
                            t = n * TB + i
                            ins = nc.tensor.matmul(banks[2 + n][:, i * D:(i + 1) * D], xnT[:, t * P:(t + 1) * P], wv_s[:, :], start=True, stop=True)
                        ins.then_inc(v_made, 1)
                    pe.wait_ge(small_in, SMALL)
                    nc.tensor.transpose(banks[0][:, 0:E * FCH], gb_rows[:, 0, :], ident[0:E * FCH, 0:E * FCH])
                    nc.tensor.transpose(banks[0][:, E * FCH:E * FCH + E], gb_rows[0:E, 1, :], ident[0:E, 0:E]).then_inc(gb_turned, 1)

        att = ExitStack()
        with att:
            def asem(name):
                return att.enter_context(nc.semaphore(name))

            rows_in = [asem(f"rows_in{i}") for i in range(2)]
            ROWS = PARTS * 16
            sc_made, sc_read = asem("sc_made"), asem("sc_read")
            split, nm_turned, nm_copied = asem("split"), asem("nm_turned"), asem("nm_copied")
            v_staged, exp_done, pv_done, pv_copied, turned, turned_copied = (asem(n) for n in (
                "v_staged", "exp_done", "pv_done", "pv_copied", "turned", "turned_copied"))
            rsum_ready, half_read, summed, pool_step = asem("rsum_ready"), asem("half_read"), asem("summed"), asem("pool_step")
            last_half, exp_table, t0_copied = asem("last_half"), asem("exp_table"), asem("t0_copied")

            x_made, x_read = asem("x_made"), asem("x_read")
            xn1_ready, part_step, side_parts = asem("xn1_ready"), asem("part_step"), asem("side_parts")
            route, gate_in, gate_exp, mask_ready, index_ready = (asem(n) for n in (
                "route", "gate_in", "gate_exp", "mask_ready", "index_ready"))
            scattered, pool_comb, base_ready = asem("scattered"), asem("pool_comb"), asem("base_ready")
            gathered = [asem(f"gathered{c}") for c in range(CHUNKS)]
            fc_in = [asem(f"fc_in{i}") for i in range(2)]
            fc_out, stored0 = asem("fc_out"), asem("stored0")

            LOGITS = NQ_SIDE
            C0 = LOGITS + 1
            QKV0 = C0 + 2
            EI = 2 + 2 * FCH + CT
            X0 = QKV0 + 3 * NQ_SIDE
            XO = X0 + E * EI

            def pool_side1(pool):
                for t in range(SIDE_TILES, TILES):
                    nc.gpsimd.tensor_scalar(xn[:, t, :], base[:, t, :], mv[:, t, 0:1], ln[:, 5, t:t + 1],
                                            ALU.subtract, ALU.mult).then_inc(xn1_ready, 1)

            def pe_side1(pe, w):
                if w < W // 2:
                    if w % 2:
                        return
                    c = w // 2
                    pe.wait_ge(xn1_ready, (c + 1) * TB)
                    if c >= 2:
                        pe.wait_ge(x_read, c - 1)
                    for q in range(TB):
                        ins = nc.tensor.transpose(x_bank[c % 2][:, q * P:(q + 1) * P], xn[:, (NQ_SIDE + c) * TB + q, :], ident[:, :])
                    ins.then_inc(x_made, 1)
                else:
                    if w == W // 2:
                        pe.wait_ge(x_read, LOGITS)
                    share = TILES // (W // 2)
                    for t in range((w - W // 2) * share, (w - W // 2 + 1) * share):
                        ins = nc.tensor.matmul(x_bank[LOGITS % 2][:, t * E:(t + 1) * E], xnT[:, t * P:(t + 1) * P], gw_s[:, :], start=True, stop=True)
                    if w == W - 1:
                        ins.then_inc(x_made, 1)

            def dve_side1(dve, w):
                if w < W // 2 and w % 2 == 0:
                    c = w // 2
                    n = NQ_SIDE + c
                    dve.wait_ge(x_made, c + 1)
                    nc.vector.tensor_copy(xnT[:, n * BANK:(n + 1) * BANK], x_bank[c % 2][:, :]).then_inc(x_read, 1)

            def pe_qkv(pe, par, w):
                c4, phase_ = w // (W // 4), w % 4
                if phase_ == 0:
                    j = par * NQ_SIDE + c4
                    n = NQ_SIDE + j // 2
                    i = QKV0 + (j if par == 0 else NQ_SIDE + 2 * c4)
                    pe.wait_ge(x_read, i - 1)
                    nc.tensor.matmul(x_bank[i % 2][:, :], (wq_s, wk_s)[j % 2][:, :], xnT[:, n * BANK:(n + 1) * BANK],
                                     start=True, stop=True).then_inc(x_made, 1)
                elif par and phase_ >= 2:
                    i = QKV0 + NQ_SIDE + 2 * c4 + 1
                    pe.wait_ge(x_read, i - 1)
                    for q in range((phase_ - 2) * TB // 2, (phase_ - 1) * TB // 2):
                        t = (NQ_SIDE + c4) * TB + q
                        ins = nc.tensor.matmul(x_bank[i % 2][:, q * D:(q + 1) * D], xnT[:, t * P:(t + 1) * P], wv_s[:, :], start=True, stop=True)
                    if phase_ == 3:
                        ins.then_inc(x_made, 1)

            def dve_qkv(dve, par, w):
                c4, phase_ = w // (W // 4), w % 4
                j = par * NQ_SIDE + c4
                i = QKV0 + (j if par == 0 else NQ_SIDE + 2 * c4)
                p_, r_ = part[j % 2], rest[j % 2]
                if phase_ == 0:
                    dve.wait_ge(x_made, i + 1)
                    dve.wait_ge(parts_out[j % 2], 16 * (NQ_SIDE + j // 2))
                    nc.vector.tensor_scalar(p_[:, 0, :], x_bank[i % 2][:, :], (bq_s, bk_s)[j % 2][:, :], None, ALU.add).then_inc(part_step, 1)
                    dve.wait_ge(part_step, 2 * j + 1)
                    nc.vector.scalar_tensor_tensor(r_, x_bank[i % 2][:, :], (bq_s, bk_s)[j % 2][:, :], p_[:, 0, :],
                                                   ALU.add, ALU.subtract).then_inc(x_read, 1)
                elif phase_ == 1:
                    dve.wait_ge(x_read, i + 1)
                    nc.vector.tensor_copy(p_[:, 1, :], r_).then_inc(part_step, 1)
                    dve.wait_ge(part_step, 2 * j + 2)
                    nc.vector.tensor_tensor(p_[:, 2, :], r_, p_[:, 1, :], ALU.subtract).then_inc(side_parts, 1)
                elif par and phase_ == 3:
                    dve.wait_ge(x_made, i + 2)
                    v_to_tiles(NQ_SIDE + c4, x_bank[(i + 1) % 2]).then_inc(x_read, 1)

            PARTS1 = 2 * NQ_SIDE

            def sp_side1(sp, i0, i1):
                for i in range(i0, i1):
                    sp.wait_ge(side_parts, i + 1)
                    store_parts(sp, 2 * NQ_SIDE + i)
                if i1 == PARTS1:
                    for i in range(2):
                        sp.wait_ge(parts_out[i], 16 * NQ)

            def pe_routing(pe, w):
                if w == 6:
                    pe.wait_ge(mask_ready, 1)
                    pe.wait_ge(x_read, C0)
                    for i, before in enumerate((below_b, ones_b)):
                        nc.tensor.matmul(x_bank[i][:, 0:TILES * E], before[:, :], maskb[:, :], start=True, stop=True).then_inc(x_made, 1)

            def dve_routing(dve, w):
                te = [P, TILES, E]
                g = [lg[:, a, :].rearrange("p (t e) -> p t e", e=E) for a in range(6)]
                n = [ROUTED[w]]

                def link(ins):
                    n[0] += 1
                    ins.then_inc(route, 1)
                    dve.wait_ge(route, n[0])

                if w == 0:
                    dve.wait_ge(x_made, C0)
                    nc.vector.tensor_copy(lg[:, 5, :], x_bank[LOGITS % 2][:, 0:TILES * E]).then_inc(x_read, 1)
                if w == 4:
                    dve.wait_ge(x_read, C0)
                    link(nc.vector.reduce_max(r[:, 0, :], g[5], AX.X))
                    nc.vector.tensor_tensor(g[0], g[5], over(r[:, 0, :], E), ALU.subtract).then_inc(gate_in, 1)
                    dve.wait_ge(gate_in, 1)
                    link(nc.vector.scalar_tensor_tensor(g[2], g[0], 0.0, order8[:, :].unsqueeze(1).to_broadcast(te), ALU.is_ge, ALU.mult))
                if w == 5:
                    link(nc.vector.reduce_max(r[:, 1, :], g[2], AX.X))
                    link(nc.vector.tensor_tensor(g[3], g[2], over(r[:, 1, :], E), ALU.is_equal))
                    nc.vector.tensor_copy(maskb[:, :], lg[:, 3, :]).then_inc(mask_ready, 1)
                if w == 6:
                    dve.wait_ge(x_made, C0 + 2)
                    dve.wait_ge(gate_exp, 1)
                    link(nc.vector.tensor_copy(lg[:, 2, :], x_bank[0][:, 0:TILES * E]))
                    link(nc.vector.memset(lg[:, 0, 0:E], 0.0))
                    nc.vector.tensor_copy(lg[:, 0, E:TILES * E], x_bank[1][:, 0:(TILES - 1) * E]).then_inc(x_read, 2)
                    dve.wait_ge(x_read, C0 + 2)
                if 7 <= w < 12:
                    shift = 1 << (w - 7)
                    a, b = (0, 4) if w % 2 else (4, 0)
                    link(nc.vector.tensor_copy(lg[:, b, 0:shift * E], lg[:, a, 0:shift * E]))
                    link(nc.vector.tensor_tensor(lg[:, b, shift * E:], lg[:, a, shift * E:], lg[:, a, 0:(TILES - shift) * E], ALU.add))
                if w == 12:
                    link(nc.vector.tensor_tensor(g[5], g[2], g[4], ALU.add))
                    link(nc.vector.tensor_tensor(g[2], g[5], g[3], ALU.mult))
                    link(nc.vector.reduce_sum(r[:, 4, :], g[2], AX.X))
                if w == 13:
                    link(nc.vector.tensor_tensor(g[5], g[3], ebase[:, :].unsqueeze(1).to_broadcast(te), ALU.mult))
                    link(nc.vector.reduce_sum(r[:, 5, :], g[5], AX.X))
                    link(nc.vector.reduce_sum(r[:, 2, :], g[1], AX.X))
                    link(nc.vector.reciprocal(r[:, 3, :], r[:, 2, :]))
                if w == 14:
                    link(nc.vector.tensor_scalar(r[:, 6, :], r[:, 4, :], float(CAP), None, ALU.is_lt))
                    link(nc.vector.tensor_tensor(r[:, 7, :], r[:, 4, :], r[:, 5, :], ALU.add))
                    link(nc.vector.tensor_tensor(r[:, 8, :], r[:, 7, :], token_row[:, :], ALU.subtract))
                    link(nc.vector.tensor_tensor(r[:, 9, :], r[:, 8, :], r[:, 6, :], ALU.mult))
                    link(nc.vector.tensor_tensor(r[:, 8, :], r[:, 9, :], token_row[:, :], ALU.add))
                if w == 15:
                    nc.vector.tensor_copy(idx_scatter[:, :], r[:, 8, :]).then_inc(index_ready, 1)
                    link(nc.vector.tensor_tensor(r[:, 9, :], r[:, 7, :], r[:, 6, :], ALU.mult))
                    nc.vector.tensor_copy(idx_gather[:, :], r[:, 9, :]).then_inc(index_ready, 1)
                    nc.vector.tensor_tensor(r[:, 0, :], r[:, 3, :], r[:, 6, :], ALU.mult).then_inc(index_ready, 1)

            links = {4: 2, 5: 2, 6: 2, 7: 2, 8: 2, 9: 2, 10: 2, 11: 2, 12: 3, 13: 4, 14: 5, 15: 1}
            ROUTED = [sum(links.get(v, 0) for v in range(w)) for w in range(W)]

            def act_gate(act):
                act.wait_ge(gate_in, 1)
                nc.scalar.activation(lg[:, 1, :], lg[:, 0, :], ACT.Exp).then_inc(gate_exp, 1)

            def pool_scatter(pool, c):
                if c == 0:
                    pool.wait_ge(index_ready, 3)
                for t in range(c * CH, (c + 1) * CH):
                    pool.indirect_dma_start(out=slots_dram, out_offset=bass.IndirectOffsetOnAxis(
                        ap=idx_scatter[:, t:t + 1], axis=0), in_=xn[:, t, :], in_offset=None).then_inc(scattered, 16)

            def sp_expert_in(sp, e, par):
                sp.dma_start(e_x[par], slots_dram[ds(e * CAP, CAP), :].rearrange("(t p) d -> p t d", p=P)).then_inc(fc_in[par], 16)
                w1_rows = w1.rearrange("e d f -> (e d) f")
                w2_rows = w2.rearrange("e f d -> (e f) d")
                sp.dma_start(e_w1[par], w1_rows[ds(e * D, D), :]).then_inc(fc_in[par], 16)
                sp.dma_start(e_w2[par], w2_rows[ds(e * DFF, DFF), :].rearrange("(f p) d -> p f d", p=P)).then_inc(fc_in[par], 16)
                sp.dma_start(e_b2[par][:, :], b2.rearrange("e d -> (e d)")[ds(e * D, D)].partition_broadcast(P)).then_inc(fc_in[par], 16)

            def sp_expert_out(sp, e):
                sp.wait_ge(x_read, (e + 1) * EI + X0)
                sp.dma_start(expert_dram[ds(e * CAP, CAP), :].rearrange("(t p) d -> p t d", p=P), e_o).then_inc(fc_out, 16)

            def pe_expert(pe, e, pair_e, par, w):
                if w >= EI:
                    return
                bank = x_bank[w % 2]
                if w == 0:
                    pe.wait_ge(fc_in[par], (pair_e + 1) * 64)
                pe.wait_ge(x_read, e * EI + (X0 + w - 1 if w else X0))
                if w < 2:
                    for t in range(w * TB, min(CT, (w + 1) * TB)):
                        ins = nc.tensor.transpose(bank[:, (t % TB) * P:(t % TB + 1) * P], e_x[par][:, t, :], ident[:, :])
                elif w < 2 + 2 * FCH:
                    f, half = (w - 2) // 2, (w - 2) % 2
                    if w == 2:
                        pe.wait_ge(x_read, e * EI + (X0 + 2))
                    ins = nc.tensor.matmul(bank[:, 0:HC], e_w1[par][:, f * P:(f + 1) * P], e_xT[:, half * HC:(half + 1) * HC],
                                           start=True, stop=True)
                else:
                    t = w - 2 - 2 * FCH
                    if t == 0:
                        pe.wait_ge(x_read, e * EI + (X0 + 2 + 2 * FCH))
                    for f in range(FCH):
                        ins = nc.tensor.matmul(bank[:, 0:D], e_h[:, f, t * P:(t + 1) * P], e_w2[par][:, f, :], start=f == 0, stop=f == FCH - 1)
                ins.then_inc(x_made, 1)

            def dve_expert(dve, e, par, w):
                if w >= EI:
                    return
                bank = x_bank[w % 2]
                dve.wait_ge(x_made, e * EI + (X0 + w + 1))
                if w < 2:
                    t0, t1 = w * TB, min(CT, (w + 1) * TB)
                    ins = nc.vector.tensor_copy(e_xT[:, t0 * P:t1 * P], bank[:, 0:(t1 - t0) * P])
                elif w < 2 + 2 * FCH:
                    f, half = (w - 2) // 2, (w - 2) % 2
                    ins = nc.vector.tensor_scalar(e_h[:, f, half * HC:(half + 1) * HC], bank[:, 0:HC],
                                                  b1_s[:, :, :].rearrange("p e f -> p (e f)")[:, ds(e * FCH + f, 1)], 0.0, ALU.add, ALU.max)
                else:
                    t = w - 2 - 2 * FCH
                    if t == 0:
                        dve.wait_ge(fc_out, e * 16 + 16)
                    ins = nc.vector.tensor_tensor(e_o[:, t, :], bank[:, 0:D], e_b2[par][:, :], ALU.add)
                ins.then_inc(x_read, 1)

            def pool_combine(pool, c):
                if c == 0:
                    pool.wait_ge(fc_out, 16 * (E + 1))
                s = slice(c * CH, (c + 1) * CH)
                got = region[:, :].rearrange("p (t d) -> p t d", d=D)
                for t in range(c * CH, (c + 1) * CH):
                    pool.indirect_dma_start(out=got[:, t, :], out_offset=None, in_=expert_dram,
                                            in_offset=bass.IndirectOffsetOnAxis(ap=idx_gather[:, t:t + 1], axis=0)).then_inc(gathered[c], 16)
                nc.gpsimd.tensor_tensor(base[:, s, :], base[:, s, :], bo_s[:, :].unsqueeze(1).to_broadcast([P, CH, D]),
                                        ALU.add).then_inc(pool_comb, 1)
                pool.wait_ge(gathered[c], 16 * CH)
                nc.gpsimd.tensor_tensor(got[:, s, :], got[:, s, :], over(r[:, 0, s], D), ALU.mult).then_inc(pool_comb, 1)
                pool.wait_ge(pool_comb, 2 * (c + 1))
                nc.gpsimd.tensor_tensor(base[:, s, :], base[:, s, :], got[:, s, :], ALU.add).then_inc(base_ready, 1)

            hv = heads[:, :].rearrange("p (t f) -> p t f", f=D)
            hT0 = region[:, 0:BANK]
            OUT_STEPS = W // 2

            def pe_output(pe, n, w):
                i = XO + 2 * n
                if w == 0:
                    pe.wait_ge(x_read, i)
                    for q in range(TB):
                        ins = nc.tensor.transpose(x_bank[0][:, q * P:(q + 1) * P], hv[:, n * TB + q, :], ident[:, :])
                    ins.then_inc(x_made, 1)
                if w == 2:
                    pe.wait_ge(x_read, i + 1)
                    for q in range(TB):
                        ins = nc.tensor.matmul(x_bank[1][:, q * D:(q + 1) * D], hT0[:, q * P:(q + 1) * P], wo_s[:, :], start=True, stop=True)
                    ins.then_inc(x_made, 1)

            def dve_output(dve, n, w):
                i = XO + 2 * n
                if w == 0:
                    dve.wait_ge(x_made, i + 1)
                    dve.wait_ge(base_ready, CHUNKS)
                    nc.vector.tensor_copy(hT0, x_bank[0][:, :]).then_inc(x_read, 1)
                if w == 2:
                    dve.wait_ge(x_made, i + 2)
                    b = base[:, n * TB:(n + 1) * TB, :]
                    nc.vector.tensor_tensor(b, b, x_bank[1][:, :].rearrange("p (t d) -> p t d", d=D), ALU.add).then_inc(x_read, 1)

            ov = out.rearrange("b (t p) d -> p (b t) d", p=P)

            def sp_output(sp):
                for n in range(NQ_SIDE):
                    sp.wait_ge(x_read, XO + 2 * n + 2)
                    sp.dma_start(ov[:, n * TB:(n + 1) * TB, :], base[:, n * TB:(n + 1) * TB, :]).then_inc(stored0, 16)
                sp.wait_ge(stored0, 16 * NQ_SIDE)

            def load_rows(sp, u, par):
                sp.wait_ge(nm_copied, u + 2)
                for i in range(PARTS):
                    sp.dma_start(Qs[par][MAXROW + i:MAXROW + i + 1, :].rearrange("a (t c) -> a t c", c=P),
                                 nm_rows[i * SIDE_TILES:(i + 1) * SIDE_TILES, :]).then_inc(rows_in[par], 16)

            BEFORE = 3 * SIDE_B
            EARLY = SIDE_B // 2
            T0_NO = SIDE_B + EARLY

            def pair_no(u, kind, two_ahead=True):
                if isinstance(u, int) and u == 0:
                    return BEFORE + (0 if kind else SIDE_B)
                return BEFORE + 2 * SIDE_B * u + (SIDE_B if kind and two_ahead else 0)

            def pe_scores(pe, no, par, p, rr):
                pe.wait_ge(sc_read, no + p + 1)
                for qt in range(QT):
                    ins = nc.tensor.matmul(sc_bank[rr][:, qt * SEQ:(qt + 1) * SEQ], Qs[par][0:PROD, ds(p * SEQ + qt * P, P)],
                                           Ks[par][0:PROD, ds(p * SEQ, SEQ)], start=True, stop=True)
                ins.then_inc(sc_made, 1)

            def dve_scores(dve, no, par, p, rr):
                dve.wait_ge(sc_made, no + p + 1)
                nc.vector.reduce_max(negmax[par][:, ds(p * QT, QT)], sc_bank[rr][:, :].rearrange("p (t k) -> p t k", k=SEQ),
                                     AX.X, negate=True).then_inc(sc_read, 1)

            def pe_transposed(pe, no, par, p, rr):
                pe.wait_ge(sc_read, no + p + 1)
                transposed_products(par, p, rr)

            def transposed_products(par, p, rr):
                for kt in range(QT):
                    ins = nc.tensor.matmul(sc_bank[rr][:, kt * SEQ:(kt + 1) * SEQ], Ks[par][0:STACK, ds(p * SEQ + kt * P, P)],
                                           Qs[par][0:STACK, ds(p * SEQ, SEQ)], start=True, stop=True)
                ins.then_inc(sc_made, 1)

            def dve_transposed(dve, no, par, p, rr):
                dve.wait_ge(sc_made, no + p + 1)
                nc.vector.tensor_copy(T[par][:, ds(p * BANK, BANK)], sc_bank[rr][:, :]).then_inc(sc_read, 1)

            def dve_split(dve, no, u, par):
                n = SIDE_TILES
                dve.wait_ge(sc_read, no + SIDE_B + 2)
                dve.wait_ge(nm_turned, u + 1)
                nc.vector.tensor_copy(nm_parts[:, 0:n], negmax[par][:, :]).then_inc(split, 1)
                dve.wait_ge(split, 4 * u + 1)
                nc.vector.tensor_tensor(nm_rest[:, :], negmax[par][:, :], nm_parts[:, 0:n], ALU.subtract).then_inc(split, 1)
                dve.wait_ge(split, 4 * u + 2)
                nc.vector.tensor_copy(nm_parts[:, n:2 * n], nm_rest[:, :]).then_inc(split, 1)
                dve.wait_ge(split, 4 * u + 3)
                nc.vector.tensor_tensor(nm_parts[:, 2 * n:3 * n], nm_rest[:, :], nm_parts[:, n:2 * n], ALU.subtract).then_inc(split, 1)

            def pe_turn_max(pe, u):
                pe.wait_ge(split, 4 * u + 4)
                pe.wait_ge(nm_copied, u + 1)
                nc.tensor.transpose(bank_b[:, 0:P], nm_parts[:, :], identb[:, :]).then_inc(nm_turned, 1)

            def dve_turn_max(dve, pair, par):
                u = 2 * pair + par
                if not (isinstance(pair, int) and u == 0):
                    dve.wait_ge(rows_in[1 - par], ROWS * (pair + par))
                dve.wait_ge(nm_turned, u + 2)
                nc.vector.tensor_copy(nm_rows[:, :], bank_b[0:PARTS * SIDE_TILES, 0:P]).then_inc(nm_copied, 1)

            def pe_products(pe, u, par, g, rr):
                pe.wait_ge(v_staged, u + 1)
                pe.wait_ge(exp_done, g + 1)
                pe.wait_ge(pv_copied, g + 1)
                for half in range(2):
                    for kt in range(QT):
                        for j in range(GR):
                            blk = (2 * j + half) * QT + kt
                            ins = nc.tensor.matmul(pv_bank[rr][VC * j:VC * (j + 1), half * SEQ:(half + 1) * SEQ], Vst[par][:, blk, :],
                                                   Pr[rr][:, blk * SEQ:(blk + 1) * SEQ], start=kt == 0, stop=kt == QT - 1)
                ins.then_inc(pv_done, 1)

            def dve_products(dve, g, rr):
                dve.wait_ge(pv_done, g + 1 + 2)
                dve.wait_ge(turned, g + 1)
                nc.vector.tensor_copy(pv_s[rr][:, :], pv_bank[rr][:, :]).then_inc(pv_copied, 1)

            def pe_turn(pe, g, rr):
                pe.wait_ge(pv_copied, g + 1 + 2)
                pe.wait_ge(turned_copied, g + 1)
                for q in range(BANK // P):
                    ins = nc.tensor.transpose(tr_bank[:, q * P:(q + 1) * P], pv_s[rr][:, q * P:(q + 1) * P], ident[:, :])
                ins.then_inc(turned, 1)

            def dve_turned(dve, u, g, half, w):
                dve.wait_ge(half_read, 2 * u + half + 1)
                dve.wait_ge(turned, g + 1 + 2)
                dst = OT[half][:, ds(w * OTW * OC, OTW * OC)].rearrange("p (a c) -> p a c", c=OC)
                nc.vector.tensor_copy(dst, tr_bank[:, :].rearrange("p (a c) -> p a c", c=VC)[:, :, 0:OC]).then_inc(turned_copied, 1)

            def dve_row_sums(dve, u, half):
                dve.wait_ge(turned_copied, W * u + WH * (half + 1) + 1)
                row_sums = OT[half][:, :].rearrange("p (a c) -> p a c", c=OC)[:, :, HD:OC]
                nc.vector.reciprocal(rsum[half][:, :].rearrange("p (a b) -> p a b", b=1), row_sums).then_inc(rsum_ready, 1)

            def act_step(act, g, par, rr):
                act.wait_ge(pv_done, g + 1)
                nc.scalar.activation(Pr[rr][:, :], T[par][:, :], ACT.Exp, scale=cw[:, ds(g, 1)]).then_inc(exp_done, 1)

            def sum_half(eng, ops, step, first, u, half):
                a = WH * OTW
                eng.wait_ge(rsum_ready, 2 * u + half + 1)
                ops.tensor_tensor(gain[:, :].rearrange("p (w a) -> p w a", a=OTW), rsum[half][:, :].rearrange("p (w a) -> p w a", a=OTW),
                                  over(iw_s[:, half * WH:(half + 1) * WH], OTW), ALU.mult).then_inc(step, 1)
                eng.wait_ge(step, first + 1)
                o = OT[half][:, :].rearrange("p (a c) -> p a c", c=OC)[:, :, 0:HD]
                ops.tensor_tensor(terms[:, 0:WH, :].rearrange("p w (a d) -> p (w a) d", d=HD), o, over(gain[:, :], HD),
                                  ALU.mult).then_inc(half_read, 1)
                eng.wait_ge(half_read, 2 * u + half + 3)
                n, k = WH // 2, 1
                while n > 1:
                    ops.tensor_tensor(terms[:, 0:n, :], terms[:, 0:n, :], terms[:, n:2 * n, :], ALU.add).then_inc(step, 1)
                    n, k = n // 2, k + 1
                    eng.wait_ge(step, first + k)
                if half == 0:
                    ops.tensor_tensor(terms[:, WH, :], terms[:, 0, :], terms[:, 1, :], ALU.add).then_inc(step, 1)
                    return k + 1
                ops.tensor_tensor(terms[:, 0, :], terms[:, 0, :], terms[:, 1, :], ALU.add).then_inc(step, 1)
                eng.wait_ge(step, first + k + 1)
                at = u * HD + (u // H) * (SIDE_TILES - 1) * D
                dst = heads[:, ds(at, (SIDE_TILES - 1) * D + HD)]
                dst = bass.AP(dst.tensor, dst.offset, [dst.ap[0], [D, BANK // P], [GR * D, GR], [1, HD]])
                x_, y_ = (terms[:, i, :].rearrange("p (q j d) -> p q j d", j=GR, d=HD) for i in (0, WH))
                ops.tensor_tensor(dst, x_, y_, ALU.add).then_inc(summed, 1)
                return k + 1

            HALF_STEPS = WH.bit_length()

            def stage_v(pool, u, par):
                nc.gpsimd.tensor_copy(Vst[par][:, :, 0:HD], Vall[:, ds(u * SIDE_TILES * HD, SIDE_TILES * HD)]
                                      .rearrange("p (t d) -> p t d", d=HD)).then_inc(v_staged, 1)

            A, B, C, D_ = range(4)
            PHASES = ((A, 0, W // 4), (B, W // 4, 3 * W // 4), (C, 3 * W // 4, W))
            PHASES0 = ((D_, 0, 2), (B, 2, 2 + SIDE_B), (A, 2 + SIDE_B, W - 2), (C, W - 2, W))
            A_PAIRS = SIDE_B // (W // 4)
            LAST = UNITS // 2 - 1
            EPAIR = 2
            EU = 2 * EPAIR

            def run_steps(step, after, first):
                for phase, w0, w1_ in (PHASES0 if first else PHASES):
                    for w in range(w0, w1_):
                        step(phase, w, w - w0, w % 2)
                        if w == WH - 1:
                            after(None)
                    after(phase)

            FIRST, SECOND, PLAIN, EXPERT, FINAL = range(5)

            def units(eng, unit):
                for par in range(2):
                    unit(0, par, FIRST)
                for par in range(2):
                    unit(1, par, SECOND)
                with eng.Fori(EPAIR, EPAIR + E // 2) as pair:
                    for par in range(2):
                        unit(pair, par, EXPERT)
                with eng.Fori(EPAIR + E // 2, LAST) as pair:
                    for par in range(2):
                        unit(pair, par, PLAIN)
                for par in range(2):
                    unit(LAST, par, FINAL)

            def plain_tensor(pe):
                pe.sem_inc(pv_done, 2)
                pe.sem_inc(turned, 2)
                pe.sem_inc(nm_turned, 1)
                for u in range(2):
                    pe.wait_ge(stack_in[u], LOADS * (2 - u))
                    for p in range(SIDE_B):
                        if u == 1 and p == EARLY:
                            pe.wait_ge(rows_in[0], ROWS)
                            for q in range(SIDE_B):
                                if q % 2 == 0 and q:
                                    pe.wait_ge(t0_copied, q // 2)
                                else:
                                    pe.wait_ge(sc_read, T0_NO + q // 2 + q % 2 + 1)
                                transposed_products(0, q, q % 2)
                        pe_scores(pe, 2 * SIDE_B if u and p >= EARLY else SIDE_B * u, u, p, p % 2)
                    pe_turn_max(pe, u)

                def unit(pair, par, kind):
                    u = 2 * pair + par
                    two, one = kind != FINAL, kind != FINAL or par == 0
                    first = kind == FIRST and par == 0

                    def step(phase, w, k, rr):
                        g = u * W + w
                        pe_products(pe, u, par, g, rr)
                        if phase == A and two:
                            pe.wait_ge(stack_in[par], LOADS * (pair + 3 - par))
                            for c in range(A_PAIRS):
                                pe_scores(pe, pair_no(u, 0), par, k * A_PAIRS + c, c % 2)
                        if phase == B and one:
                            pe.wait_ge(rows_in[1 - par], ROWS * (pair + 1 + par))
                            pe_transposed(pe, pair_no(u, 1, two), 1 - par, k, rr)
                        if kind == FIRST:
                            (pe_side1, pe_routing)[par](pe, w)
                        elif kind == SECOND:
                            pe_qkv(pe, par, w)
                        elif kind == EXPERT:
                            pe_expert(pe, u - EU, pair - EPAIR, par, w)
                        elif kind == FINAL:
                            pe_output(pe, 2 * par + w // OUT_STEPS, w % OUT_STEPS)
                        pe_turn(pe, g, rr)

                    def after(phase):
                        if phase == (C if first else B) and two:
                            pe_turn_max(pe, u + 2)

                    run_steps(step, after, first)
                units(pe, unit)

            def plain_vector(dve):
                dve.sem_inc(sc_read, 2)
                dve.sem_inc(pv_copied, 2)
                dve.sem_inc(turned_copied, 1)
                dve.sem_inc(nm_copied, 1)
                for u in range(2):
                    for p in range(SIDE_B):
                        if u == 1 and p == EARLY:
                            for q in range(1, SIDE_B, 2):
                                dve_transposed(dve, T0_NO, 0, q, q % 2)
                            dve.wait_ge(t0_copied, SIDE_B // 2)
                            dve.sem_inc(sc_read, SIDE_B // 2)
                        dve_scores(dve, 2 * SIDE_B if u and p >= EARLY else SIDE_B * u, u, p, p % 2)
                    dve_split(dve, 2 * SIDE_B * u, u, u)
                    dve_turn_max(dve, 0, u)

                def unit(pair, par, kind):
                    u = 2 * pair + par
                    two, one = kind != FINAL, kind != FINAL or par == 0
                    first = kind == FIRST and par == 0

                    def step(phase, w, k, rr):
                        g = u * W + w
                        dve_products(dve, g, rr)
                        if phase == A and two:
                            for c in range(A_PAIRS):
                                dve_scores(dve, pair_no(u, 0), par, k * A_PAIRS + c, c % 2)
                        if phase == B and one:
                            dve.wait_ge(exp_done, W * u + 1)
                            dve_transposed(dve, pair_no(u, 1, two), 1 - par, k, rr)
                        if kind == FIRST:
                            (dve_side1, dve_routing)[par](dve, w)
                        elif kind == SECOND:
                            dve_qkv(dve, par, w)
                        elif kind == EXPERT:
                            dve_expert(dve, u - EU, par, w)
                        elif kind == FINAL:
                            dve_output(dve, 2 * par + w // OUT_STEPS, w % OUT_STEPS)
                        half = halves[0]
                        dve_turned(dve, u, g, half, w - half * WH)

                    halves = [0]

                    def after(phase):
                        if phase == A and two:
                            dve_split(dve, pair_no(u, 0), u + 2, par)
                        if phase is None:
                            dve_row_sums(dve, u, 0)
                            halves[0] = 1
                        if phase == (C if first else B) and two:
                            dve_turn_max(dve, pair + 1, par)
                        if phase == C:
                            dve_row_sums(dve, u, 1)

                    run_steps(step, after, first)
                units(dve, unit)
                dve.wait_ge(pool_step, HALF_STEPS * (2 * UNITS - 1))
                sum_half(dve, nc.vector, last_half, 0, UNITS - 1, 1)
                dve.wait_ge(summed, UNITS)

            def plain_scalar(act):
                nc.scalar.activation(gain[:, 0:1], one_col[:, :], ACT.Exp).then_inc(exp_table, 1)
                for q in range(0, SIDE_B, 2):
                    act.wait_ge(sc_made, T0_NO + q + 1)
                    nc.scalar.activation(T[0][:, q * BANK:(q + 1) * BANK], sc_bank[0][:, :], ACT.Copy).then_inc(t0_copied, 1)

                def unit(pair, par, kind):
                    u = 2 * pair + par
                    if kind == FIRST and par == 0:
                        act.wait_ge(sc_read, T0_NO + SIDE_B + 2)
                    elif kind == FINAL and par == 1:
                        act.wait_ge(sc_read, pair_no(u, 0) - SIDE_B + 2)
                    for half in range(2):
                        with act.Fori(0, WH // 2) as k:
                            for rr in range(2):
                                if kind == FIRST and par == 1:
                                    act.wait_ge(sc_read, pair_no(0, 1) + SIDE_B + 2)
                                elif kind != FIRST and not (kind == FINAL and par == 1):
                                    act.wait_ge(sc_read, pair_no(u, 0) + 2)
                                act_step(act, u * W + half * WH + 2 * k + rr, par, rr)
                        if kind == FIRST and par == 1 and half == 0:
                            act_gate(act)
                units(act, unit)

            def plain_gpsimd(pool):
                pool.sem_inc(half_read, 2)
                pool.wait_ge(exp_table, 1)
                pool.wait_ge(xn1_ready, SIDE_TILES)
                pool.sem_inc(fc_out, 16)
                for u in range(2):
                    stage_v(pool, u, u)

                def unit(u, par, last=False):
                    for half in range(1 if last else 2):
                        sum_half(pool, nc.gpsimd, pool_step, HALF_STEPS * (2 * u + half), u, half)
                        c = 2 * u + half - 3
                        if isinstance(u, int) and 0 <= c < CHUNKS:
                            pool_scatter(pool, c)
                        if isinstance(u, int) and CU <= u < CU + 2:
                            pool_combine(pool, 2 * (u - CU) + half)

                CU = EU + E + 1
                for u in range(H):
                    unit(u, u % 2)
                    stage_next(pool, u)
                with pool.Fori(H // 2, LAST) as pair:
                    for par in range(2):
                        unit(2 * pair + par, par)
                        stage_v(pool, 2 * pair + par + 2, par)
                unit(UNITS - 2, 0)
                unit(UNITS - 1, 1, last=True)

            def stage_next(pool, u):
                if u == H - 2:
                    pool.wait_ge(x_read, X0)
                stage_v(pool, u + 2, u % 2)

            def plain_sync(sp):
                for u in range(2):
                    load_rows(sp, u, u)

                def unit(u, par, e=None, next_expert=False):
                    sp.wait_ge(sc_made, pair_no(u, 0))
                    load_stack(sp, u + 2, par)
                    if e is not None:
                        sp_expert_out(sp, e)
                    if next_expert:
                        sp_expert_in(sp, e + 2, 1 - par)
                    load_rows(sp, u + 2, par)

                sp.wait_ge(sc_made, T0_NO + SIDE_B)
                load_stack(sp, 2, 0)
                sp.wait_ge(sc_made, pair_no(0, 1) + SIDE_B)
                load_stack(sp, 3, 1)
                load_rows(sp, 2, 0)
                load_rows(sp, 3, 1)
                for u in range(2, 4):
                    j = (u - 2) * NQ_SIDE
                    sp.wait_ge(sc_made, pair_no(u, 0))
                    load_stack(sp, u + 2, u % 2)
                    sp_side1(sp, j, j + NQ_SIDE - 1)
                    load_rows(sp, u + 2, u % 2)
                    sp_side1(sp, j + NQ_SIDE - 1, j + NQ_SIDE)
                sp.wait_ge(scattered, 16 * TILES)
                sp_expert_in(sp, 0, 0)
                sp.wait_ge(sc_made, pair_no(EU, 0))
                load_stack(sp, EU + 2, 0)
                sp_expert_in(sp, 1, 1)
                load_rows(sp, EU + 2, 0)
                with sp.Fori(0, E // 2 - 1) as pair:
                    for k in range(2):
                        unit(EU + 1 + 2 * pair + k, 1 - k, 2 * pair + k, next_expert=True)
                for k in range(2):
                    unit(EU + E - 1 + k, 1 - k, E - 2 + k)
                unit(EU + E + 1, 1)
                with sp.Fori(EPAIR + E // 2 + 1, LAST) as pair:
                    for par in range(2):
                        unit(2 * pair + par, par)
                sp_output(sp)
                for i in range(2):
                    sp.wait_ge(rows_in[i], ROWS * UNITS // 2)
                    sp.wait_ge(stack_in[i], LOADS * (UNITS // 2 + 1 - i))

            Qg, Kg = Qs[0][0:PROD, 0:SEQ], Ks[0][0:PROD, 0:SEQ]
            g_raw, g_s, g_n, g_a, g_b, g_cos, g_y, g_p = (T[0][:, i * SEQ:(i + 1) * SEQ] for i in range(8))
            g_acc = T[0][:, 8 * SEQ:9 * SEQ]
            g_accT = T[0][:, 9 * SEQ:10 * SEQ]
            g_col = sb("g_col", [P, 4])
            g_in, g_start, g_scores, g_angle, g_sine, g_exp, g_sum, g_chain, g_turned, g_copied, g_out, g_done = (asem(n) for n in (
                "g_in", "g_start", "g_scores", "g_angle", "g_sine", "g_exp", "g_sum", "g_chain", "g_turned", "g_copied",
                "g_out", "g_done"))
            CHAIN = 13

            def general_tiles(eng, tile):
                with eng.Fori(0, UNITS) as u:
                    with eng.Fori(0, SIDE_B) as b:
                        tile(u, b, (u * SIDE_B + b) * QT)

            def general_sync(sp):
                def tile(u, b, n):
                    sp.wait_ge(g_scores, n + QT)
                    load_stack(sp, u, 0, b * SEQ, SEQ, g_in)
                for i in range(2):
                    sp.wait_ge(stack_in[i], LOADS * (2 - i))
                general_tiles(sp, tile)
                sp.wait_ge(g_in, LOADS * UNITS * SIDE_B)

            def general_tensor(pe):
                pe.sem_inc(g_scores, QT)

                def tile(u, b, n0):
                    for qt in range(QT):
                        n = n0 + qt
                        if qt == 0:
                            pe.wait_ge(g_in, (u * SIDE_B + b + 1) * LOADS)
                        pe.wait_ge(g_done, n + 1)
                        nc.tensor.matmul(banks[0][:, 0:SEQ], Qg[:, qt * P:(qt + 1) * P], Kg, start=True, stop=True).then_inc(g_scores, 1)
                        pe.wait_ge(g_sum, W * (n + 1))
                        for kt in range(QT):
                            ins = nc.tensor.transpose(banks[1][:, kt * P:(kt + 1) * P], g_acc[:, kt * P:(kt + 1) * P], ident[:, :])
                        ins.then_inc(g_turned, 1)
                        pe.wait_ge(g_copied, n + 1)
                        for kt in range(QT):
                            ins = nc.tensor.matmul(banks[2][:, 0:HD], g_accT[:, kt * P:(kt + 1) * P],
                                                   Vall[:, ds(u * SIDE_TILES * HD + (b * QT + kt) * HD, HD)], start=kt == 0, stop=kt == QT - 1)
                        ins.then_inc(g_out, 1)
                general_tiles(pe, tile)

            def general_scalar(act):
                def tile(u, b, n0):
                    for qt in range(QT):
                        with act.Fori(0, W) as w:
                            m = (n0 + qt) * W + w
                            act.wait_ge(g_angle, m + 1)
                            nc.scalar.activation(g_cos, g_b, ACT.Sin).then_inc(g_sine, 1)
                            act.wait_ge(g_chain, CHAIN * m + 11)
                            nc.scalar.activation(g_p, g_y, ACT.Exp, bias=g_col[:, 0:1], accum_out=g_col[:, 1:2]).then_inc(g_exp, 1)
                general_tiles(act, tile)

            def general_vector(dve):
                dve.sem_inc(g_done, 1)

                def tile(u, b, n0):
                    for qt in range(QT):
                        n = n0 + qt
                        dve.wait_ge(g_scores, n + 1 + QT)
                        nc.vector.tensor_copy(g_raw, banks[0][:, 0:SEQ]).then_inc(g_start, 1)
                        nc.vector.memset(g_acc, 0.0).then_inc(g_start, 1)
                        with dve.Fori(0, W) as w:
                            m = n * W + w

                            def link(k, ins):
                                ins.then_inc(g_chain, 1)
                                dve.wait_ge(g_chain, CHAIN * m + k)

                            dve.wait_ge(g_start, 2 * (n + 1))
                            link(1, nc.vector.tensor_scalar(g_s, g_raw, cw[:, ds(u * W + w, 1)], None, ALU.mult))
                            link(2, nc.vector.scalar_tensor_tensor(g_a, g_s, KERR, g_s, ALU.mult, ALU.mult))
                            link(3, nc.vector.tensor_scalar(g_n, g_a, 1.0 / TWO_PI, 0.25, ALU.mult, ALU.add))
                            link(4, nc.vector.tensor_scalar(g_b, g_n, ROUND, None, ALU.add))
                            link(5, nc.vector.tensor_scalar(g_n, g_b, -ROUND, None, ALU.add))
                            link(6, nc.vector.scalar_tensor_tensor(g_b, g_n, -C1, g_a, ALU.mult, ALU.add))
                            link(7, nc.vector.scalar_tensor_tensor(g_a, g_n, -C2, g_b, ALU.mult, ALU.add))
                            link(8, nc.vector.scalar_tensor_tensor(g_b, g_n, -C3, g_a, ALU.mult, ALU.add))
                            link(9, nc.vector.tensor_scalar(g_a, g_b, np.pi / 2, np.pi, ALU.add, ALU.min))
                            nc.vector.tensor_scalar(g_b, g_a, -np.pi, None, ALU.max).then_inc(g_angle, 1)
                            dve.wait_ge(g_sine, m + 1)
                            link(10, nc.vector.tensor_tensor(g_y, g_s, g_cos, ALU.mult))
                            link(11, nc.vector.reduce_max(g_col[:, 0:1], g_y, AX.X, negate=True))
                            dve.wait_ge(g_exp, m + 1)
                            link(12, nc.vector.reciprocal(g_col[:, 2:3], g_col[:, 1:2]))
                            link(13, nc.vector.tensor_tensor(g_col[:, 3:4], g_col[:, 2:3], iw_s[:, ds(w, 1)], ALU.mult))
                            nc.vector.scalar_tensor_tensor(g_acc, g_p, g_col[:, 3:4], g_acc, ALU.mult, ALU.add).then_inc(g_sum, 1)
                            dve.wait_ge(g_sum, m + 1)
                        dve.wait_ge(g_turned, n + 1)
                        nc.vector.tensor_copy(g_accT, banks[1][:, 0:SEQ]).then_inc(g_copied, 1)
                        dve.wait_ge(g_out, n + 1)
                        first = u * HD + (u // H) * (SIDE_TILES - 1) * D + (b * QT + qt) * D
                        nc.vector.tensor_copy(heads[:, ds(first, HD)], banks[2][:, 0:HD]).then_inc(g_done, 1)
                general_tiles(dve, tile)

            def general_experts(eng, expert):
                with eng.Fori(0, E // 2) as pair:
                    for par in range(2):
                        expert(2 * pair + par, pair, par)

            def plain_or_general(eng, plain, general):
                chosen = eng.value_load(flag[0:1, 0:1], min_val=0, max_val=1)
                with eng.If(chosen == 1):
                    plain(eng)
                with eng.Else():
                    general(eng)

            def all_general_sync(sp):
                sp_side1(sp, 0, PARTS1)
                sp.wait_ge(scattered, 16 * TILES)

                def expert(e, pair, par):
                    sp.wait_ge(x_read, e * EI + X0)
                    sp_expert_in(sp, e, par)
                    sp_expert_out(sp, e)
                general_experts(sp, expert)
                general_sync(sp)
                sp_output(sp)

            def all_general_tensor(pe):
                for w in range(W):
                    pe_side1(pe, w)
                for w in range(W):
                    pe_routing(pe, w)
                for par in range(2):
                    for w in range(W):
                        pe_qkv(pe, par, w)

                def expert(e, pair, par):
                    for w in range(EI):
                        pe_expert(pe, e, pair, par, w)
                general_experts(pe, expert)
                general_tensor(pe)
                pe.wait_ge(g_done, UNITS * SIDE_B * QT + 1)
                for n in range(NQ_SIDE):
                    for w in range(OUT_STEPS):
                        pe_output(pe, n, w)

            def all_general_scalar(act):
                act_gate(act)
                general_scalar(act)

            def all_general_vector(dve):
                for w in range(W):
                    dve_side1(dve, w)
                for w in range(W):
                    dve_routing(dve, w)
                for par in range(2):
                    for w in range(W):
                        dve_qkv(dve, par, w)

                def expert(e, pair, par):
                    for w in range(EI):
                        dve_expert(dve, e, par, w)
                general_experts(dve, expert)
                general_vector(dve)
                for n in range(NQ_SIDE):
                    for w in range(OUT_STEPS):
                        dve_output(dve, n, w)

            def all_general_gpsimd(pool):
                pool.sem_inc(fc_out, 16)
                for c in range(CHUNKS):
                    pool_scatter(pool, c)
                for c in range(CHUNKS):
                    pool_combine(pool, c)

            with nc.Block() as block:

                @block.sync
                def _(sp):
                    plain_or_general(sp, plain_sync, all_general_sync)

                @block.tensor
                def _(pe):
                    plain_or_general(pe, plain_tensor, all_general_tensor)

                @block.scalar
                def _(act):
                    plain_or_general(act, plain_scalar, all_general_scalar)

                @block.vector
                def _(dve):
                    plain_or_general(dve, plain_vector, all_general_vector)

                @block.gpsimd
                def _(pool):
                    pool_side1(pool)
                    plain_or_general(pool, plain_gpsimd, all_general_gpsimd)

        fin = ExitStack()
        with fin:
            def fsem(name):
                return fin.enter_context(nc.semaphore(name))

            hT = [T[1][:, i * BANK:(i + 1) * BANK] for i in range(2)]
            h_turned, h_copied, o_made, o_added, stored = (fsem(n) for n in (
                "h_turned", "h_copied", "o_made", "o_added", "stored"))
            hv = heads[:, :].rearrange("p (t f) -> p t f", f=D)
            T0 = SIDE_TILES
            N = SIDE_TILES // TB

            with nc.Block() as block:

                @block.tensor
                def _(pe):
                    def project(n):
                        pe.wait_ge(h_copied, n + 1)
                        if n >= 2:
                            pe.wait_ge(o_added, n - 1)
                        for i in range(TB):
                            ins = nc.tensor.matmul(banks[2 + n % 2][:, i * D:(i + 1) * D], hT[n % 2][:, i * P:(i + 1) * P],
                                                   wo_s[:, :], start=True, stop=True)
                        ins.then_inc(o_made, 1)

                    for n in range(N):
                        if n >= 2:
                            pe.wait_ge(h_copied, n - 1)
                        for i in range(TB):
                            t = T0 + n * TB + i
                            ins = nc.tensor.transpose(banks[n % 2][:, i * P:(i + 1) * P],
                                                      hv[:, t, :], ident[:, :])
                        ins.then_inc(h_turned, 1)
                        if n:
                            project(n - 1)
                    project(N - 1)

                @block.scalar
                def _(act):
                    for n in range(N):
                        act.wait_ge(h_turned, n + 1)
                        if n >= 2:
                            act.wait_ge(o_made, n - 1)
                        nc.scalar.activation(hT[n % 2], banks[n % 2][:, :], ACT.Copy).then_inc(h_copied, 1)

                @block.vector
                def _(dve):
                    for n in range(N):
                        dve.wait_ge(o_made, n + 1)
                        b = base[:, T0 + n * TB:T0 + (n + 1) * TB, :]
                        nc.vector.tensor_tensor(b, b, banks[2 + n % 2][:, :].rearrange("p (t d) -> p t d", d=D), ALU.add).then_inc(o_added, 1)

                @block.sync
                def _(sp):
                    ov = out.rearrange("b (t p) d -> p (b t) d", p=P)
                    for n in range(N):
                        sp.wait_ge(o_added, n + 1)
                        sp.dma_start(ov[:, T0 + n * TB:T0 + (n + 1) * TB, :], base[:, T0 + n * TB:T0 + (n + 1) * TB, :]).then_inc(stored, 16)
                    sp.wait_ge(stored, 16 * (N))
_INS = ['L0_attn_x', 'L0_attn_Wq', 'L0_attn_bq', 'L0_attn_Wk', 'L0_attn_bk', 'L0_attn_Wv', 'L0_attn_bv', 'L0_attn_Wo',
        'L0_attn_bo', 'L0_attn_phase_modulators', 'L0_attn_interference_weights', 'L0_ffn_gate_w', 'L0_ffn_w1',
        'L0_ffn_b1', 'L0_ffn_w2', 'L0_ffn_b2']


def kernel(**inputs):
    import numpy as _np
    import concourse.bacc as _bacc
    from concourse import mybir as _mybir
    from concourse.bass_utils import run_bass_kernel_spmd as _run

    nc = _bacc.Bacc("TRN2", target_bir_lowering=False, num_devices=1)
    arrays, args = {}, []
    for name in _INS:
        a = _np.ascontiguousarray(inputs[name])
        arrays[f"in_{name}_dram"] = a
        args.append(nc.dram_tensor(f"in_{name}_dram", a.shape, _mybir.dt.from_np(a.dtype), kind="ExternalInput").ap())
    shape = inputs['L0_attn_x'].shape
    out = nc.dram_tensor("out_0_dram", shape, _mybir.dt.float32, kind="ExternalOutput").ap()
    attention_and_experts(nc, *args, out)
    r = _run(nc, [arrays], core_ids=[0])
    return r.results[0]["out_0_dram"]
```
